# Optimizing a Trainium2 kernel written in Bass

```python
import numpy as np
import jax
import jax.numpy as jnp

def _softmax(x, axis=-1):
    return jax.nn.softmax(x, axis=axis)

def _gelu(x):
    return jax.nn.gelu(x, approximate=True)

def _silu(x):
    return jax.nn.silu(x)

def _sigmoid(x):
    return jax.nn.sigmoid(x)

def _layernorm(x, axis=-1, eps=1e-05):
    m = jnp.mean(x, axis=axis, keepdims=True)
    v = jnp.var(x, axis=axis, keepdims=True)
    return (x - m) / jnp.sqrt(v + eps)

def _scatter_add(tgt, idx, src, axis=0):
    return tgt.at[idx].add(src)

def _segment_sum(src, seg, n):
    return jax.ops.segment_sum(src, seg, n)
kernel_name = 'mk_gnn_resnorm_d2_gnn_r8_9a1a3d'

def setup_inputs(seed: int=0):
    np.random.seed(seed)
    _w = jnp.asarray

    def _rec_inputs():
        import jax
        import jax.numpy as jnp
        _gk = jax.random.key(seed)
        x = -0.0002117 + 1 * jax.random.normal(jax.random.fold_in(_gk, 1), (3125, 1024), jnp.float32)
        src = jax.random.randint(jax.random.fold_in(_gk, 2), (50000,), 0, 3125, jnp.int32)
        dst = jax.random.randint(jax.random.fold_in(_gk, 3), (50000,), 0, 3125, jnp.int32)
        _o = jnp.argsort(dst, stable=True)
        src = src[_o]
        dst = dst[_o]
        edge_weight = jax.random.uniform(jax.random.fold_in(_gk, 13), (50000,), jnp.float32, 0.0, 0.999994)
        return (x, src, dst, edge_weight)
    x, src, dst, edge_weight = _rec_inputs()

    def _L0_gnn_setup():
        import jax, jax.numpy as jnp
        import numpy as np
        N = 3125
        E = 50000
        H = 4
        C = 256
        D_IN = 1024
        NEG_SLOPE = 0.2
        key = jax.random.key(seed)
        k1, k2, k3, k4, k5, k6 = jax.random.split(key, 6)
        x = jax.random.normal(k1, (N, D_IN), dtype=jnp.float32)
        edge_index = jax.random.randint(k2, (2, E), 0, N, dtype=jnp.int64)
        scale = 1.0 / np.sqrt(D_IN)
        W = jax.random.normal(k3, (D_IN, H * C), dtype=jnp.float32) * scale
        att_src = jax.random.normal(k4, (H, C), dtype=jnp.float32) * 0.1
        att_dst = jax.random.normal(k5, (H, C), dtype=jnp.float32) * 0.1
        bias = jax.random.normal(k6, (H * C,), dtype=jnp.float32) * 0.01
        return {'x': x, 'edge_index': edge_index, 'W': W, 'att_src': att_src, 'att_dst': att_dst, 'bias': bias}
    _L0_gnn_all = _L0_gnn_setup()
    _L0_gnn_in = {k: v for k, v in _L0_gnn_all.items() if k in ('W', 'att_src', 'att_dst', 'bias')}
    del _L0_gnn_all

    def _L1_gnn_setup():
        import jax, jax.numpy as jnp
        import numpy as np
        N_NODES = 2048
        N_EDGES = 16384
        D = 1024
        key = jax.random.key(seed)
        k_x, k_w, k_W, k_s, k_d = jax.random.split(key, 5)
        x = jax.random.normal(k_x, (N_NODES, D), dtype=jnp.float32)
        edge_w = jax.random.uniform(k_w, (N_EDGES,), dtype=jnp.float32)
        W = jax.random.normal(k_W, (D, D), dtype=jnp.float32) * (1.0 / np.sqrt(D))
        b = jnp.zeros((D,), dtype=jnp.float32)
        src = jax.random.randint(k_s, (N_EDGES,), 0, N_NODES)
        dst = jax.random.randint(k_d, (N_EDGES,), 0, N_NODES)
        return {'x': x, 'edge_w': edge_w, 'W': W, 'b': b, 'src': src, 'dst': dst}
    _L1_gnn_all = _L1_gnn_setup()
    _L1_gnn_in = {k: v for k, v in _L1_gnn_all.items() if k in ('W', 'b')}
    del _L1_gnn_all
    return {'x': x, 'src': src, 'dst': dst, 'edge_weight': edge_weight, 'L0_gnn_W': _L0_gnn_in['W'], 'L0_gnn_att_src': _L0_gnn_in['att_src'], 'L0_gnn_att_dst': _L0_gnn_in['att_dst'], 'L0_gnn_bias': _L0_gnn_in['bias'], 'L1_gnn_W': _L1_gnn_in['W'], 'L1_gnn_b': _L1_gnn_in['b']}

def reference(x, src, dst, edge_weight, L0_gnn_W, L0_gnn_att_src, L0_gnn_att_dst, L0_gnn_bias, L1_gnn_W, L1_gnn_b):
    import jax
    import jax.numpy as jnp

    def _L0_gnn_ref(x, edge_index, W, att_src, att_dst, bias):
        import jax, jax.numpy as jnp
        import numpy as np
        N = 3125
        E = 50000
        H = 4
        C = 256
        D_IN = 1024
        NEG_SLOPE = 0.2
        xp = (x @ W).reshape(N, H, C)
        a_src = jnp.einsum('nhc,hc->nh', xp, att_src)
        a_dst = jnp.einsum('nhc,hc->nh', xp, att_dst)
        loops = jnp.arange(N, dtype=edge_index.dtype)
        src = jnp.concatenate([edge_index[0], loops])
        dst = jnp.concatenate([edge_index[1], loops])
        e = jax.nn.leaky_relu(a_src[src] + a_dst[dst], NEG_SLOPE)
        m = jax.ops.segment_max(e, dst, num_segments=N)
        ee = jnp.exp(e - m[dst])
        z = jax.ops.segment_sum(ee, dst, num_segments=N)
        alpha = ee / z[dst]
        msgs = xp[src] * alpha[:, :, None]
        out = jax.ops.segment_sum(msgs, dst, num_segments=N)
        out = out.reshape(N, H * C) + bias
        return jax.nn.relu(out)

    def _L1_gnn_ref(x, edge_w, W, b, src, dst):
        import jax, jax.numpy as jnp
        import numpy as np
        N_NODES = 2048
        N_EDGES = 16384
        D = 1024
        "EdgeWeightNorm(norm='both') -> GraphConv(norm='both', weight, bias) -> ReLU.\n\n            Matches DGL semantics:\n              c_ij   = w_ij / sqrt(sum_out_w[src] * sum_in_w[dst])   (EdgeWeightNorm 'both')\n              h_j    = relu( D_in[j]^-1/2 * sum_i c_ij * D_out[i]^-1/2 * x_i  @ W + b )\n            where D_out/D_in are structural degrees clamped to >= 1.\n            "
        n = x.shape[0]
        ones = jnp.ones_like(edge_w)
        w_out = jax.ops.segment_sum(edge_w, src, num_segments=n)
        w_in = jax.ops.segment_sum(edge_w, dst, num_segments=n)
        c = edge_w * jax.lax.rsqrt(w_out[src] * w_in[dst])
        deg_out = jnp.clip(jax.ops.segment_sum(ones, src, num_segments=n), 1.0)
        deg_in = jnp.clip(jax.ops.segment_sum(ones, dst, num_segments=n), 1.0)
        xs = x * jax.lax.rsqrt(deg_out)[:, None]
        msg = xs[src] * c[:, None]
        agg = jax.ops.segment_sum(msg, dst, num_segments=n)
        agg = agg * jax.lax.rsqrt(deg_in)[:, None]
        return jax.nn.relu(agg @ W + b)
    edge_index = jnp.stack([src, dst])
    x = _layernorm(x + _L0_gnn_ref(x, edge_index, L0_gnn_W, L0_gnn_att_src, L0_gnn_att_dst, L0_gnn_bias), axis=-1)
    x = _layernorm(x + _L1_gnn_ref(x, edge_weight, L1_gnn_W, L1_gnn_b, src, dst), axis=-1)
    return x

_drawn_inputs = setup_inputs


def setup_inputs(seed=0):
    import zlib

    import numpy as np

    out = dict(_drawn_inputs(seed))
    spreads = {'L1_gnn_b': (0.0, 0.1)}
    factors = {'edge_weight': 8.0, 'L0_gnn_bias': 7.912, 'L1_gnn_W': 4.283}
    for name, (base, spread) in spreads.items():
        noise = np.random.default_rng([zlib.crc32(name.encode()), seed]).standard_normal(out[name].shape)
        drawn = base * np.exp(spread * noise) if base else spread * noise
        out[name] = jnp.asarray(drawn.astype(out[name].dtype))
    for name, factor in factors.items():
        out[name] = (out[name] * factor).astype(out[name].dtype)
    return out
```

```python
from contextlib import ExitStack

import concourse.bass as bass
from concourse import mybir

P = 128
N = 3125
NT = -(-N // P)
NP = NT * P
D = 1024
KT = D // P
H = 4
C = D // H
E = 50000
EB = 256
NB = -(-E // EB)
VISITS = NB + NT - 1
VPAD = 2 * P
G = VPAD // P
HALF = EB // P
TILES = VISITS * HALF
RING = 8
VPI = RING // HALF
ITERS = VISITS // VPI
ROW1 = D + 4
NV = 10
BIG = float(2.0 ** 100)
SLOPE = 0.2
EPS = 1e-5
XP_BANKS = ((0, 1), (2, 3), (5, 6))
assert VISITS % VPI == 0 and VISITS <= VPAD

ALU = mybir.AluOpType
ACT = mybir.ActivationFunctionType
AX = mybir.AxisListType
F32 = mybir.dt.float32
BF16 = mybir.dt.bfloat16
I32 = mybir.dt.int32


class Tally:

    def __init__(self, sem):
        self.sem, self.n, self.off, self.start = sem, 0, 0, 0

    def inc(self, ins):
        ins.then_inc(self.sem, 1)
        self.n += 1

    def value(self):
        return self.off + self.n

    def enter(self, i, per):
        self.off, self.start, self.per = i * per, self.n, per

    def leave(self, count):
        assert self.n - self.start == self.per, (self.n - self.start, self.per)
        self.off, self.n = 0, self.start + count * self.per


class Tile:

    def __init__(self, turn, slot):
        self.turn, self.at = turn, turn * 2 + slot

    def __add__(self, n):
        return self.at + n

    def __sub__(self, n):
        return self.at - n

    def __mul__(self, n):
        return self.at * n


def gnn_kernel(nc, xT, x, src_blocks, dst_blocks, w_blocks, W0, att_src, att_dst, bias0, W1, bias1, out):
    ctx = ExitStack()
    with ctx:
        def sb(name, shape, dt=F32):
            return ctx.enter_context(nc.sbuf_tensor(name, shape, dt))

        def sem(name):
            return ctx.enter_context(nc.semaphore(name))

        xp_dram = nc.dram_tensor("xp_rows", [NP, D], F32, kind="Internal").ap()
        as_dram = nc.dram_tensor("source_scores", [NP, H], F32, kind="Internal").ap()
        rel_dram = nc.dram_tensor("relative_dst", [VPAD, EB], BF16, kind="Internal").ap()
        x1_dram = nc.dram_tensor("x1_rows", [NP, ROW1], F32, kind="Internal").ap()

        psum = ctx.enter_context(nc.psum_tensor("psum", [P, 8, 512], F32))
        bank = [psum[:, i, :] for i in range(8)]

        def pair(b):
            return psum[:, 2 * b:2 * b + 2, :]


        sums = sb("sums", [P, NT * D])
        Wt = sb("Wt", [P, KT, D])
        rows = sb("rows", [P, RING * ROW1])
        vals = sb("vals", [P, (TILES + HALF) * NV])
        relT = sb("relT", [P, VPAD * HALF])
        srcT = sb("srcT", [P, VPAD * HALF], I32)
        hots = sb("hots", [P, 4, (1 + H) * P])
        iota_f = sb("iota_f", [P, EB])
        ident = sb("ident", [P, P])
        visit_no = sb("visit_no", [P, G])
        tab = sb("tab", [P, NT * 2 * H])
        nodesum = sb("nodesum", [P, NT * NV])
        tile_of = sb("tile_of", [1, VPAD], I32)
        fsrc = sb("fsrc", [P, NT])
        idx = sb("idx", [P, RING], I32)
        fdst = sb("fdst", [P, NT])
        zero1 = sb("zero1", [P, 1])

        valv = vals[:, :].rearrange("p (u k) -> p u k", k=NV)
        nodev = nodesum[:, :].rearrange("p (j k) -> p j k", k=NV)
        tabv = tab[:, :].rearrange("p (j k) -> p j k", k=2 * H)

        def cut(tensor, at, n):
            return tensor[:, at:at + n]

        xT_ring = [cut(rows, b * D, D).rearrange("p (k n) -> p k n", k=KT) for b in range(5)]
        xp_stage = [cut(rows, (5 + b) * D, D) for b in range(2)]

        row_ring = [cut(rows, q * ROW1, ROW1) for q in range(RING)]
        x_in = [cut(rows, b * D, D) for b in range(2)]
        xp_in = [cut(rows, (2 + b) * D, D) for b in range(2)]
        mix = [cut(rows, (4 + b) * D, D) for b in range(2)]
        x1_out = [cut(rows, 6 * D + b * ROW1, ROW1) for b in range(2)]
        agg = [cut(rows, b * D, D) for b in range(2)]
        aggT = [cut(rows, (2 + b) * D, D).rearrange("p (k n) -> p k n", k=KT) for b in range(2)]
        x1_in = [cut(rows, (6 + b) * D, D) for b in range(2)]

        hots_flat = hots[:, :, :].rearrange("p q c -> p (q c)")
        bias_at = hots_flat[:, 0:D]
        diag = [hots_flat[:, D + b * H * P:D + (b + 1) * H * P] for b in range(2)]
        spare = hots_flat[:, 2 * D:]
        r_self = spare[:, 0:NT * H]
        c_self = spare[:, 104:104 + (NT + 1) * H]
        t_self = spare[:, 208:208 + NT * H]
        stats = [spare[:, 312 + b * 20:312 + b * 20 + 12] for b in range(2)]
        moments = [spare[:, 312 + b * 20 + 12:312 + b * 20 + 14] for b in range(2)]
        spread = [spare[:, 312 + b * 20 + 14:312 + b * 20 + 16] for b in range(2)]
        ones1 = spare[0:1, 352:352 + P]

        place = [0]

        def take(n):
            at = place[0]
            place[0] += n
            assert place[0] <= NT * D
            return cut(sums, at, n)

        def take3(a, b):
            return take(a * b).rearrange("p (a b) -> p a b", a=a)

        ad_flat = take(TILES * 2 * H)
        adT = ad_flat.rearrange("p (u k) -> p u k", k=2 * H)
        att = ad_flat[:, 0:2 * H * C].rearrange("p (h c) -> p h c", c=C)
        dump = ad_flat[:, 2 * H * C:2 * H * C + 4 * C]
        wa = take3(KT, 2 * H)
        iota_i = take(EB).bitcast(I32)
        visit_i = take(G).bitcast(I32)
        ends_i = take(2 * NB).bitcast(I32)
        ends_t = take(2 * NB).bitcast(I32)
        ends_f = take(2 * NB)
        ones_row = take(EB)
        span = take(NB)
        endk = take(2 * NB)
        tmp_row = take(NB)
        tcount = take(G)
        mask = take(NB)
        ksel = take(G)
        jv = take(G)
        jv2 = take(G)
        j128 = take(G)
        block_i = take(G).bitcast(I32)
        dst_i = take3(G, EB).bitcast(I32)
        src_i = take3(G, EB).bitcast(I32)
        w_f = take3(G, EB)
        dst_f = take3(G, EB)
        src_f = take3(G, EB)
        rel_f = take3(G, EB)
        rel_c = take(G * EB // 2).bitcast(BF16).rearrange("p (g e) -> p g e", g=G)
        brk = take(2 * G * EB).rearrange("p (a g e) -> p a g e", a=2, g=G)
        pen = take(2 * G * EB).rearrange("p (a g e) -> p a g e", a=2, g=G)
        ends2 = take3(G, 2)
        shift = take(VPAD + 2)
        near = take(4 * G).rearrange("p (a g k) -> p a g k", a=2, g=G)
        lastT = take(VPAD * HALF)
        tab3 = take(NT * 3 * 2 * H // 2).bitcast(BF16).rearrange("p (j t k) -> p j t k", t=3, k=2 * H)
        res = take3(NT, 2 * H)
        asT = take((1 + VPAD * HALF // RING) * RING * H)
        seg = take(2 * H * G * EB).rearrange("p (a h g e) -> p a h g e", a=2, h=H, g=G)
        lo_i = take(VPAD * HALF).bitcast(I32)
        lo_f = take(VPAD * HALF)
        hi_f = take(VPAD * HALF)
        okT = take(VPAD * HALF)
        wokT = take(VPAD * HALF)
        tip = take(2 * G * H).rearrange("p (a g h) -> p a g h", a=2, g=G)
        rst = take(2 * G * H).rearrange("p (a g h) -> p a g h", a=2, g=G)
        rst_h = take3(2, VPAD)
        carry = take3(2, VPAD + 1)
        seed = take(2 * G * H).rearrange("p (a g h) -> p a g h", a=2, g=G)
        stage = [take(4 * H) for _ in range(2)]
        hist_f = take(4 * NT)
        zero50 = take(P)
        asT3 = asT.rearrange("p (u h) -> p u h", h=H)[:, RING:, :]
        seg_flat = seg.rearrange("p a h g e -> p (a h g e)")
        rel_bc = [seg_flat[:, b * 2 * EB:(b + 1) * 2 * EB].bitcast(BF16) for b in range(5)]
        hotT = [hots_flat[:, b * 2 * EB:(b + 1) * 2 * EB].bitcast(BF16) for b in range(5)]

        s = {}

        def S(name):
            if name not in s:
                s[name] = sem(name)
            return s[name]

        for name in """vector_order vector_passed pool_order pool_passed consts ends_in W0_in att_in xT_in0 xT_in1 xT_in2 xT_in3 xT_in4
            xT_scored block_ends_ready block_ends_spread blocks_known blocks_in tiles_ready tiles_turned
            rel_clamped rel_stored rel_bc0 rel_bc1 rel_bc2 rel_bc3 rel_bc4 tile_of_ready hotT_ready hotT_used
            spread_taken block_tips block_tips_turned tips_shifted tips_back wa_ready scores_out scores_stored
            edge_turned edge_taken node_parts src_index_ready xp_done xp_taken xp_copied xp_stored0 xp_stored1 W1_in
            index_copied scores_got0 scores_got1 source_scores_ready histo_ready histo_used histo_done histo_flags
            as_turned first_scan carry_turned carry_ready seeds_turned seg_ready seg_turned seg_taken exp_in exp_out
            weights_in0 sums_zero factors_in factors_out
            rows_in0 rows_in1 rows_in2 rows_in3 rows_in4 rows_in5 rows_in6 rows_in7
            rows_used0 rows_used1 hot_ready0 hot_ready1 scaled_v0 scaled_v1 scaled_a0 scaled_a1 sums_taken0 sums_taken1
            bias0_in bias1_in x_in0 x_in1 self_in self_out self_ready diag_ready mixed sums_read variance0 variance1
            deviation0 deviation1 x_free x1_ready x1_stored0 x1_stored1
            agg_ready agg_turned aggT_ready product_ready product_taken x1_free x1_in0 x1_in1 out_ready out_stored0 out_stored1
            dst_sq_in dst_sq_out sums_zero1""".split():
            S(name)

        v, a, pe, gp, sp = nc.vector, nc.scalar, nc.tensor, nc.gpsimd, nc.sync

        def by_tiles(eng, body):
            with eng.Fori(0, NT // 2) as i:
                body(Tile(i, 0), 0)
                body(Tile(i, 1), 1)
            body(NT - 1, 0)

        def turn_of(j, b):
            return (j - b) // 2 if isinstance(j, int) else j.turn

        def ahead(eng, body):
            with eng.Fori(0, (NT - 3) // 2) as i:
                body(Tile(i, 0), 0)
                body(Tile(i, 1), 1)
            body(NT - 3, 0)

        def by_visits(eng, body):
            with eng.Fori(0, ITERS) as i:
                for k in range(VPI):
                    body(i, k)

        block = ctx.enter_context(nc.Block())

        @block.sync
        def _(eng):
            with nc.allow_non_contiguous_dma(reason="two words of each block"):
                eng.dma_start(ends_i[0:1, 0:NB], dst_blocks[0:NB, 0:1].rearrange("b e -> e b")).then_inc(s["ends_in"], 16)
                eng.dma_start(ends_i[0:1, NB:2 * NB],
                              dst_blocks[0:NB, EB - 1:EB].rearrange("b e -> e b")).then_inc(s["ends_in"], 16)
            eng.dma_start(Wt[:, :, :], W0.rearrange("(k p) n -> p k n", p=P)).then_inc(s["W0_in"], 16)
            eng.dma_start(att[:, 0:H, :], att_src.unsqueeze(0).broadcast_to([P, H, C])).then_inc(s["att_in"], 16)
            eng.dma_start(att[:, H:2 * H, :], att_dst.unsqueeze(0).broadcast_to([P, H, C])).then_inc(s["att_in"], 16)

            xT_tiles = xT.rearrange("(k p) n -> p k n", p=P)
            with eng.Fori(0, NT // 5) as i:
                for b in range(5):
                    eng.wait_ge(s["xT_scored"], i * 5 + b + 1)
                    eng.dma_start(xT_ring[b], xT_tiles[:, :, bass.ds(i * (5 * P) + b * P, P)]).then_inc(s[f"xT_in{b}"], 16)
            eng.wait_ge(s["rel_clamped"], 1)
            eng.dma_start(rel_dram.rearrange("(g s) e -> s g e", g=G), rel_c).then_inc(s["rel_stored"], 16)
            eng.wait_ge(s["rel_stored"], 16)
            flat = rel_dram.rearrange("s e -> (s e)").unsqueeze(0)
            with eng.Fori(0, 11) as i:
                for b in range(5):
                    eng.wait_ge(s["hotT_ready"], i * 5 + b + 1)
                    eng.dma_start(rel_bc[b], flat[:, bass.ds(i * (5 * 4 * EB) + b * 4 * EB, 4 * EB)]
                                  .broadcast_to([P, 4 * EB])).then_inc(s[f"rel_bc{b}"], 16)
            for b in range(5):
                eng.wait_ge(s["xT_scored"], NT + b + 1)
                eng.dma_start(xT_ring[b], xT_tiles[:, :, b * P:(b + 1) * P]).then_inc(s[f"xT_in{b}"], 16)
            with eng.Fori(0, NT // 5 - 1) as i:
                for b in range(5):
                    eng.wait_ge(s["xp_done"], i * 10 + 2 * b + 2)
                    eng.dma_start(xT_ring[b], xT_tiles[:, :, bass.ds(i * (5 * P) + (5 + b) * P, P)]) \
                        .then_inc(s[f"xT_in{b}"], 16)
            eng.wait_ge(s["xp_done"], 2 * NT)
            eng.dma_start(Wt[:, :, :], W1.rearrange("(k p) n -> p k n", p=P)).then_inc(s["W1_in"], 16)

            eng.wait_ge(s["rows_used0"], VPI + VISITS)
            eng.wait_ge(s["scaled_v0"], VISITS + 1)
            eng.dma_start(bias_at[0:1, :], bias0.unsqueeze(0)).then_inc(s["bias0_in"], 16)

            def load_x(j, b):
                eng.wait_ge(s["x_free"], j + 1)
                eng.dma_start(x_in[b], x[bass.ds(j * P, P), :]).then_inc(s[f"x_in{b}"], 16)
                eng.dma_start(xp_in[b], xp_dram[bass.ds(j * P, P), :]).then_inc(s[f"x_in{b}"], 16)

            by_tiles(eng, load_x)

            eng.wait_ge(s["rows_used1"], VPI + VISITS)
            eng.wait_ge(s["hot_ready1"], VISITS + 1)
            eng.dma_start(bias_at, bias1.unsqueeze(0).broadcast_to([P, D])).then_inc(s["bias1_in"], 16)

            def load_x1(j, b):
                eng.wait_ge(s["x1_free"], j + 1)
                eng.dma_start(x1_in[b], x1_dram[bass.ds(j * P, P), 0:D]).then_inc(s[f"x1_in{b}"], 16)

            by_tiles(eng, load_x1)

        @block.gpsimd
        def _(eng):
            order = Tally(s["pool_order"])

            def passed(sem, value):
                eng.wait_ge(sem, value)
                eng.sem_inc(s["pool_passed"], 1)

            gp.iota(iota_i, pattern=[[1, EB]], base=0, channel_multiplier=0).then_inc(s["consts"], 1)
            gp.iota(visit_i, pattern=[[P, G]], base=0, channel_multiplier=1).then_inc(s["consts"], 1)
            eng.wait_ge(s["blocks_known"], 1)
            for g in range(G):
                off = bass.IndirectOffsetOnAxis(ap=block_i[:, g:g + 1], axis=0)
                for to, dram in ((dst_i, dst_blocks), (src_i, src_blocks), (w_f, w_blocks)):
                    gp.indirect_dma_start(to[:, g, :], None, dram, off).then_inc(s["blocks_in"], 16)

            eng.wait_ge(s["src_index_ready"], 1)
            eng.wait_ge(s["scores_stored"], 16)

            def gather_scores(half, i, first):
                if not first:
                    passed(s[f"scores_got{half}"], i * 64)
                    order.inc(gp.tensor_copy(asT[:, bass.ds(i * (RING * H) + half * 4 * H, 4 * H)], stage[half]))
                order.inc(gp.tensor_copy(idx[:, half * 4:half * 4 + 4], srcT[:, bass.ds(i * RING + half * 4, 4)]))
                passed(order.sem, order.value())
                for q in range(4):
                    gp.indirect_dma_start(stage[half][:, q * H:(q + 1) * H], None, as_dram,
                                          bass.IndirectOffsetOnAxis(ap=idx[:, half * 4 + q:half * 4 + q + 1], axis=0)) \
                        .then_inc(s[f"scores_got{half}"], 16)

            gather_scores(0, 0, True)
            gather_scores(1, 0, True)
            with eng.Fori(0, ITERS - 1) as i:
                order.enter(i, 4)
                gather_scores(0, i + 1, False)
                gather_scores(1, i + 1, False)
                order.leave(ITERS - 1)
            for half in range(2):
                eng.wait_ge(s[f"scores_got{half}"], 64 * ITERS)
                gp.tensor_copy(asT[:, ITERS * RING * H + half * 4 * H:ITERS * RING * H + half * 4 * H + 4 * H],
                               stage[half]).then_inc(s["source_scores_ready"], 1)

            def gather_rows(layer, table, width):
                def visit(i, k):
                    passed(s[f"rows_used{layer}"], i * VPI + k + 1)
                    order.inc(gp.tensor_copy(idx[:, k * 2:k * 2 + 2], srcT[:, bass.ds(i * RING + k * 2, 2)]))
                    passed(order.sem, order.value())
                    for q in (2 * k, 2 * k + 1):
                        gp.indirect_dma_start(row_ring[q][:, 0:width], None, table,
                                              bass.IndirectOffsetOnAxis(ap=idx[:, q:q + 1], axis=0)) \
                            .then_inc(s[f"rows_in{q}"], 16)

                with eng.Fori(0, ITERS) as i:
                    order.enter(i, VPI)
                    for k in range(VPI):
                        visit(i, k)
                    order.leave(ITERS)

            eng.wait_ge(s["xp_stored0"], 16 * NT * 3 // 5)
            eng.wait_ge(s["xp_stored1"], 16 * NT * 2 // 5)
            gather_rows(0, xp_dram, D)

            def store_x1(j, b):
                eng.wait_ge(s["sums_read"], j + 3)
                gp.tensor_copy(sums[:, bass.ds(j * D, D)], zero1[:, :].broadcast_to([P, D])).then_inc(s["sums_zero1"], 1)
                eng.wait_ge(s["x1_ready"], j + 1)
                gp.dma_start(x1_dram[bass.ds(j * P, P), :], x1_out[b]).then_inc(s[f"x1_stored{b}"], 16)

            by_tiles(eng, store_x1)
            eng.wait_ge(s["x1_stored0"], 16 * (NT - NT // 2))
            eng.wait_ge(s["x1_stored1"], 16 * (NT // 2))
            gather_rows(1, x1_dram, ROW1)

            def store_out(j, b):
                eng.wait_ge(s["out_ready"], j + 1)
                gp.dma_start(out[bass.ds(j * P, P), :], mix[b]).then_inc(s[f"out_stored{b}"], 16)

            with eng.Fori(0, NT // 2) as i:
                store_out(i * 2, 0)
                store_out(i * 2 + 1, 1)
            eng.wait_ge(s["out_ready"], NT)
            gp.dma_start(out[(NT - 1) * P:N, :], mix[0][0:N - (NT - 1) * P, :]).then_inc(s["out_stored0"], 16)
            eng.wait_ge(s["out_stored0"], 16 * (NT - NT // 2))
            eng.wait_ge(s["out_stored1"], 16 * (NT // 2))

        @block.tensor
        def _(eng):
            eng.wait_ge(s["block_ends_ready"], 1)
            pe.matmul(bank[5][:, 0:2 * NB], ones_row[0:1, 0:P], endk[0:1, :], start=True, stop=True) \
                .then_inc(s["block_ends_spread"], 1)
            eng.wait_ge(s["tiles_ready"], 1)
            for g in range(G):
                ins = pe.transpose(bank[6][0:1, g * P:(g + 1) * P], jv[:, g:g + 1], ident[:, :])
            ins.then_inc(s["tiles_turned"], 1)
            eng.wait_ge(s["block_tips"], 1)
            for g in range(G):
                ins = pe.transpose(bank[7][0:2, g * P:(g + 1) * P], ends2[:, g, :], ident[:, :])
            ins.then_inc(s["block_tips_turned"], 1)
            eng.wait_ge(s["tips_shifted"], 1)
            for side in range(2):
                for g in range(G):
                    ins = pe.transpose(bank[4][:, (side * G + g) * 2:(side * G + g) * 2 + 2],
                                       shift[0:2, g * P + 2 * side:g * P + 2 * side + P], ident[0:2, 0:2])
            ins.then_inc(s["tips_back"], 1)

            eng.wait_ge(s["edge_turned"], 1)
            for n, item in enumerate((src_f, rel_f, w_f, brk[:, 1])):
                for g in range(G):
                    for h2 in range(HALF):
                        ins = pe.transpose(bank[n][:, (g * HALF + h2) * P:(g * HALF + h2 + 1) * P],
                                           item[:, g, h2 * P:(h2 + 1) * P], ident[:, :])
                ins.then_inc(s["edge_taken"], 1)

            eng.wait_ge(s["wa_ready"], KT * 2 * H)
            with eng.Fori(0, NT // 5) as i:
                for b in range(5):
                    eng.wait_ge(s[f"xT_in{b}"], i * 16 + 16)
                    for k in range(KT):
                        ins = pe.matmul(bank[5][:, bass.ds(i * (5 * 2 * H) + b * 2 * H, 2 * H)], xT_ring[b][:, k, :],
                                        wa[:, k, :], start=(k == 0), stop=(k == KT - 1))
                    ins.then_inc(s["xT_scored"], 1)

            eng.wait_ge(s["node_parts"], 1)
            eng.wait_ge(s["tile_of_ready"], 1)
            eng.wait_ge(s["edge_taken"], 8)
            with eng.Fori(0, 11) as i:
                for b in range(5):
                    eng.wait_ge(s["hotT_ready"], i * 5 + b + 6)
                    eng.wait_ge(s["spread_taken"], i * 5 + b + 1)
                    for q in range(4):
                        j = eng.value_load(tile_of[0:1, bass.ds(i * 20 + b * 4 + q, 1)], min_val=0, max_val=NT - 1)
                        for h2 in range(HALF):
                            t = q * HALF + h2
                            ins = pe.matmul(bank[b][:, t * 24:(t + 1) * 24], hotT[b][:, t * P:(t + 1) * P],
                                            tab3.rearrange("p j t k -> p (j t k)")[:, bass.ds(j * 24, 24)],
                                            start=True, stop=True)
                    ins.then_inc(s["hotT_used"], 1)

            eng.wait_ge(s["spread_taken"], 5 + 55)
            with eng.Fori(0, NT // 5) as i:
                for b in range(5):
                    eng.wait_ge(s[f"xT_in{b}"], i * 16 + 16 * (NT // 5) + 16)
                    for c in range(2):
                        eng.wait_ge(s["xp_taken"], i * 10 + b * 2 + c + 1)
                        pb = bank[XP_BANKS[b % 3][c]]
                        for k in range(KT):
                            ins = pe.matmul(pb[:, :], xT_ring[b][:, k, :], Wt[:, k, c * 512:(c + 1) * 512],
                                            start=(k == 0), stop=(k == KT - 1))
                        ins.then_inc(s["xp_done"], 1)

            eng.wait_ge(s["histo_flags"], 1)
            pe.matmul(bank[4][:, 0:2 * NT], zero50[:, :], zero50[:, 0:2 * NT], start=True, stop=False, skip_group_check=True)
            with eng.Fori(0, ITERS) as i:
                for q in range(RING):
                    eng.wait_ge(s["histo_ready"], i * RING + q + 1)
                    pe.matmul(bank[4][:, 0:2 * NT], hots[:, q % 4, 0:P], hots[:, q % 4, P:P + 2 * NT], start=False,
                              stop=False, skip_group_check=True).then_inc(s["histo_used"], 1)
            pe.matmul(bank[4][:, 0:2 * NT], zero50[:, :], zero50[:, 0:2 * NT], start=False, stop=True,
                      skip_group_check=True).then_inc(s["histo_done"], 1)

            eng.wait_ge(s["source_scores_ready"], 2)
            eng.wait_ge(s["xp_taken"], 4 + 2 * NT)
            for h in range(H):
                for g in range(G):
                    for h2 in range(HALF):
                        u = asT3[:, g * P * HALF:(g + 1) * P * HALF, h].rearrange("p (s a) -> p s a", a=HALF)[:, :, h2]
                        ins = pe.transpose(bank[h][:, (g * HALF + h2) * P:(g * HALF + h2 + 1) * P], u, ident[:, :])
                ins.then_inc(s["as_turned"], 1)
            eng.wait_ge(s["first_scan"], 1)
            for side in range(2):
                for g in range(G):
                    pe.transpose(bank[5][0:H, side * VPAD + g * P:side * VPAD + (g + 1) * P], tip[:, side, g, :], ident[:, :])
                    ins = pe.transpose(bank[6][0:H, side * VPAD + g * P:side * VPAD + (g + 1) * P], rst[:, side, g, :],
                                       ident[:, :])
            ins.then_inc(s["carry_turned"], 1)
            eng.wait_ge(s["carry_ready"], 1)
            for side in range(2):
                for g in range(G):
                    ins = pe.transpose(bank[7][:, (side * G + g) * H:(side * G + g + 1) * H],
                                       carry[0:H, side, g * P + side:g * P + side + P], ident[0:H, 0:H])
            ins.then_inc(s["seeds_turned"], 1)
            for h in range(H):
                eng.wait_ge(s["seg_ready"], h + 1)
                for g in range(G):
                    for h2 in range(HALF):
                        ins = pe.transpose(bank[4 + h][:, (g * HALF + h2) * P:(g * HALF + h2 + 1) * P],
                                           seg[:, 0, h, g, h2 * P:(h2 + 1) * P], ident[:, :])
                ins.then_inc(s["seg_turned"], 1)

            def carry_rows(layer):
                def visit(i, k):
                    b = k % 2
                    eng.wait_ge(s[f"scaled_v{layer}"], i * VPI + k + 1)
                    eng.wait_ge(s[f"scaled_a{layer}"], i * VPI + k + 1)
                    eng.wait_ge(s[f"sums_taken{layer}"], i * VPI + k + 1)
                    for h2 in range(HALF):
                        q = 2 * k + h2
                        slot = q % 4
                        eng.wait_ge(s[f"rows_in{q}"], i * 16 + 16 * ITERS * layer + 16)
                        if layer == 0:
                            for h in range(H):
                                pe.matmul(psum[:, 2 * b + h // 2, (h % 2) * C:(h % 2 + 1) * C],
                                          hots[:, slot, (1 + h) * P:(2 + h) * P], row_ring[q][:, h * C:(h + 1) * C],
                                          start=(h2 == 0 and h % 2 == 0), stop=(h2 == 1), skip_group_check=True)
                            ins = pe.matmul(bank[4 + b][:, 0:NV], hots[:, slot, 0:P],
                                            vals[:, bass.ds(i * (RING * NV) + q * NV, NV)],
                                            start=(h2 == 0), stop=(h2 == 1))
                        else:
                            for c in range(2):
                                ins = pe.matmul(psum[:, 2 * b + c, :], hots[:, slot, P:2 * P],
                                                row_ring[q][:, c * 512:(c + 1) * 512], start=(h2 == 0), stop=(h2 == 1))
                    ins.then_inc(s[f"rows_used{layer}"], 1)

                by_visits(eng, visit)

            carry_rows(0)

            eng.wait_ge(s["bias0_in"], 16)
            eng.wait_ge(s["self_ready"], 1)

            def self_loop(j, b):
                eng.wait_ge(s["diag_ready"], j + 1)
                eng.wait_ge(s[f"x_in{b}"], turn_of(j, b) * 32 + 32)
                eng.wait_ge(s["sums_read"], j + 1)
                for c in range(2):
                    pe.matmul(psum[:, 2 * b + c, :], ones1, bias_at[0:1, c * 512:(c + 1) * 512], start=True, stop=False,
                              skip_group_check=True)
                    for h in (2 * c, 2 * c + 1):
                        ins = pe.matmul(psum[:, 2 * b + c, (h % 2) * C:(h % 2 + 1) * C], diag[b][:, h * P:(h + 1) * P],
                                        xp_in[b][:, h * C:(h + 1) * C], start=False, stop=True, skip_group_check=True)
                ins.then_inc(s["mixed"], 1)

            by_tiles(eng, self_loop)
            carry_rows(1)

            eng.wait_ge(s["W1_in"], 16)
            eng.wait_ge(s["sums_taken1"], 2 + VISITS)

            def turn_sums(j, b):
                eng.wait_ge(s["agg_ready"], j + 1)
                if not (isinstance(j, int) and j == 0):
                    eng.wait_ge(s["aggT_ready"], j)
                for k in range(KT):
                    ins = pe.transpose(psum[:, 4 + k // 4, (k % 4) * P:(k % 4 + 1) * P], agg[b][:, k * P:(k + 1) * P],
                                       ident[:, :])
                ins.then_inc(s["agg_turned"], 1)

            def product(j, b):
                eng.wait_ge(s["aggT_ready"], j + 1)
                eng.wait_ge(s["product_taken"], j + 1)
                for c in range(2):
                    for k in range(KT):
                        ins = pe.matmul(psum[:, 2 * b + c, :], aggT[b][:, k, :], Wt[:, k, c * 512:(c + 1) * 512],
                                        start=(k == 0), stop=(k == KT - 1))
                ins.then_inc(s["product_ready"], 1)

            turn_sums(0, 0)
            turn_sums(1, 1)
            ahead(eng, lambda j, b: (product(j, b), turn_sums(j + 2, b)))
            product(NT - 2, 1)
            product(NT - 1, 0)

        @block.scalar
        def _(eng):
            eng.wait_ge(s["scores_out"], 1)
            with nc.allow_non_contiguous_dma(reason="four scores per node"):
                a.dma_start(as_dram.rearrange("(j p) h -> p j h", p=P), tabv[:, :, 0:H]).then_inc(s["scores_stored"], 16)
            eng.wait_ge(s["spread_taken"], 5 + 55)

            def take_xp(i, b, first):
                slot = b % 2
                if not (first and b < 2):
                    eng.wait_ge(s[f"xp_stored{slot}"], (i * 3 + b // 2) * 16 if slot == 0 else (i * 2 + b // 2) * 16)
                for c in range(2):
                    eng.wait_ge(s["xp_done"], i * 10 + b * 2 + c + 1)
                    a.copy(xp_stage[slot][:, c * 512:(c + 1) * 512], bank[XP_BANKS[b % 3][c]][:, :]).then_inc(s["xp_taken"], 1)
                eng.wait_ge(s["xp_taken"], 4 + i * 10 + b * 2 + 2)
                a.dma_start(xp_dram[bass.ds(i * (5 * P) + b * P, P), :], xp_stage[slot]).then_inc(s[f"xp_stored{slot}"], 16)

            for b in range(5):
                take_xp(0, b, True)
            with eng.Fori(0, NT // 5 - 1) as i:
                for b in range(5):
                    take_xp(i + 1, b, False)
            eng.wait_ge(s["factors_in"], 1)
            a.activation(hist_f[:, 0:2 * NT], hist_f[:, 0:2 * NT], ACT.Sqrt).then_inc(s["factors_out"], 1)
            eng.wait_ge(s["exp_in"], 1)
            a.activation(valv[:, 0:TILES, 0:H], adT[:, :, 0:H], ACT.Exp).then_inc(s["exp_out"], 1)

            def scale0(i, k):
                eng.wait_ge(s["hot_ready0"], i * VPI + k + 1)
                for q in (2 * k, 2 * k + 1):
                    for h in (2, 3):
                        ins = a.activation(hots[:, q % 4, (1 + h) * P:(2 + h) * P], hots[:, q % 4, 0:P], ACT.Copy,
                                           scale=vals[:, bass.ds(i * (RING * NV) + q * NV + h, 1)])
                ins.then_inc(s["scaled_a0"], 1)

            by_visits(eng, scale0)

            eng.wait_ge(s["self_in"], 1)
            a.activation(t_self, t_self, ACT.Exp, scale=-1.0).then_inc(s["self_out"], 1)
            eng.wait_ge(s["dst_sq_in"], 1)
            a.activation(mix[1][:, 0:2 * NT], mix[1][:, 0:2 * NT], ACT.Sqrt).then_inc(s["dst_sq_out"], 1)
            eng.wait_ge(s["self_ready"], 1)

            def make_diag(j, b):
                eng.wait_ge(s["mixed"], j + 1)
                for h in range(H):
                    ins = a.activation(diag[b][:, h * P:(h + 1) * P], ident[:, :], ACT.Copy,
                                       scale=c_self[:, bass.ds(j * H + h, 1)])
                ins.then_inc(s["diag_ready"], 1)

            def deviate(layer):
                def one(j, b):
                    eng.wait_ge(s[f"variance{layer}"], j + 1)
                    a.activation(spread[b][:, 1:2], spread[b][:, 0:1], ACT.Sqrt).then_inc(s[f"deviation{layer}"], 1)
                return one

            make_diag(0, 0)
            with eng.Fori(0, NT // 2) as i:
                make_diag(i * 2 + 1, 1)
                deviate(0)(i * 2, 0)
                make_diag(i * 2 + 2, 0)
                deviate(0)(i * 2 + 1, 1)
            deviate(0)(NT - 1, 0)

            def scale1(i, k):
                eng.wait_ge(s["hot_ready1"], i * VPI + k + 1)
                for q in (2 * k, 2 * k + 1):
                    eng.wait_ge(s[f"rows_in{q}"], i * 16 + 16 * ITERS + 16)
                    ins = a.activation(hots[:, q % 4, P:2 * P], hots[:, q % 4, 0:P], ACT.Copy,
                                       scale=row_ring[q][:, D:D + 1])
                ins.then_inc(s["scaled_a1"], 1)

            by_visits(eng, scale1)

            def scale_sums(j, b):
                if not (isinstance(j, int) and j < 2):
                    eng.wait_ge(s["agg_turned"], j - 1)
                a.activation(agg[b], sums[:, bass.ds(j * D, D)], ACT.Copy, scale=fdst[:, bass.ds(j + 0, 1)]) \
                    .then_inc(s["agg_ready"], 1)

            def take_turned(j, b):
                eng.wait_ge(s["agg_turned"], j + 1)
                if not (isinstance(j, int) and j < 2):
                    eng.wait_ge(s["product_ready"], j - 1)
                a.copy(aggT[b].rearrange("p k n -> p (k n)"), psum[:, 4:6, :].rearrange("p c n -> p (c n)")) \
                    .then_inc(s["aggT_ready"], 1)

            eng.wait_ge(s["sums_taken1"], 2 + VISITS)
            for j in range(2):
                scale_sums(j, j)
                take_turned(j, j)
            ahead(eng, lambda j, b: (scale_sums(j + 2, b), take_turned(j + 2, b), deviate(1)(j, b)))
            deviate(1)(NT - 2, 1)
            deviate(1)(NT - 1, 0)

        @block.vector
        def _(eng):
            order = Tally(s["vector_order"])

            def then(ins):
                order.inc(ins)
                eng.wait_ge(order.sem, order.value())

            eng.sem_inc(s["xT_scored"], 5)
            eng.sem_inc(s["hotT_ready"], 5)
            eng.sem_inc(s["spread_taken"], 5)
            eng.sem_inc(s["xp_taken"], 4)
            eng.sem_inc(s["histo_used"], 4)
            eng.wait_ge(s["consts"], 2)
            v.tensor_copy(iota_f[:, :], iota_i)
            v.memset(ones_row, 1.0)
            v.memset(vals[:, :], 0.0)
            v.memset(nodesum[:, :], 0.0)
            v.memset(asT, 0.0)
            v.memset(shift, -7.0)
            v.memset(carry, -BIG)
            v.memset(zero50, 0.0)
            then(v.tensor_copy(visit_no[:, :], visit_i))
            then(v.tensor_scalar(ident[:, :], iota_f[:, 0:P], visit_no[:, 0:1], None, ALU.is_equal))
            v.memset(valv[:, 0:TILES, NV - 1], 1.0)

            eng.wait_ge(s["ends_in"], 32)
            then(v.tensor_single_scalar(ends_t[0:1, :], ends_i[0:1, :], 7, ALU.arith_shift_right))
            then(v.tensor_copy(ends_f[0:1, :], ends_t[0:1, :]))
            then(v.scalar_tensor_tensor(span[0:1, :], ends_f[0:1, NB:2 * NB], 1.0, ends_f[0:1, 0:NB], ALU.add, ALU.subtract))
            then(v.tensor_tensor_scan(endk[0:1, 0:NB], ones_row[0:1, 0:NB], span[0:1, :], 0.0, ALU.mult, ALU.add))
            then(v.tensor_tensor(tmp_row[0:1, :], endk[0:1, 0:NB], span[0:1, :], ALU.subtract))
            v.tensor_tensor(endk[0:1, NB:2 * NB], tmp_row[0:1, :], ends_f[0:1, 0:NB], ALU.subtract) \
                .then_inc(s["block_ends_ready"], 1)
            eng.wait_ge(s["block_ends_spread"], 1)
            for g in range(G):
                then(v.tensor_scalar(dump[:, 0:NB], bank[5][:, 0:NB], visit_no[:, g:g + 1], None, ALU.is_le, ALU.add,
                                     accum_out=tcount[:, g:g + 1]))
                then(v.tensor_scalar(mask, iota_f[:, 0:NB], tcount[:, g:g + 1], None, ALU.is_equal))
                then(v.tensor_tensor_reduce(dump[:, 0:NB], mask, bank[5][:, NB:2 * NB], 1.0, 0.0, ALU.mult, ALU.add,
                                            ksel[:, g:g + 1]))
            v.tensor_copy(block_i, tcount).then_inc(s["blocks_known"], 1)
            then(v.scalar_tensor_tensor(jv2, ksel, -1.0, visit_no[:, :], ALU.mult, ALU.add))
            v.tensor_scalar(jv, jv2, float(NT - 1), None, ALU.min).then_inc(s["tiles_ready"], 1)
            eng.wait_ge(s["tiles_ready"], 1)
            then(v.tensor_scalar(j128, jv, float(P), None, ALU.mult))
            eng.wait_ge(s["tiles_turned"], 1)
            v.tensor_copy(tile_of[:, :], bank[6][0:1, 0:VPAD]).then_inc(s["tile_of_ready"], 1)

            eng.wait_ge(s["W0_in"], 16)
            eng.wait_ge(s["att_in"], 32)
            for k in range(KT):
                for h in range(2 * H):
                    if k * 2 * H + h >= 4:
                        eng.wait_ge(s["wa_ready"], k * 2 * H + h - 3)
                    ins = v.tensor_tensor_reduce(dump[:, (h % 4) * C:(h % 4 + 1) * C], Wt[:, k, (h % H) * C:(h % H + 1) * C], att[:, h, :], 1.0, 0.0,
                                                 ALU.mult, ALU.add, wa[:, k, h:h + 1]).then_inc(s["wa_ready"], 1)

            eng.wait_ge(s["blocks_in"], 16 * 3 * G)
            v.tensor_copy(src_f, src_i)
            then(v.tensor_copy(dst_f, dst_i))
            v.tensor_copy(ends2, dst_f[:, :, 0:EB:EB - 1]).then_inc(s["block_tips"], 1)
            for g in range(G):
                ins = v.tensor_scalar(rel_f[:, g, :], dst_f[:, g, :], j128[:, g:g + 1], None, ALU.subtract)
            then(ins)
            v.tensor_scalar(rel_c, rel_f, -1.0, float(P), ALU.max, ALU.min).then_inc(s["rel_clamped"], 1)
            v.tensor_tensor(brk[:, 0, :, 1:EB], dst_f[:, :, 1:EB], dst_f[:, :, 0:EB - 1], ALU.not_equal)
            v.tensor_tensor(brk[:, 1, :, 0:EB - 1], dst_f[:, :, 1:EB], dst_f[:, :, 0:EB - 1], ALU.not_equal)
            eng.wait_ge(s["block_tips_turned"], 1)
            v.tensor_copy(shift[0:2, 1:VPAD + 1], bank[7][0:2, 0:VPAD]).then_inc(s["tips_shifted"], 1)
            eng.wait_ge(s["tips_back"], 1)
            then(v.tensor_copy(near, bank[4][:, 0:4 * G].rearrange("p (a g k) -> p a g k", a=2, g=G)))
            v.tensor_tensor(brk[:, 0, :, 0:1], dst_f[:, :, 0:1], near[:, 0, :, 1:2], ALU.not_equal)
            then(v.tensor_tensor(brk[:, 1, :, EB - 1:EB], dst_f[:, :, EB - 1:EB], near[:, 1, :, 0:1], ALU.not_equal))
            eng.sem_inc(s["edge_turned"], 1)
            then(v.tensor_scalar(pen.rearrange("p a g e -> p (a g e)"), brk.rearrange("p a g e -> p (a g e)"), -BIG, None,
                                 ALU.mult))

            def turned(n, to, width=1):
                eng.wait_ge(s["edge_taken"], n + 1)
                for g in range(G):
                    cnt = min(P, VISITS - g * P)
                    src = bank[n][:, g * HALF * P:(g + 1) * HALF * P].rearrange("p (a s) -> p s a", a=HALF)[:, 0:cnt, :]
                    dst = to[:, g * P * HALF:(g * P + cnt) * HALF].rearrange("p (s a) -> p s a", a=HALF)
                    ins = v.tensor_copy(dst, src)
                return ins

            v.memset(srcT[:, :].bitcast(F32), 0.0)
            v.memset(relT[:, :], -1.0)
            then(v.memset(lastT, 0.0))
            turned(0, srcT[:, :]).then_inc(s["src_index_ready"], 1)
            turned(1, relT[:, :])
            turned(2, valv[:, :, 2 * H])
            then(turned(3, lastT))
            eng.sem_inc(s["edge_taken"], 4)

            eng.wait_ge(s["xT_scored"], 5 + NT)
            then(v.tensor_copy(tab[:, :], bank[5][:, 0:NT * 2 * H]))
            eng.sem_inc(s["scores_out"], 1)
            then(v.tensor_copy(tab3[:, :, 0, :], tabv))
            then(v.tensor_tensor(res, tabv, tab3[:, :, 0, :], ALU.subtract))
            then(v.tensor_copy(tab3[:, :, 1, :], res))
            then(v.tensor_tensor(res, res, tab3[:, :, 1, :], ALU.subtract))
            v.tensor_copy(tab3[:, :, 2, :], res).then_inc(s["node_parts"], 1)

            def take_spread(i, b):
                eng.wait_ge(s["hotT_used"], i * 5 + b + 1)
                v.tensor_reduce(adT.rearrange("p u k -> p (u k)")[:, bass.ds(i * (5 * 8 * 2 * H) + b * 8 * 2 * H, 8 * 2 * H)]
                                .rearrange("p (u k) -> p u k", u=8),
                                bank[b][:, 0:8 * 24].rearrange("p (u t k) -> p u k t", u=8, t=3), AX.X, ALU.add) \
                    .then_inc(s["spread_taken"], 1)

            with eng.Fori(0, 11) as i:
                for b in range(5):
                    eng.wait_ge(s[f"rel_bc{b}"], i * 16 + 16)
                    v.tensor_scalar(hotT[b], rel_bc[b], visit_no[:, 0:1], None, ALU.is_equal).then_inc(s["hotT_ready"], 1)
                for b in range(5):
                    take_spread(i, b)
            eng.wait_ge(s["spread_taken"], 5 + 55)

            then(v.tensor_single_scalar(lo_i, srcT[:, :], P - 1, ALU.bitwise_and))
            then(v.tensor_copy(lo_f, lo_i))
            then(v.tensor_single_scalar(lo_i, srcT[:, :], 7, ALU.arith_shift_right))
            v.tensor_copy(hi_f, lo_i)
            then(v.tensor_scalar(wokT, relT[:, :], 0.0, None, ALU.is_ge))
            then(v.scalar_tensor_tensor(okT, relT[:, :], float(P - 1), wokT, ALU.is_le, ALU.mult))
            then(v.tensor_tensor(wokT[:, 0:TILES], okT[:, 0:TILES], valv[:, 0:TILES, 2 * H], ALU.mult))
            eng.sem_inc(s["histo_flags"], 1)
            with eng.Fori(0, ITERS) as i:
                for q in range(RING):
                    eng.wait_ge(s["histo_used"], i * RING + q + 1)
                    u = bass.ds(i * RING + q, 1)
                    v.tensor_scalar(hots[:, q % 4, 0:P], iota_f[:, 0:P], lo_f[:, u], None, ALU.is_equal)
                    v.tensor_scalar(hots[:, q % 4, P:P + NT], iota_f[:, 0:NT], hi_f[:, u], okT[:, u], ALU.is_equal, ALU.mult)
                    v.tensor_scalar(hots[:, q % 4, P + NT:P + 2 * NT], iota_f[:, 0:NT], hi_f[:, u], wokT[:, u],
                                    ALU.is_equal, ALU.mult).then_inc(s["histo_ready"], 1)
            eng.wait_ge(s["histo_done"], 1)
            then(v.tensor_scalar(hist_f[:, 0:NT], bank[4][:, 0:NT], 1.0, None, ALU.max))
            then(v.tensor_scalar(hist_f[:, 2 * NT:3 * NT], bank[4][:, 0:NT], 0.0, None, ALU.is_equal))
            then(v.tensor_tensor(hist_f[:, NT:2 * NT], bank[4][:, NT:2 * NT], hist_f[:, 2 * NT:3 * NT], ALU.add))
            eng.sem_inc(s["factors_in"], 1)
            eng.wait_ge(s["factors_out"], 1)
            then(v.tensor_tensor(hist_f[:, 2 * NT:3 * NT], hist_f[:, 0:NT], hist_f[:, NT:2 * NT], ALU.mult))
            then(v.reciprocal(fsrc[:, :], hist_f[:, 2 * NT:3 * NT]))

            eng.wait_ge(s["as_turned"], H)

            def scan(side, h, g, first):
                o, p_, d_ = seg[:, side, h, g, :], pen[:, side, g, :], bank[h][:, g * EB:(g + 1) * EB]
                if side:
                    o, p_, d_ = o[:, ::-1], p_[:, ::-1], d_[:, ::-1]
                return v.tensor_tensor_scan(o, p_, d_, -BIG if first else seed[:, side, g, h:h + 1], ALU.add, ALU.max)

            for side in range(2):
                for h in range(H):
                    for g in range(G):
                        ins = scan(side, h, g, True)
            then(ins)
            for side in range(2):
                v.tensor_copy(tip[:, side], seg[:, side, :, :, EB - 1 if side == 0 else 0].rearrange("p h g -> p g h"))
                for h in range(H):
                    ins = v.tensor_reduce(rst[:, side, :, h], pen[:, side], AX.X, ALU.min)
            ins.then_inc(s["first_scan"], 1)
            eng.wait_ge(s["carry_turned"], 1)
            then(v.tensor_copy(rst_h[0:H], bank[6][0:H, :].rearrange("p (a n) -> p a n", a=2)))
            v.tensor_tensor_scan(carry[0:H, 0, 1:VPAD + 1], rst_h[0:H, 0, :], bank[5][0:H, 0:VPAD], -BIG, ALU.add, ALU.max)
            then(v.tensor_tensor_scan(carry[0:H, 1, 0:VPAD][:, ::-1], rst_h[0:H, 1, ::-1],
                                      bank[5][0:H, VPAD:2 * VPAD][:, ::-1], -BIG, ALU.add, ALU.max))
            eng.sem_inc(s["carry_ready"], 1)
            eng.wait_ge(s["seeds_turned"], 1)
            then(v.tensor_copy(seed, bank[7][:, 0:2 * G * H].rearrange("p (a g h) -> p a g h", a=2, g=G)))
            for h in range(H):
                for side in range(2):
                    for g in range(G):
                        ins = scan(side, h, g, False)
                then(ins)
                v.tensor_tensor(seg[:, 0, h], seg[:, 0, h], seg[:, 1, h], ALU.max).then_inc(s["seg_ready"], 1)
            eng.wait_ge(s["seg_ready"], H)
            mm = seg.rearrange("p a h g e -> p (a h g e)")[:, H * G * EB:H * G * EB + TILES * H].rearrange("p (u h) -> p u h", h=H)
            for h in range(H):
                eng.wait_ge(s["seg_turned"], h + 1)
                for g in range(G):
                    cnt = min(P, VISITS - g * P)
                    src = bank[4 + h][:, g * HALF * P:(g + 1) * HALF * P].rearrange("p (a s) -> p s a", a=HALF)[:, 0:cnt, :]
                    u = slice(g * P * HALF, (g * P + cnt) * HALF)
                    ins = v.tensor_copy(mm[:, u, h].rearrange("p (s a) -> p s a", a=HALF), src)
            then(ins)
            then(v.tensor_tensor(mm, mm, adT[:, :, 0:H], ALU.max))
            then(v.tensor_tensor(mm, mm, adT[:, :, H:2 * H], ALU.add))
            then(v.scalar_tensor_tensor(mm, mm, SLOPE, mm, ALU.mult, ALU.max))
            then(v.tensor_tensor(adT[:, :, 0:H], asT3[:, 0:TILES, :], adT[:, :, H:2 * H], ALU.add))
            then(v.scalar_tensor_tensor(adT[:, :, 0:H], adT[:, :, 0:H], SLOPE, adT[:, :, 0:H], ALU.mult, ALU.max))
            v.tensor_tensor(adT[:, :, 0:H], adT[:, :, 0:H], mm, ALU.subtract).then_inc(s["exp_in"], 1)
            for h in range(H):
                ins = v.tensor_tensor(valv[:, 0:TILES, H + h], mm[:, :, h], lastT[:, 0:TILES], ALU.mult)
            then(ins)
            eng.wait_ge(s["exp_out"], 1)
            for layer in range(2):
                eng.sem_inc(s[f"rows_used{layer}"], VPI)
                eng.sem_inc(s[f"sums_taken{layer}"], 2)
            for name in ("x_free", "mixed", "sums_read", "product_taken", "x1_free"):
                eng.sem_inc(s[name], 2)
            then(v.memset(sums[:, :], 0.0))

            def build(layer, i, k, n):
                eng.wait_ge(s[f"rows_used{layer}"], n + 3)
                for h2 in range(HALF):
                    u, slot = i * RING + 2 * k + h2, (2 * k + h2) % 4
                    w = u * NV + 2 * H
                    ins = v.tensor_scalar(hots[:, slot, 0:P], iota_f[:, 0:P], relT[:, bass.ds(u, 1)],
                                          None if layer == 0 else vals[:, bass.ds(w, 1)],
                                          *((ALU.is_equal,) if layer == 0 else (ALU.is_equal, ALU.mult)))
                ins.then_inc(s[f"hot_ready{layer}"], 1)
                if layer == 0:
                    for h2 in range(HALF):
                        u, slot = i * RING + 2 * k + h2, (2 * k + h2) % 4
                        for h in range(2):
                            ins = v.tensor_scalar(hots[:, slot, (1 + h) * P:(2 + h) * P], iota_f[:, 0:P],
                                                  relT[:, bass.ds(u, 1)], vals[:, bass.ds(u * NV + h, 1)],
                                                  ALU.is_equal, ALU.mult)
                    ins.then_inc(s["scaled_v0"], 1)

            def take_sums(layer, i, k):
                n = i * VPI + k
                j = eng.value_load(tile_of[0:1, bass.ds(n, 1)], min_val=0, max_val=NT - 1)
                eng.wait_ge(s[f"rows_used{layer}"], n + VPI + 1)
                eng.wait_ge(s[f"sums_taken{layer}"], n + 2)
                to = sums[:, bass.ds(j * D, D)]
                ins = v.tensor_tensor(to, to, pair(k % 2).rearrange("p c n -> p (c n)"), ALU.add)
                if layer == 0:
                    to = nodesum[:, bass.ds(j * NV, NV)]
                    ins = v.tensor_tensor(to, to, bank[4 + k % 2][:, 0:NV], ALU.add)
                ins.then_inc(s[f"sums_taken{layer}"], 1)

            def edge_loop(layer):
                build(layer, 0, 0, 0)
                with eng.Fori(0, ITERS) as i:
                    for k in range(VPI):
                        build(layer, i, k + 1, i * VPI + k + 1)
                        take_sums(layer, i, k)
                eng.wait_ge(s[f"sums_taken{layer}"], 2 + VISITS)

            eng.sem_inc(s["scaled_v1"], VISITS)
            edge_loop(0)

            tv = t_self.rearrange("p (j h) -> p j h", h=H)
            cv = c_self[:, 0:NT * H].rearrange("p (j h) -> p j h", h=H)
            rv = r_self.rearrange("p (j h) -> p j h", h=H)
            v.memset(c_self[:, NT * H:], 0.0)
            v.memset(ones1, 1.0)
            v.memset(zero1[:, :], 0.0)
            then(v.tensor_tensor(tv, tabv[:, :, 0:H], tabv[:, :, H:2 * H], ALU.add))
            then(v.scalar_tensor_tensor(t_self, t_self, SLOPE, t_self, ALU.mult, ALU.max))
            then(v.tensor_tensor(tv, nodev[:, :, H:2 * H], tv, ALU.subtract))
            then(v.tensor_scalar(fdst[:, :], nodev[:, :, NV - 1], 0.0, None, ALU.is_gt))
            for h in range(H):
                ins = v.tensor_tensor(tv[:, :, h], tv[:, :, h], fdst[:, :], ALU.mult)
            ins.then_inc(s["self_in"], 1)
            sq = mix[1][:, 0:2 * NT]
            eng.wait_ge(s["self_in"], 1)
            then(v.tensor_scalar(fdst[:, :], nodev[:, :, NV - 1], 0.0, None, ALU.is_equal))
            v.tensor_scalar(sq[:, 0:NT], nodev[:, :, NV - 1], 1.0, None, ALU.max)
            v.tensor_tensor(sq[:, NT:2 * NT], nodev[:, :, 2 * H], fdst[:, :], ALU.add).then_inc(s["dst_sq_in"], 1)
            eng.wait_ge(s["self_out"], 1)
            then(v.tensor_tensor(rv, nodev[:, :, 0:H], tv, ALU.add))
            then(v.reciprocal(r_self, r_self))
            then(v.tensor_tensor(cv, tv, rv, ALU.mult))
            eng.wait_ge(s["dst_sq_out"], 1)
            then(v.tensor_tensor(sq[:, 0:NT], sq[:, 0:NT], sq[:, NT:2 * NT], ALU.mult))
            then(v.reciprocal(fdst[:, :], sq[:, 0:NT]))
            eng.sem_inc(s["self_ready"], 1)

            def normalize(layer, j, b, to):
                for c in range(2):
                    ins = v.bn_stats(stats[b][:, c * 6:(c + 1) * 6], mix[b][:, c * 512:(c + 1) * 512])
                then(ins)
                eng.sem_inc(s["vector_passed"], 1)
                then(v.bn_aggr(moments[b], stats[b]))
                v.tensor_scalar(spread[b][:, 0:1], moments[b][:, 1:2], EPS, None, ALU.add).then_inc(s[f"variance{layer}"], 1)
                eng.wait_ge(s[f"deviation{layer}"], j + 1)
                then(v.reciprocal(spread[b][:, 0:1], spread[b][:, 1:2]))
                return v.tensor_scalar(to, mix[b], moments[b][:, 0:1], spread[b][:, 0:1], ALU.subtract, ALU.mult)

            def finish0(j, b, first=False):
                eng.wait_ge(s["mixed"], j + 3)
                for h in range(H):
                    ins = v.scalar_tensor_tensor(mix[b][:, h * C:(h + 1) * C], sums[:, bass.ds(j * D + h * C, C)],
                                                 r_self[:, bass.ds(j * H + h, 1)],
                                                 psum[:, 2 * b + h // 2, (h % 2) * C:(h % 2 + 1) * C], ALU.mult, ALU.add)
                ins.then_inc(s["sums_read"], 1)
                eng.wait_ge(s["sums_read"], j + 3)
                then(v.scalar_tensor_tensor(mix[b], mix[b], 0.0, x_in[b], ALU.max, ALU.add))
                if not first:
                    eng.wait_ge(s[f"x1_stored{b}"], turn_of(j, b) * 16)
                v.tensor_copy(x1_out[b][:, D:D + 1], fsrc[:, bass.ds(j + 0, 1)])
                normalize(0, j, b, x1_out[b][:, 0:D]).then_inc(s["x1_ready"], 1)
                eng.wait_ge(s["x1_ready"], j + 1)
                eng.sem_inc(s["x_free"], 1)

            def tiles_with_first(finish, per):
                finish(0, 0, True)
                finish(1, 1, True)
                with eng.Fori(1, NT // 2) as i:
                    order.enter(i - 1, 2 * per)
                    finish(Tile(i, 0), 0)
                    finish(Tile(i, 1), 1)
                    order.leave(NT // 2 - 1)
                finish(NT - 1, 0)

            for b in range(2):
                v.memset(x1_out[b][:, D:], 0.0)
            tiles_with_first(finish0, 4)
            edge_loop(1)

            def finish1(j, b, first=False):
                eng.wait_ge(s["product_ready"], j + 1)
                if not first:
                    eng.wait_ge(s[f"out_stored{b}"], turn_of(j, b) * 16)
                v.tensor_tensor(mix[b], pair(b).rearrange("p c n -> p (c n)"), bias_at, ALU.add) \
                    .then_inc(s["product_taken"], 1)
                eng.wait_ge(s["product_taken"], j + 3)
                eng.wait_ge(s[f"x1_in{b}"], turn_of(j, b) * 16 + 16)
                then(v.scalar_tensor_tensor(mix[b], mix[b], 0.0, x1_in[b], ALU.max, ALU.add))
                eng.sem_inc(s["x1_free"], 1)
                normalize(1, j, b, mix[b]).then_inc(s["out_ready"], 1)

            eng.wait_ge(s["bias1_in"], 16)
            tiles_with_first(finish1, 4)


def kernel(x, src, dst, edge_weight, L0_gnn_W, L0_gnn_att_src, L0_gnn_att_dst, L0_gnn_bias, L1_gnn_W, L1_gnn_b):
    import numpy as np
    import concourse.bacc as bacc
    from concourse.bass_utils import run_bass_kernel_spmd

    x = np.asarray(x)
    xpad = np.zeros((NP, D), x.dtype)
    xpad[:N] = x

    def blocks(v, fill):
        v = np.asarray(v)
        b = np.full(((NB + 1) * EB,), fill, v.dtype)
        b[:E] = v
        return b.reshape(NB + 1, EB)

    arrays = {
        "xT": np.ascontiguousarray(xpad.T), "x": xpad,
        "src_blocks": blocks(src, NP - 1), "dst_blocks": blocks(dst, NP - 1), "w_blocks": blocks(edge_weight, 1),
        "W0": np.asarray(L0_gnn_W), "att_src": np.asarray(L0_gnn_att_src), "att_dst": np.asarray(L0_gnn_att_dst),
        "bias0": np.asarray(L0_gnn_bias), "W1": np.asarray(L1_gnn_W), "bias1": np.asarray(L1_gnn_b),
    }
    nc = bacc.Bacc("TRN2", target_bir_lowering=False, num_devices=1)
    args = {n: nc.dram_tensor(n, v.shape, mybir.dt.from_np(v.dtype), kind="ExternalInput").ap() for n, v in arrays.items()}
    out = nc.dram_tensor("out", (N, D), F32, kind="ExternalOutput").ap()
    gnn_kernel(nc, **args, out=out)
    r = run_bass_kernel_spmd(nc, [arrays], core_ids=[0])
    return r.results[0]["out"]
```

```python
from contextlib import ExitStack

import concourse.bass as bass
from concourse import mybir

P = 128
N = 3125
NT = -(-N // P)
NP = NT * P
D = 1024
KT = D // P
H = 4
C = D // H
E = 50000
EB = P
NB = -(-E // EB)
RING = 8
ITERS = -(-(NB + NT - 1) // RING)
VISITS = ITERS * RING
G = -(-VISITS // P)
VPAD = G * P
STEP = -(-VISITS // NT)
SPREAD = NT * STEP
AHEAD = 2
ROW1 = D + 4
NV = 10
BIG = float(2.0 ** 100)
SLOPE = 0.2
EPS = 1e-5
XP_BANKS = ((0, 1), (2, 3), (5, 6))
assert SPREAD <= VPAD and VISITS + AHEAD <= SPREAD and NT % 5 == 0

ALU = mybir.AluOpType
ACT = mybir.ActivationFunctionType
AX = mybir.AxisListType
F32 = mybir.dt.float32
BF16 = mybir.dt.bfloat16
I32 = mybir.dt.int32


class Tally:

    def __init__(self, sem):
        self.sem, self.n, self.off, self.start = sem, 0, 0, 0

    def inc(self, ins):
        ins.then_inc(self.sem, 1)
        self.n += 1

    def value(self):
        return self.off + self.n

    def enter(self, i, per):
        self.off, self.start, self.per = i * per, self.n, per

    def leave(self, count):
        assert self.n - self.start == self.per, (self.n - self.start, self.per)
        self.off, self.n = 0, self.start + count * self.per


class Tile:

    def __init__(self, turn, slot):
        self.turn, self.at = turn, turn * 2 + slot

    def __add__(self, n):
        return self.at + n

    def __sub__(self, n):
        return self.at - n

    def __mul__(self, n):
        return self.at * n


def gnn_kernel(nc, xT, x, src_blocks, dst_blocks, w_blocks, W0, att_src, att_dst, bias0, W1, bias1, out):
    ctx = ExitStack()
    with ctx:
        def sb(name, shape, dt=F32):
            return ctx.enter_context(nc.sbuf_tensor(name, shape, dt))

        def sem(name):
            return ctx.enter_context(nc.semaphore(name))

        xp_dram = nc.dram_tensor("xp_rows", [NP, D], F32, kind="Internal").ap()
        as_dram = nc.dram_tensor("source_scores", [NP, H], F32, kind="Internal").ap()
        rel_dram = nc.dram_tensor("relative_dst", [VPAD, EB], BF16, kind="Internal").ap()
        x1_dram = nc.dram_tensor("x1_rows", [NP, ROW1], F32, kind="Internal").ap()

        psum = ctx.enter_context(nc.psum_tensor("psum", [P, 8, 512], F32))
        bank = [psum[:, i, :] for i in range(8)]

        def pair(b):
            return psum[:, 2 * b:2 * b + 2, :]


        sums = sb("sums", [P, NT * D])
        Wt = sb("Wt", [P, KT, D])
        rows = sb("rows", [P, RING * ROW1])
        vals = sb("vals", [P, SPREAD * NV])
        relT = sb("relT", [P, VPAD])
        srcT = sb("srcT", [P, VPAD], I32)
        hots = sb("hots", [P, 4, (1 + H) * P])
        iota_f = sb("iota_f", [P, EB])
        ident = sb("ident", [P, P])
        visit_no = sb("visit_no", [P, G])
        tab = sb("tab", [P, NT * 2 * H])
        nodesum = sb("nodesum", [P, NT * NV])
        tile_of = sb("tile_of", [1, VPAD], I32)
        fsrc = sb("fsrc", [P, NT])
        idx = sb("idx", [P, RING], I32)
        fdst = sb("fdst", [P, NT])
        zero1 = sb("zero1", [P, 1])

        valv = vals[:, :].rearrange("p (u k) -> p u k", k=NV)
        nodev = nodesum[:, :].rearrange("p (j k) -> p j k", k=NV)
        tabv = tab[:, :].rearrange("p (j k) -> p j k", k=2 * H)

        def cut(tensor, at, n):
            return tensor[:, at:at + n]

        xT_flat = [cut(rows, b * D, D) for b in range(5)]
        xT_ring = [f.rearrange("p (k n) -> p k n", k=KT) for f in xT_flat]
        xp_stage = [cut(rows, (5 + b) * D, D) for b in range(2)]

        row_ring = [cut(rows, q * ROW1, ROW1) for q in range(RING)]
        x_in = [cut(rows, b * D, D) for b in range(2)]
        xp_in = [cut(rows, (2 + b) * D, D) for b in range(2)]
        mix = [cut(rows, (4 + b) * D, D) for b in range(2)]
        x1_out = [cut(rows, 6 * D + b * ROW1, ROW1) for b in range(2)]
        agg = [cut(rows, b * D, D) for b in range(2)]
        aggT = [cut(rows, (2 + b) * D, D).rearrange("p (k n) -> p k n", k=KT) for b in range(2)]
        x1_in = [cut(rows, (6 + b) * D, D) for b in range(2)]

        hots_flat = hots[:, :, :].rearrange("p q c -> p (q c)")
        bias_at = hots_flat[:, 0:D]
        diag = [hots_flat[:, D + b * H * P:D + (b + 1) * H * P] for b in range(2)]
        spare = hots_flat[:, 2 * D:]
        r_self = spare[:, 0:NT * H]
        c_self = spare[:, 104:104 + (NT + 1) * H]
        t_self = spare[:, 208:208 + NT * H]
        stats = [spare[:, 312 + b * 20:312 + b * 20 + 12] for b in range(2)]
        moments = [spare[:, 312 + b * 20 + 12:312 + b * 20 + 14] for b in range(2)]
        spread = [spare[:, 312 + b * 20 + 14:312 + b * 20 + 16] for b in range(2)]
        ones1 = spare[0:1, 352:352 + P]

        place = [0]

        def take(n):
            at = place[0]
            place[0] += n
            assert place[0] <= NT * D
            return cut(sums, at, n)

        def take3(a, b):
            return take(a * b).rearrange("p (a b) -> p a b", a=a)

        ad_flat = take(SPREAD * 2 * H)
        adT = ad_flat.rearrange("p (u k) -> p u k", k=2 * H)
        att = ad_flat[:, 0:2 * H * C].rearrange("p (h c) -> p h c", c=C)
        dump = ad_flat[:, 2 * H * C:2 * H * C + 4 * C]
        brk = take(2 * G * EB).rearrange("p (a g e) -> p a g e", a=2, g=G)
        lastT = take(VPAD)
        asT = take(RING * H + VPAD * H)
        seg = take(2 * H * G * EB).rearrange("p (a h g e) -> p a h g e", a=2, h=H, g=G)
        tip = take(2 * G * H).rearrange("p (a g h) -> p a g h", a=2, g=G)
        rst = take(2 * G * H).rearrange("p (a g h) -> p a g h", a=2, g=G)
        rst_flat, carry_flat = take(2 * VPAD), take(2 * (VPAD + 1))
        rst_h = rst_flat.rearrange("p (a u) -> p a u", a=2)
        carry = carry_flat.rearrange("p (a u) -> p a u", a=2)
        seed = take(2 * G * H).rearrange("p (a g h) -> p a g h", a=2, g=G)
        stage = [take(4 * H) for _ in range(2)]
        hist_f = take(4 * NT)
        late = place[0]
        wa = take3(KT, 2 * H)
        rows_of_nb = take(3 * NB)
        iota_i = rows_of_nb[:, 0:NB].bitcast(I32)
        iota_w, tmp_row = (rows_of_nb[:, n * NB:(n + 1) * NB] for n in (1, 2))
        visit_i = take(G).bitcast(I32)
        iota_b = take(P // 2).bitcast(BF16)
        tcount = take(G)
        mask = take(NB)
        ksel = take(G)
        jv = take(G)
        jv2 = take(G)
        j128 = take(G)
        block_i = take(G).bitcast(I32)
        dst_flat, src_flat, w_flat, rel_flat = (take(G * EB) for _ in range(4))
        dst_i, src_i = (f.rearrange("p (g e) -> p g e", g=G).bitcast(I32) for f in (dst_flat, src_flat))
        w_f = w_flat.rearrange("p (g e) -> p g e", g=G)
        rel_f = rel_flat.rearrange("p (g e) -> p g e", g=G)
        parts_of_dst = take(5 * G * EB // 2)
        dst_f, src_f = (parts_of_dst[:, n * G * EB:(n + 1) * G * EB].rearrange("p (g e) -> p g e", g=G) for n in range(2))
        rel_c = parts_of_dst[:, 2 * G * EB:].bitcast(BF16).rearrange("p (g e) -> p g e", g=G)
        ends2 = take3(G, 2)
        shift = take(VPAD + 2)
        near = take(4 * G).rearrange("p (a g k) -> p a g k", a=2, g=G)
        lo_i = dst_f.rearrange("p g e -> p (g e)").bitcast(I32)
        hi_i = src_f.rearrange("p g e -> p (g e)").bitcast(I32)
        lo_f, hi_f, okT, wok = dst_flat, src_flat, w_flat, rel_flat
        w_part = take(3 * VPAD // 2).bitcast(BF16).rearrange("p (t u) -> p t u", t=3)
        zeros = take(P)
        near_tab = take(SPREAD * 3 * 2 * H // 2).bitcast(BF16)
        near_tab4 = near_tab.rearrange("p (u t k) -> p u t k", t=3, k=2 * H)
        tabT = carry_flat[0:NT, 0:2 * H * P]
        chosen = rst_flat[0:NT, 0:VPAD]
        tile_row = rst_flat[0:1, VPAD:2 * VPAD]
        print('PLACE',place[0],late,W2 if 0 else 0,NT*D)
        asT3 = asT.rearrange("p (u h) -> p u h", h=H)[:, RING:, :]
        seg_flat = seg.rearrange("p a h g e -> p (a h g e)")
        ends_i, ends_t, ends_f, endk = (seg_flat[:, n * 2 * NB:(n + 1) * 2 * NB] for n in range(4))
        ends_i, ends_t = ends_i.bitcast(I32), ends_t.bitcast(I32)
        span, ones_row = (seg_flat[:, n * NB:(n + 1) * NB] for n in (8, 9))
        ones_tiles = tip.rearrange("p a g h -> p (a g h)")[0:1, 0:NT]
        W2 = STEP * P // 2
        rel_bc = [seg_flat[:, b * W2:(b + 1) * W2].bitcast(BF16) for b in range(2)]
        hi_w = STEP * 4 * NT // 2
        hi_hot = [seg_flat[:, 2 * W2 + b * hi_w:2 * W2 + (b + 1) * hi_w].bitcast(BF16)
                  .rearrange("p (u t n) -> p u t n", u=STEP, t=4) for b in range(2)]
        hotT = [hots_flat[:, b * W2:(b + 1) * W2].bitcast(BF16) for b in range(2)]
        lo_hot = [free[:, 0:W2].bitcast(BF16) for free in (parts_of_dst, rows_of_nb)]
        last = lastT
        visit_tab = valv[:, :, 0:2 * H]

        s = {}

        def S(name):
            if name not in s:
                s[name] = sem(name)
            return s[name]

        for name in """vector_order vector_passed pool_order pool_passed consts ends_in W0_in att_in xT_in0 xT_in1 xT_in2 xT_in3 xT_in4
            xT_scored block_ends_ready block_ends_spread blocks_known blocks_in tiles_ready tiles_turned
            rel_clamped rel_stored rel_bc0 rel_bc1 rel_bc2 rel_bc3 rel_bc4 tile_row_ready tile_row_spread scores_turned chosen_ready visit_tab_done visit_tab_taken scratch_used sums_zero0 last_taken hotT_ready hotT_used
            spread_done spread_taken block_tips block_tips_turned tips_shifted tips_back wa_ready scores_out scores_stored
            edge_turned edge_taken src_index_ready xp_done xp_taken xp_copied xp_stored0 xp_stored1 W1_in
            index_copied scores_got0 scores_got1 source_scores_ready histo_ready histo_used histo_done histo_flags
            as_turned first_scan carry_turned carry_ready seeds_turned seg_ready seg_turned seg_taken exp_in exp_out
            weights_in0 sums_zero factors_in factors_out
            rows_in0 rows_in1 rows_in2 rows_in3 rows_in4 rows_in5 rows_in6 rows_in7
            rows_used0 rows_used1 hot_ready0 hot_ready1 scaled_v0 scaled_v1 scaled_a0 scaled_a1 sums_taken0 sums_taken1
            bias0_in bias1_in x_in0 x_in1 self_in self_out self_ready diag_ready mixed sums_read variance0 variance1
            deviation0 deviation1 x_free x1_ready x1_stored0 x1_stored1
            agg_ready agg_turned aggT_ready product_ready product_taken x1_free x1_in0 x1_in1 out_ready out_stored0 out_stored1
            dst_sq_in dst_sq_out sums_zero1""".split():
            S(name)

        v, a, pe, gp, sp = nc.vector, nc.scalar, nc.tensor, nc.gpsimd, nc.sync

        def by_tiles(eng, body):
            with eng.Fori(0, NT // 2) as i:
                body(Tile(i, 0), 0)
                body(Tile(i, 1), 1)
            body(NT - 1, 0)

        def turn_of(j, b):
            return (j - b) // 2 if isinstance(j, int) else j.turn

        def ahead(eng, body):
            with eng.Fori(0, (NT - 3) // 2) as i:
                body(Tile(i, 0), 0)
                body(Tile(i, 1), 1)
            body(NT - 3, 0)

        def by_visits(eng, body):
            with eng.Fori(0, ITERS) as i:
                for k in range(RING):
                    body(i, k)

        def by_steps(eng, body):
            with eng.Fori(0, NT // 5) as i:
                for b in range(5):
                    body(i, b)

        def load_xT(eng, slots):
            with eng.Fori(0, NT // 5) as i:
                for b in slots:
                    eng.wait_ge(s["xT_scored"], i * 5 + b + 1)
                    eng.dma_start(xT_flat[b], xT[bass.ds(i * (5 * P) + b * P, P), :]).then_inc(s[f"xT_in{b}"], 16)

        block = ctx.enter_context(nc.Block())

        @block.sync
        def _(eng):
            with nc.allow_non_contiguous_dma(reason="two words of each block"):
                eng.dma_start(ends_i[0:1, 0:NB], dst_blocks[0:NB, 0:1].rearrange("b e -> e b")).then_inc(s["ends_in"], 16)
                eng.dma_start(ends_i[0:1, NB:2 * NB],
                              dst_blocks[0:NB, EB - 1:EB].rearrange("b e -> e b")).then_inc(s["ends_in"], 16)
            eng.dma_start(Wt[:, :, :], W0.rearrange("(k p) n -> p k n", p=P)).then_inc(s["W0_in"], 16)
            eng.dma_start(att[:, 0:H, :], att_src.unsqueeze(0).broadcast_to([P, H, C])).then_inc(s["att_in"], 16)
            eng.dma_start(att[:, H:2 * H, :], att_dst.unsqueeze(0).broadcast_to([P, H, C])).then_inc(s["att_in"], 16)

            load_xT(eng, (0, 2, 4))
            eng.wait_ge(s["rel_clamped"], 1)
            eng.dma_start(rel_dram.rearrange("(g s) e -> s g e", g=G), rel_c).then_inc(s["rel_stored"], 16)
            eng.wait_ge(s["rel_stored"], 16)
            flat = rel_dram.rearrange("s e -> (s e)").unsqueeze(0)
            for b in range(5):
                eng.wait_ge(s["xT_scored"], NT + b + 1)
                eng.dma_start(xT_flat[b], xT[b * P:(b + 1) * P, :]).then_inc(s[f"xT_in{b}"], 16)

            def load_rel(i, b):
                eng.wait_ge(s["hotT_ready"], i * 5 + b + (2 if b == 0 else 1))
                eng.dma_start(rel_bc[b % 2], flat[:, bass.ds(i * (5 * STEP * P) + b * STEP * P, STEP * P)]
                              .broadcast_to([P, STEP * P])).then_inc(s[f"rel_bc{b}"], 16)

            with eng.Fori(0, NT // 5 - 1) as i:
                for b in range(5):
                    load_rel(i, b)
                    eng.wait_ge(s["xp_done"], i * 10 + 2 * b + 2)
                    eng.dma_start(xT_flat[b], xT[bass.ds(i * (5 * P) + (5 + b) * P, P), :]).then_inc(s[f"xT_in{b}"], 16)
            for b in range(5):
                load_rel(NT // 5 - 1, b)
            eng.wait_ge(s["xp_done"], 2 * NT)
            eng.dma_start(Wt[:, :, :], W1.rearrange("(k p) n -> p k n", p=P)).then_inc(s["W1_in"], 16)

            eng.wait_ge(s["rows_used0"], RING + VISITS)
            eng.wait_ge(s["hot_ready0"], VISITS + AHEAD)
            eng.dma_start(bias_at[0:1, :], bias0.unsqueeze(0)).then_inc(s["bias0_in"], 16)

            def load_x(j, b):
                eng.wait_ge(s["x_free"], j + 1)
                eng.dma_start(x_in[b], x[bass.ds(j * P, P), :]).then_inc(s[f"x_in{b}"], 16)
                eng.dma_start(xp_in[b], xp_dram[bass.ds(j * P, P), :]).then_inc(s[f"x_in{b}"], 16)

            by_tiles(eng, load_x)

            eng.wait_ge(s["rows_used1"], RING + VISITS)
            eng.wait_ge(s["hot_ready1"], VISITS + AHEAD)
            eng.dma_start(bias_at, bias1.unsqueeze(0).broadcast_to([P, D])).then_inc(s["bias1_in"], 16)

            def load_x1(j, b):
                eng.wait_ge(s["x1_free"], j + 1)
                eng.dma_start(x1_in[b], x1_dram[bass.ds(j * P, P), 0:D]).then_inc(s[f"x1_in{b}"], 16)

            by_tiles(eng, load_x1)

        @block.gpsimd
        def _(eng):
            order = Tally(s["pool_order"])

            def passed(sem, value):
                eng.wait_ge(sem, value)
                eng.sem_inc(s["pool_passed"], 1)

            gp.iota(iota_i, pattern=[[1, NB]], base=0, channel_multiplier=0).then_inc(s["consts"], 1)
            gp.iota(visit_i, pattern=[[P, G]], base=0, channel_multiplier=1).then_inc(s["consts"], 1)
            eng.wait_ge(s["blocks_known"], 1)
            for g in range(G):
                off = bass.IndirectOffsetOnAxis(ap=block_i[:, g:g + 1], axis=0)
                for to, dram in ((dst_i, dst_blocks), (src_i, src_blocks), (w_f, w_blocks)):
                    gp.indirect_dma_start(to[:, g, :], None, dram, off).then_inc(s["blocks_in"], 16)

            eng.wait_ge(s["src_index_ready"], 1)
            eng.wait_ge(s["scores_stored"], 16)

            def gather_scores(half, i, first):
                if not first:
                    passed(s[f"scores_got{half}"], i * 64)
                    order.inc(gp.tensor_copy(asT[:, bass.ds(i * (RING * H) + half * 4 * H, 4 * H)], stage[half]))
                order.inc(gp.tensor_copy(idx[:, half * 4:half * 4 + 4], srcT[:, bass.ds(i * RING + half * 4, 4)]))
                passed(order.sem, order.value())
                for q in range(4):
                    gp.indirect_dma_start(stage[half][:, q * H:(q + 1) * H], None, as_dram,
                                          bass.IndirectOffsetOnAxis(ap=idx[:, half * 4 + q:half * 4 + q + 1], axis=0)) \
                        .then_inc(s[f"scores_got{half}"], 16)

            gather_scores(0, 0, True)
            gather_scores(1, 0, True)
            with eng.Fori(0, ITERS - 1) as i:
                order.enter(i, 4)
                gather_scores(0, i + 1, False)
                gather_scores(1, i + 1, False)
                order.leave(ITERS - 1)
            for half in range(2):
                eng.wait_ge(s[f"scores_got{half}"], 64 * ITERS)
                gp.tensor_copy(asT[:, ITERS * RING * H + half * 4 * H:ITERS * RING * H + half * 4 * H + 4 * H],
                               stage[half]).then_inc(s["source_scores_ready"], 1)

            def gather_rows(layer, table, width):
                def visits(i, k):
                    passed(s[f"rows_used{layer}"], i * RING + k + 2)
                    order.inc(gp.tensor_copy(idx[:, k:k + 2], srcT[:, bass.ds(i * RING + k, 2)]))
                    passed(order.sem, order.value())
                    for q in (k, k + 1):
                        gp.indirect_dma_start(row_ring[q][:, 0:width], None, table,
                                              bass.IndirectOffsetOnAxis(ap=idx[:, q:q + 1], axis=0)) \
                            .then_inc(s[f"rows_in{q}"], 16)

                with eng.Fori(0, ITERS) as i:
                    order.enter(i, RING // 2)
                    for k in range(0, RING, 2):
                        visits(i, k)
                    order.leave(ITERS)

            eng.wait_ge(s["xp_stored0"], 16 * NT * 3 // 5)
            eng.wait_ge(s["xp_stored1"], 16 * NT * 2 // 5)
            gather_rows(0, xp_dram, D)

            def store_x1(j, b):
                eng.wait_ge(s["sums_read"], j + 3)
                gp.tensor_copy(sums[:, bass.ds(j * D, D)], zero1[:, :].broadcast_to([P, D])).then_inc(s["sums_zero1"], 1)
                eng.wait_ge(s["x1_ready"], j + 1)
                gp.dma_start(x1_dram[bass.ds(j * P, P), :], x1_out[b]).then_inc(s[f"x1_stored{b}"], 16)

            by_tiles(eng, store_x1)
            eng.wait_ge(s["x1_stored0"], 16 * (NT - NT // 2))
            eng.wait_ge(s["x1_stored1"], 16 * (NT // 2))
            gather_rows(1, x1_dram, ROW1)

            def store_out(j, b):
                eng.wait_ge(s["out_ready"], j + 1)
                gp.dma_start(out[bass.ds(j * P, P), :], mix[b]).then_inc(s[f"out_stored{b}"], 16)

            with eng.Fori(0, NT // 2) as i:
                store_out(i * 2, 0)
                store_out(i * 2 + 1, 1)
            eng.wait_ge(s["out_ready"], NT)
            gp.dma_start(out[(NT - 1) * P:N, :], mix[0][0:N - (NT - 1) * P, :]).then_inc(s["out_stored0"], 16)
            eng.wait_ge(s["out_stored0"], 16 * (NT - NT // 2))
            eng.wait_ge(s["out_stored1"], 16 * (NT // 2))

        @block.tensor
        def _(eng):
            eng.wait_ge(s["block_ends_ready"], 1)
            for c in range(2):
                ins = pe.matmul(bank[5 + c][:, 0:NB], ones_row[0:1, 0:P], endk[0:1, c * NB:(c + 1) * NB], start=True,
                                stop=True)
            ins.then_inc(s["block_ends_spread"], 1)
            eng.wait_ge(s["tiles_ready"], 1)
            for g in range(G):
                ins = pe.transpose(bank[2][0:1, g * P:(g + 1) * P], jv[:, g:g + 1], ident[:, :])
            ins.then_inc(s["tiles_turned"], 1)
            eng.wait_ge(s["block_tips"], 1)
            for g in range(G):
                ins = pe.transpose(bank[7][0:2, g * P:(g + 1) * P], ends2[:, g, :], ident[:, :])
            ins.then_inc(s["block_tips_turned"], 1)
            eng.wait_ge(s["tips_shifted"], 1)
            for side in range(2):
                for g in range(G):
                    ins = pe.transpose(bank[4][:, (side * G + g) * 2:(side * G + g) * 2 + 2],
                                       shift[0:2, g * P + 2 * side:g * P + 2 * side + P], ident[0:2, 0:2])
            ins.then_inc(s["tips_back"], 1)

            eng.wait_ge(s["edge_turned"], 1)
            for n, item in enumerate((src_f, rel_f, w_f, brk[:, 1])):
                for g in range(G):
                    ins = pe.transpose(bank[(0, 1, 3, 6)[n]][:, g * P:(g + 1) * P], item[:, g, :], ident[:, :])
                ins.then_inc(s["edge_taken"], 1)

            eng.wait_ge(s["wa_ready"], KT * 2 * H)
            with eng.Fori(0, NT // 5) as i:
                for b in range(5):
                    eng.wait_ge(s[f"xT_in{b}"], i * 16 + 16)
                    for k in range(KT):
                        ins = pe.matmul(bank[5][:, bass.ds(i * (5 * 2 * H) + b * 2 * H, 2 * H)], xT_ring[b][:, k, :],
                                        wa[:, k, :], start=(k == 0), stop=(k == KT - 1))
                    ins.then_inc(s["xT_scored"], 1)

            eng.wait_ge(s["tile_row_ready"], 1)
            pe.matmul(bank[2][0:NT, 0:VPAD], ones_tiles[0:1, 0:NT], tile_row, start=True, stop=True) \
                .then_inc(s["tile_row_spread"], 1)
            eng.wait_ge(s["scores_out"], 1)
            for k in range(2 * H):
                ins = pe.transpose(bank[k // 4][0:NT, (k % 4) * P:(k % 4 + 1) * P], tabv[:, :, k], ident[:, :])
            ins.then_inc(s["scores_turned"], 1)
            eng.wait_ge(s["chosen_ready"], 2)
            for k in range(2 * H):
                pe.matmul(bank[k][:, 0:SPREAD], tabT[:, k * P:(k + 1) * P], chosen[:, 0:SPREAD], start=True, stop=True) \
                    .then_inc(s["visit_tab_done"], 1)
            eng.wait_ge(s["visit_tab_taken"], 2 * H)
            eng.wait_ge(s["histo_flags"], 1)

            pe.matmul(bank[4][:, 0:4 * NT], zeros, zeros[:, 0:4 * NT], start=True, stop=False, skip_group_check=True)

            def project(i, b):
                eng.wait_ge(s[f"xT_in{b}"], i * 16 + 16 * (NT // 5) + 16)
                for c in range(2):
                    eng.wait_ge(s["xp_taken"], i * 10 + b * 2 + c + 1)
                    for k in range(KT):
                        ins = pe.matmul(bank[XP_BANKS[b % 3][c]][:, :], xT_ring[b][:, k, :],
                                        Wt[:, k, c * 512:(c + 1) * 512], start=(k == 0), stop=(k == KT - 1))
                    ins.then_inc(s["xp_done"], 1)
                eng.wait_ge(s["hotT_ready"], i * 5 + b + 3)
                eng.wait_ge(s["spread_taken"], i * 5 + b + 1)
                for u in range(STEP):
                    ins = pe.matmul(bank[7][:, u * 24:(u + 1) * 24], hotT[b % 2][:, u * P:(u + 1) * P],
                                    near_tab[:, bass.ds((i * 5 + b) * (STEP * 24) + u * 24, 24)], start=True, stop=True)
                ins.then_inc(s["spread_done"], 1)
                eng.wait_ge(s["histo_ready"], i * 5 + b + 1)
                for u in range(STEP):
                    ins = pe.matmul(bank[4][:, 0:4 * NT], lo_hot[b % 2][:, u * P:(u + 1) * P],
                                    hi_hot[b % 2][:, u, :, :].rearrange("p t n -> p (t n)"), start=False,
                                    stop=False, skip_group_check=True)
                ins.then_inc(s["histo_used"], 1)

            by_steps(eng, project)
            pe.matmul(bank[4][:, 0:4 * NT], zeros, zeros[:, 0:4 * NT], start=False, stop=True,
                      skip_group_check=True).then_inc(s["histo_done"], 1)

            eng.wait_ge(s["source_scores_ready"], 2)
            eng.wait_ge(s["xp_taken"], 4 + 2 * NT)
            for h in range(H):
                for g in range(G):
                    ins = pe.transpose(bank[h][:, g * P:(g + 1) * P], asT3[:, g * P:(g + 1) * P, h], ident[:, :])
                ins.then_inc(s["as_turned"], 1)
            eng.wait_ge(s["first_scan"], 1)
            for side in range(2):
                for g in range(G):
                    pe.transpose(bank[(5, 7)[side]][0:H, g * P:(g + 1) * P], tip[:, side, g, :], ident[:, :])
                    ins = pe.transpose(bank[(6, 4)[side]][0:H, g * P:(g + 1) * P], rst[:, side, g, :], ident[:, :])
            ins.then_inc(s["carry_turned"], 1)
            eng.wait_ge(s["carry_ready"], 1)
            for side in range(2):
                for g in range(G):
                    ins = pe.transpose(bank[5][:, (side * G + g) * H:(side * G + g + 1) * H],
                                       carry[0:H, side, g * P + side:g * P + side + P], ident[0:H, 0:H])
            ins.then_inc(s["seeds_turned"], 1)
            for h in range(H):
                eng.wait_ge(s["seg_ready"], h + 1)
                for g in range(G):
                    ins = pe.transpose(bank[4 + h][:, g * P:(g + 1) * P], seg[:, 0, h, g, :], ident[:, :])
                ins.then_inc(s["seg_turned"], 1)

            def carry_rows(layer):
                def visit(i, k):
                    b = k % 2
                    eng.wait_ge(s[f"scaled_a{layer}"], i * RING + k + 1)
                    eng.wait_ge(s[f"sums_taken{layer}"], i * RING + k + 1)
                    eng.wait_ge(s[f"rows_in{k}"], i * 16 + 16 * ITERS * layer + 16)
                    if layer == 0:
                        for h in range(H):
                            pe.matmul(psum[:, 2 * b + h // 2, (h % 2) * C:(h % 2 + 1) * C],
                                      hots[:, k % 4, (1 + h) * P:(2 + h) * P], row_ring[k][:, h * C:(h + 1) * C],
                                      start=(h % 2 == 0), stop=True, skip_group_check=True)
                        ins = pe.matmul(bank[4 + b][:, 0:NV], hots[:, k % 4, 0:P],
                                        vals[:, bass.ds(i * (RING * NV) + k * NV, NV)], start=True, stop=True)
                    else:
                        for c in range(2):
                            ins = pe.matmul(psum[:, 2 * b + c, :], hots[:, k % 4, P:2 * P],
                                            row_ring[k][:, c * 512:(c + 1) * 512], start=True, stop=True)
                    ins.then_inc(s[f"rows_used{layer}"], 1)

                by_visits(eng, visit)

            carry_rows(0)

            eng.wait_ge(s["bias0_in"], 16)
            eng.wait_ge(s["self_ready"], 1)

            def self_loop(j, b):
                eng.wait_ge(s["diag_ready"], j + 1)
                eng.wait_ge(s[f"x_in{b}"], turn_of(j, b) * 32 + 32)
                eng.wait_ge(s["sums_read"], j + 1)
                for c in range(2):
                    pe.matmul(psum[:, 2 * b + c, :], ones1, bias_at[0:1, c * 512:(c + 1) * 512], start=True, stop=False,
                              skip_group_check=True)
                    for h in (2 * c, 2 * c + 1):
                        ins = pe.matmul(psum[:, 2 * b + c, (h % 2) * C:(h % 2 + 1) * C], diag[b][:, h * P:(h + 1) * P],
                                        xp_in[b][:, h * C:(h + 1) * C], start=False, stop=True, skip_group_check=True)
                ins.then_inc(s["mixed"], 1)

            by_tiles(eng, self_loop)
            carry_rows(1)

            eng.wait_ge(s["W1_in"], 16)
            eng.wait_ge(s["sums_taken1"], 2 + VISITS)

            def turn_sums(j, b):
                eng.wait_ge(s["agg_ready"], j + 1)
                if not (isinstance(j, int) and j == 0):
                    eng.wait_ge(s["aggT_ready"], j)
                for k in range(KT):
                    ins = pe.transpose(psum[:, 4 + k // 4, (k % 4) * P:(k % 4 + 1) * P], agg[b][:, k * P:(k + 1) * P],
                                       ident[:, :])
                ins.then_inc(s["agg_turned"], 1)

            def product(j, b):
                eng.wait_ge(s["aggT_ready"], j + 1)
                eng.wait_ge(s["product_taken"], j + 1)
                for c in range(2):
                    for k in range(KT):
                        ins = pe.matmul(psum[:, 2 * b + c, :], aggT[b][:, k, :], Wt[:, k, c * 512:(c + 1) * 512],
                                        start=(k == 0), stop=(k == KT - 1))
                ins.then_inc(s["product_ready"], 1)

            turn_sums(0, 0)
            turn_sums(1, 1)
            ahead(eng, lambda j, b: (product(j, b), turn_sums(j + 2, b)))
            product(NT - 2, 1)
            product(NT - 1, 0)

        @block.scalar
        def _(eng):
            load_xT(eng, (1, 3))
            eng.wait_ge(s["scores_out"], 1)
            with nc.allow_non_contiguous_dma(reason="four scores per node"):
                a.dma_start(as_dram.rearrange("(j p) h -> p j h", p=P), tabv[:, :, 0:H]).then_inc(s["scores_stored"], 16)
            eng.wait_ge(s["scores_turned"], 1)
            for c in range(2):
                ins = a.copy(tabT[:, c * 512:(c + 1) * 512], bank[c][0:NT, :])
            ins.then_inc(s["chosen_ready"], 1)
            for k in range(2 * H):
                eng.wait_ge(s["visit_tab_done"], k + 1)
                a.copy(visit_tab[:, :, k], bank[k][:, 0:SPREAD]).then_inc(s["visit_tab_taken"], 1)

            def take_xp(i, b, first):
                slot = b % 2
                if not (first and b < 2):
                    eng.wait_ge(s[f"xp_stored{slot}"], (i * 3 + b // 2) * 16 if slot == 0 else (i * 2 + b // 2) * 16)
                for c in range(2):
                    eng.wait_ge(s["xp_done"], i * 10 + b * 2 + c + 1)
                    a.copy(xp_stage[slot][:, c * 512:(c + 1) * 512], bank[XP_BANKS[b % 3][c]][:, :]).then_inc(s["xp_taken"], 1)
                eng.wait_ge(s["xp_taken"], 4 + i * 10 + b * 2 + 2)
                a.dma_start(xp_dram[bass.ds(i * (5 * P) + b * P, P), :], xp_stage[slot]).then_inc(s[f"xp_stored{slot}"], 16)

            for b in range(5):
                take_xp(0, b, True)
            with eng.Fori(0, NT // 5 - 1) as i:
                for b in range(5):
                    take_xp(i + 1, b, False)
            eng.wait_ge(s["spread_taken"], 1 + NT)
            eng.wait_ge(s["histo_done"], 1)
            a.copy(sums[:, late:], zero1[:, :].broadcast_to([P, NT * D - late]))
            eng.wait_ge(s["factors_in"], 1)
            a.activation(hist_f[:, 0:2 * NT], hist_f[:, 0:2 * NT], ACT.Sqrt).then_inc(s["factors_out"], 1)
            eng.wait_ge(s["exp_in"], 1)
            a.activation(valv[:, :, 0:H], adT[:, :, 0:H], ACT.Exp).then_inc(s["exp_out"], 1)
            eng.wait_ge(s["exp_out"], 1)
            eng.wait_ge(s["scratch_used"], 1)
            a.copy(sums[:, late // 2:late], zero1[:, :].broadcast_to([P, late - late // 2])).then_inc(s["sums_zero0"], 1)

            def scale0(i, k):
                eng.wait_ge(s["hot_ready0"], i * RING + k + 1)
                for h in range(H):
                    ins = a.activation(hots[:, k % 4, (1 + h) * P:(2 + h) * P], hots[:, k % 4, 0:P], ACT.Copy,
                                       scale=vals[:, bass.ds(i * (RING * NV) + k * NV + h, 1)])
                ins.then_inc(s["scaled_a0"], 1)

            by_visits(eng, scale0)

            eng.wait_ge(s["self_in"], 1)
            a.activation(t_self, t_self, ACT.Exp, scale=-1.0).then_inc(s["self_out"], 1)
            eng.wait_ge(s["dst_sq_in"], 1)
            a.activation(mix[1][:, 0:2 * NT], mix[1][:, 0:2 * NT], ACT.Sqrt).then_inc(s["dst_sq_out"], 1)
            eng.wait_ge(s["self_ready"], 1)

            def make_diag(j, b):
                eng.wait_ge(s["mixed"], j + 1)
                for h in range(H):
                    ins = a.activation(diag[b][:, h * P:(h + 1) * P], ident[:, :], ACT.Copy,
                                       scale=c_self[:, bass.ds(j * H + h, 1)])
                ins.then_inc(s["diag_ready"], 1)

            def deviate(layer):
                def one(j, b):
                    eng.wait_ge(s[f"variance{layer}"], j + 1)
                    a.activation(spread[b][:, 1:2], spread[b][:, 0:1], ACT.Sqrt).then_inc(s[f"deviation{layer}"], 1)
                return one

            make_diag(0, 0)
            with eng.Fori(0, NT // 2) as i:
                make_diag(i * 2 + 1, 1)
                deviate(0)(i * 2, 0)
                make_diag(i * 2 + 2, 0)
                deviate(0)(i * 2 + 1, 1)
            deviate(0)(NT - 1, 0)

            def scale1(i, k):
                eng.wait_ge(s["hot_ready1"], i * RING + k + 1)
                eng.wait_ge(s[f"rows_in{k}"], i * 16 + 16 * ITERS + 16)
                ins = a.activation(hots[:, k % 4, P:2 * P], hots[:, k % 4, 0:P], ACT.Copy, scale=row_ring[k][:, D:D + 1])
                ins.then_inc(s["scaled_a1"], 1)

            by_visits(eng, scale1)

            def scale_sums(j, b):
                if not (isinstance(j, int) and j < 2):
                    eng.wait_ge(s["agg_turned"], j - 1)
                a.activation(agg[b], sums[:, bass.ds(j * D, D)], ACT.Copy, scale=fdst[:, bass.ds(j + 0, 1)]) \
                    .then_inc(s["agg_ready"], 1)

            def take_turned(j, b):
                eng.wait_ge(s["agg_turned"], j + 1)
                if not (isinstance(j, int) and j < 2):
                    eng.wait_ge(s["product_ready"], j - 1)
                a.copy(aggT[b].rearrange("p k n -> p (k n)"), psum[:, 4:6, :].rearrange("p c n -> p (c n)")) \
                    .then_inc(s["aggT_ready"], 1)

            eng.wait_ge(s["sums_taken1"], 2 + VISITS)
            for j in range(2):
                scale_sums(j, j)
                take_turned(j, j)
            ahead(eng, lambda j, b: (scale_sums(j + 2, b), take_turned(j + 2, b), deviate(1)(j, b)))
            deviate(1)(NT - 2, 1)
            deviate(1)(NT - 1, 0)

        @block.vector
        def _(eng):
            order = Tally(s["vector_order"])

            def then(ins):
                order.inc(ins)
                eng.wait_ge(order.sem, order.value())

            eng.sem_inc(s["xT_scored"], 5)
            eng.sem_inc(s["hotT_ready"], 2)
            eng.sem_inc(s["spread_taken"], 1)
            eng.sem_inc(s["xp_taken"], 4)
            eng.sem_inc(s["histo_used"], 2)
            for layer in range(2):
                eng.sem_inc(s[f"rows_used{layer}"], RING)
                eng.sem_inc(s[f"sums_taken{layer}"], 2)
            for name in ("x_free", "mixed", "sums_read", "product_taken", "x1_free"):
                eng.sem_inc(s[name], 2)
            v.memset(zero1[:, :], 0.0)
            eng.wait_ge(s["consts"], 2)
            v.tensor_copy(iota_f[:, :], iota_i[:, 0:EB])
            v.tensor_copy(iota_w, iota_i)
            v.tensor_copy(iota_b, iota_i[:, 0:P])
            v.memset(ones_row, 1.0)
            v.memset(vals[:, :], 0.0)
            v.memset(nodesum[:, :], 0.0)
            v.memset(asT, 0.0)
            v.memset(shift, -7.0)
            v.memset(zeros, 0.0)
            then(v.tensor_copy(visit_no[:, :], visit_i))
            then(v.tensor_scalar(ident[:, :], iota_f[:, 0:P], visit_no[:, 0:1], None, ALU.is_equal))
            v.memset(valv[:, :, NV - 1], 1.0)

            eng.wait_ge(s["ends_in"], 32)
            then(v.tensor_single_scalar(ends_t[0:1, :], ends_i[0:1, :], 7, ALU.arith_shift_right))
            then(v.tensor_copy(ends_f[0:1, :], ends_t[0:1, :]))
            then(v.scalar_tensor_tensor(span[0:1, :], ends_f[0:1, NB:2 * NB], 1.0, ends_f[0:1, 0:NB], ALU.add, ALU.subtract))
            then(v.tensor_tensor_scan(endk[0:1, 0:NB], ones_row[0:1, 0:NB], span[0:1, :], 0.0, ALU.mult, ALU.add))
            then(v.tensor_tensor(tmp_row[0:1, :], endk[0:1, 0:NB], span[0:1, :], ALU.subtract))
            v.tensor_tensor(endk[0:1, NB:2 * NB], tmp_row[0:1, :], ends_f[0:1, 0:NB], ALU.subtract) \
                .then_inc(s["block_ends_ready"], 1)
            eng.wait_ge(s["block_ends_spread"], 1)
            for g in range(G):
                then(v.tensor_scalar(dump[:, 0:NB], bank[5][:, 0:NB], visit_no[:, g:g + 1], None, ALU.is_le, ALU.add,
                                     accum_out=tcount[:, g:g + 1]))
                then(v.tensor_scalar(mask, iota_w, tcount[:, g:g + 1], None, ALU.is_equal))
                then(v.tensor_tensor_reduce(dump[:, 0:NB], mask, bank[6][:, 0:NB], 1.0, 0.0, ALU.mult, ALU.add,
                                            ksel[:, g:g + 1]))
            v.tensor_copy(block_i, tcount).then_inc(s["blocks_known"], 1)
            then(v.scalar_tensor_tensor(jv2, ksel, -1.0, visit_no[:, :], ALU.mult, ALU.add))
            v.tensor_scalar(jv, jv2, float(NT - 1), None, ALU.min).then_inc(s["tiles_ready"], 1)
            eng.wait_ge(s["tiles_ready"], 1)
            then(v.tensor_scalar(j128, jv, float(P), None, ALU.mult))
            eng.wait_ge(s["tiles_turned"], 1)
            v.memset(ones_tiles, 1.0)
            v.tensor_copy(tile_row, bank[2][0:1, 0:VPAD])
            v.tensor_copy(tile_of[:, :], bank[2][0:1, 0:VPAD]).then_inc(s["tile_row_ready"], 1)

            eng.wait_ge(s["W0_in"], 16)
            eng.wait_ge(s["att_in"], 32)
            for k in range(KT):
                for h in range(2 * H):
                    if k * 2 * H + h >= 4:
                        eng.wait_ge(s["wa_ready"], k * 2 * H + h - 3)
                    ins = v.tensor_tensor_reduce(dump[:, (h % 4) * C:(h % 4 + 1) * C], Wt[:, k, (h % H) * C:(h % H + 1) * C], att[:, h, :], 1.0, 0.0,
                                                 ALU.mult, ALU.add, wa[:, k, h:h + 1]).then_inc(s["wa_ready"], 1)

            eng.wait_ge(s["blocks_in"], 16 * 3 * G)
            v.tensor_copy(src_f, src_i)
            then(v.tensor_copy(dst_f, dst_i))
            v.tensor_copy(ends2, dst_f[:, :, 0:EB:EB - 1]).then_inc(s["block_tips"], 1)
            for g in range(G):
                ins = v.tensor_scalar(rel_f[:, g, :], dst_f[:, g, :], j128[:, g:g + 1], None, ALU.subtract)
            then(ins)
            v.tensor_scalar(rel_c, rel_f, -1.0, float(P), ALU.max, ALU.min).then_inc(s["rel_clamped"], 1)
            v.tensor_tensor(brk[:, 0, :, 1:EB], dst_f[:, :, 1:EB], dst_f[:, :, 0:EB - 1], ALU.not_equal)
            v.tensor_tensor(brk[:, 1, :, 0:EB - 1], dst_f[:, :, 1:EB], dst_f[:, :, 0:EB - 1], ALU.not_equal)
            eng.wait_ge(s["block_tips_turned"], 1)
            v.tensor_copy(shift[0:2, 1:VPAD + 1], bank[7][0:2, 0:VPAD]).then_inc(s["tips_shifted"], 1)
            eng.wait_ge(s["tips_back"], 1)
            then(v.tensor_copy(near, bank[4][:, 0:4 * G].rearrange("p (a g k) -> p a g k", a=2, g=G)))
            v.tensor_tensor(brk[:, 0, :, 0:1], dst_f[:, :, 0:1], near[:, 0, :, 1:2], ALU.not_equal)
            then(v.tensor_tensor(brk[:, 1, :, EB - 1:EB], dst_f[:, :, EB - 1:EB], near[:, 1, :, 0:1], ALU.not_equal))
            eng.sem_inc(s["edge_turned"], 1)
            eng.wait_ge(s["edge_taken"], 4)
            pen = brk

            then(v.tensor_copy(srcT[:, :], bank[0]))
            eng.sem_inc(s["src_index_ready"], 1)
            v.tensor_copy(relT[:, :], bank[1])
            v.tensor_copy(valv[:, :, 2 * H], bank[3][:, 0:SPREAD])
            then(v.tensor_copy(lastT, bank[6]))
            brk_flat = brk.rearrange("p a g e -> p (a g e)")
            eng.sem_inc(s["last_taken"], 1)

            sent = [v.tensor_single_scalar(w_i, srcT[:, :], n, op) for w_i, n, op in
                    ((lo_i, P - 1, ALU.bitwise_and), (hi_i, 7, ALU.arith_shift_right))]
            then(sent[-1])
            v.tensor_copy(lo_f, lo_i)
            v.tensor_copy(hi_f, hi_i)
            then(v.tensor_scalar(wok, relT[:, :], 0.0, None, ALU.is_ge))
            then(v.scalar_tensor_tensor(okT, relT[:, :], float(P - 1), wok, ALU.is_le, ALU.mult))
            then(v.tensor_tensor(wok[:, 0:SPREAD], okT[:, 0:SPREAD], valv[:, :, 2 * H], ALU.mult))
            then(v.tensor_copy(w_part[:, 0, :], wok))
            then(v.tensor_tensor(wok, wok, w_part[:, 0, :], ALU.subtract))
            then(v.tensor_copy(w_part[:, 1, :], wok))
            then(v.tensor_tensor(wok, wok, w_part[:, 1, :], ALU.subtract))
            v.tensor_copy(w_part[:, 2, :], wok).then_inc(s["histo_flags"], 1)
            eng.wait_ge(s["histo_flags"], 1)

            eng.wait_ge(s["tile_row_spread"], 1)
            v.tensor_scalar(chosen, bank[2][0:NT, 0:VPAD], visit_no[0:NT, 0:1], None, ALU.is_equal) \
                .then_inc(s["chosen_ready"], 1)
            eng.wait_ge(s["xT_scored"], 5 + NT)
            then(v.tensor_copy(tab[:, :], bank[5][:, 0:NT * 2 * H]))
            eng.sem_inc(s["scores_out"], 1)
            eng.wait_ge(s["visit_tab_taken"], 2 * H)
            for part in range(3):
                then(v.tensor_copy(near_tab4[:, :, part, :], visit_tab))
                if part < 2:
                    then(v.tensor_tensor(visit_tab, visit_tab, near_tab4[:, :, part, :], ALU.subtract))
            v.memset(carry, -BIG)
            v.memset(rst_h[0:H], 0.0)

            def spread_step(i, b):
                u0, slot = i * (5 * STEP) + b * STEP, b % 2
                eng.wait_ge(s[f"rel_bc{b}"], i * 16 + 16)
                eng.wait_ge(s["spread_taken"], i * 5 + b + 1)
                v.tensor_scalar(hotT[slot], rel_bc[slot], visit_no[:, 0:1], None, ALU.is_equal).then_inc(s["hotT_ready"], 1)
                eng.wait_ge(s["histo_used"], i * 5 + b + (2 if b == 0 else 1))
                for u in range(STEP):
                    v.tensor_scalar(lo_hot[slot][:, u * P:(u + 1) * P], iota_b, lo_f[:, bass.ds(u0 + u, 1)], None,
                                    ALU.is_equal)
                hi = hi_f[:, bass.ds(u0, STEP)].unsqueeze(2).broadcast_to([P, STEP, NT])
                then(v.tensor_tensor(hi_hot[slot][:, :, 0, :], iota_f[:, 0:NT].unsqueeze(1).broadcast_to([P, STEP, NT]), hi,
                                     ALU.is_equal))
                for part in range(3):
                    v.tensor_tensor(hi_hot[slot][:, :, 1 + part, :], hi_hot[slot][:, :, 0, :],
                                    w_part[:, part, bass.ds(u0, STEP)].unsqueeze(2).broadcast_to([P, STEP, NT]), ALU.mult)
                then(v.tensor_tensor(hi_hot[slot][:, :, 0, :], hi_hot[slot][:, :, 0, :],
                                     okT[:, bass.ds(u0, STEP)].unsqueeze(2).broadcast_to([P, STEP, NT]), ALU.mult))
                eng.sem_inc(s["histo_ready"], 1)
                eng.wait_ge(s["spread_done"], i * 5 + b + 1)
                v.tensor_reduce(ad_flat[:, bass.ds(u0 * (2 * H), STEP * 2 * H)].rearrange("p (u k) -> p u k", u=STEP),
                                bank[7][:, 0:STEP * 24].rearrange("p (u t k) -> p u k t", u=STEP, t=3), AX.X, ALU.add) \
                    .then_inc(s["spread_taken"], 1)

            with eng.Fori(0, NT // 5) as i:
                order.enter(i, 10)
                for b in range(5):
                    spread_step(i, b)
                order.leave(NT // 5)
            eng.wait_ge(s["spread_taken"], 1 + NT)
            then(v.tensor_scalar(brk_flat, brk_flat, -BIG, None, ALU.mult))
            for side in range(2):
                for h in range(H):
                    v.tensor_reduce(rst[:, side, :, h], pen[:, side], AX.X, ALU.min)
            eng.wait_ge(s["histo_done"], 1)
            then(v.tensor_scalar(hist_f[:, 0:NT], bank[4][:, 0:NT], 1.0, None, ALU.max))
            then(v.tensor_scalar(hist_f[:, 2 * NT:3 * NT], bank[4][:, 0:NT], 0.0, None, ALU.is_equal))
            then(v.tensor_copy(hist_f[:, 3 * NT:4 * NT], bank[4][:, NT:2 * NT]))
            for part in (2, 3):
                then(v.tensor_tensor(hist_f[:, 3 * NT:4 * NT], hist_f[:, 3 * NT:4 * NT], bank[4][:, part * NT:(part + 1) * NT],
                                     ALU.add))
            then(v.tensor_tensor(hist_f[:, NT:2 * NT], hist_f[:, 3 * NT:4 * NT], hist_f[:, 2 * NT:3 * NT], ALU.add))
            eng.sem_inc(s["factors_in"], 1)
            eng.wait_ge(s["factors_out"], 1)
            then(v.tensor_tensor(hist_f[:, 2 * NT:3 * NT], hist_f[:, 0:NT], hist_f[:, NT:2 * NT], ALU.mult))
            then(v.reciprocal(fsrc[:, :], hist_f[:, 2 * NT:3 * NT]))

            eng.wait_ge(s["as_turned"], H)

            def scan(side, h, g, first):
                o, p_, d_ = seg[:, side, h, g, :], pen[:, side, g, :], bank[h][:, g * EB:(g + 1) * EB]
                if side:
                    o, p_, d_ = o[:, ::-1], p_[:, ::-1], d_[:, ::-1]
                return v.tensor_tensor_scan(o, p_, d_, -BIG if first else seed[:, side, g, h:h + 1], ALU.add, ALU.max)

            for side in range(2):
                for h in range(H):
                    for g in range(G):
                        ins = scan(side, h, g, True)
            then(ins)
            for side in range(2):
                ins = v.tensor_copy(tip[:, side], seg[:, side, :, :, EB - 1 if side == 0 else 0].rearrange("p h g -> p g h"))
            ins.then_inc(s["first_scan"], 1)
            eng.wait_ge(s["carry_turned"], 1)
            for side in range(2):
                ins = v.tensor_copy(rst_h[0:H, side, :], bank[(6, 4)[side]][0:H, :])
            then(ins)
            v.tensor_tensor_scan(carry[0:H, 0, 1:VPAD + 1], rst_h[0:H, 0, :], bank[5][0:H, :], -BIG, ALU.add, ALU.max)
            then(v.tensor_tensor_scan(carry[0:H, 1, 0:VPAD][:, ::-1], rst_h[0:H, 1, ::-1],
                                      bank[7][0:H, ::-1], -BIG, ALU.add, ALU.max))
            eng.sem_inc(s["carry_ready"], 1)
            eng.wait_ge(s["seeds_turned"], 1)
            then(v.tensor_copy(seed, bank[5][:, 0:2 * G * H].rearrange("p (a g h) -> p a g h", a=2, g=G)))
            for h in range(H):
                for side in range(2):
                    for g in range(G):
                        ins = scan(side, h, g, False)
                then(ins)
                v.tensor_tensor(seg[:, 0, h], seg[:, 0, h], seg[:, 1, h], ALU.max).then_inc(s["seg_ready"], 1)
            eng.wait_ge(s["seg_ready"], H)
            mm = seg_flat[:, H * G * EB:H * G * EB + SPREAD * H].rearrange("p (u h) -> p u h", h=H)
            for h in range(H):
                eng.wait_ge(s["seg_turned"], h + 1)
                ins = v.tensor_copy(mm[:, :, h], bank[4 + h][:, 0:SPREAD])
            then(ins)
            then(v.tensor_tensor(mm, mm, adT[:, :, 0:H], ALU.max))
            then(v.tensor_tensor(mm, mm, adT[:, :, H:2 * H], ALU.add))
            then(v.scalar_tensor_tensor(mm, mm, SLOPE, mm, ALU.mult, ALU.max))
            then(v.tensor_tensor(adT[:, :, 0:H], asT3[:, 0:SPREAD, :], adT[:, :, H:2 * H], ALU.add))
            then(v.scalar_tensor_tensor(adT[:, :, 0:H], adT[:, :, 0:H], SLOPE, adT[:, :, 0:H], ALU.mult, ALU.max))
            v.tensor_tensor(adT[:, :, 0:H], adT[:, :, 0:H], mm, ALU.subtract).then_inc(s["exp_in"], 1)
            for h in range(H):
                ins = v.tensor_tensor(valv[:, :, H + h], mm[:, :, h], last[:, 0:SPREAD], ALU.mult)
            then(ins)
            eng.wait_ge(s["exp_out"], 1)
            eng.sem_inc(s["scratch_used"], 1)
            then(v.memset(sums[:, 0:late // 2], 0.0))
            eng.wait_ge(s["sums_zero0"], 1)

            def build(layer, i, k):
                eng.wait_ge(s[f"rows_used{layer}"], i * RING + k + RING - 3)
                u = i * RING + k
                if layer == 0:
                    ins = v.tensor_scalar(hots[:, k % 4, 0:P], iota_f[:, :], relT[:, bass.ds(u, 1)], None, ALU.is_equal)
                else:
                    ins = v.tensor_scalar(hots[:, k % 4, 0:P], iota_f[:, :], relT[:, bass.ds(u, 1)],
                                          vals[:, bass.ds(u * NV + 2 * H, 1)], ALU.is_equal, ALU.mult)
                ins.then_inc(s[f"hot_ready{layer}"], 1)

            def take_sums(layer, i, k):
                n = i * RING + k
                j = eng.value_load(tile_of[0:1, bass.ds(n, 1)], min_val=0, max_val=NT - 1)
                eng.wait_ge(s[f"rows_used{layer}"], n + RING + 1)
                eng.wait_ge(s[f"sums_taken{layer}"], n + 2)
                to = sums[:, bass.ds(j * D, D)]
                ins = v.tensor_tensor(to, to, pair(k % 2).rearrange("p c n -> p (c n)"), ALU.add)
                if layer == 0:
                    to = nodesum[:, bass.ds(j * NV, NV)]
                    ins = v.tensor_tensor(to, to, bank[4 + k % 2][:, 0:NV], ALU.add)
                ins.then_inc(s[f"sums_taken{layer}"], 1)

            def edge_loop(layer):
                for k in range(AHEAD):
                    build(layer, 0, k)
                with eng.Fori(0, ITERS) as i:
                    for k in range(RING):
                        build(layer, i, k + AHEAD)
                        take_sums(layer, i, k)
                eng.wait_ge(s[f"sums_taken{layer}"], 2 + VISITS)

            edge_loop(0)

            tv = t_self.rearrange("p (j h) -> p j h", h=H)
            cv = c_self[:, 0:NT * H].rearrange("p (j h) -> p j h", h=H)
            rv = r_self.rearrange("p (j h) -> p j h", h=H)
            v.memset(c_self[:, NT * H:], 0.0)
            v.memset(ones1, 1.0)
            then(v.tensor_tensor(tv, tabv[:, :, 0:H], tabv[:, :, H:2 * H], ALU.add))
            then(v.scalar_tensor_tensor(t_self, t_self, SLOPE, t_self, ALU.mult, ALU.max))
            then(v.tensor_tensor(tv, nodev[:, :, H:2 * H], tv, ALU.subtract))
            then(v.tensor_scalar(fdst[:, :], nodev[:, :, NV - 1], 0.0, None, ALU.is_gt))
            for h in range(H):
                ins = v.tensor_tensor(tv[:, :, h], tv[:, :, h], fdst[:, :], ALU.mult)
            ins.then_inc(s["self_in"], 1)
            sq = mix[1][:, 0:2 * NT]
            eng.wait_ge(s["self_in"], 1)
            then(v.tensor_scalar(fdst[:, :], nodev[:, :, NV - 1], 0.0, None, ALU.is_equal))
            v.tensor_scalar(sq[:, 0:NT], nodev[:, :, NV - 1], 1.0, None, ALU.max)
            v.tensor_tensor(sq[:, NT:2 * NT], nodev[:, :, 2 * H], fdst[:, :], ALU.add).then_inc(s["dst_sq_in"], 1)
            eng.wait_ge(s["self_out"], 1)
            then(v.tensor_tensor(rv, nodev[:, :, 0:H], tv, ALU.add))
            then(v.reciprocal(r_self, r_self))
            then(v.tensor_tensor(cv, tv, rv, ALU.mult))
            eng.wait_ge(s["dst_sq_out"], 1)
            then(v.tensor_tensor(sq[:, 0:NT], sq[:, 0:NT], sq[:, NT:2 * NT], ALU.mult))
            then(v.reciprocal(fdst[:, :], sq[:, 0:NT]))
            eng.sem_inc(s["self_ready"], 1)

            def normalize(layer, j, b, to):
                for c in range(2):
                    ins = v.bn_stats(stats[b][:, c * 6:(c + 1) * 6], mix[b][:, c * 512:(c + 1) * 512])
                then(ins)
                eng.sem_inc(s["vector_passed"], 1)
                then(v.bn_aggr(moments[b], stats[b]))
                v.tensor_scalar(spread[b][:, 0:1], moments[b][:, 1:2], EPS, None, ALU.add).then_inc(s[f"variance{layer}"], 1)
                eng.wait_ge(s[f"deviation{layer}"], j + 1)
                then(v.reciprocal(spread[b][:, 0:1], spread[b][:, 1:2]))
                return v.tensor_scalar(to, mix[b], moments[b][:, 0:1], spread[b][:, 0:1], ALU.subtract, ALU.mult)

            def finish0(j, b, first=False):
                eng.wait_ge(s["mixed"], j + 3)
                for h in range(H):
                    ins = v.scalar_tensor_tensor(mix[b][:, h * C:(h + 1) * C], sums[:, bass.ds(j * D + h * C, C)],
                                                 r_self[:, bass.ds(j * H + h, 1)],
                                                 psum[:, 2 * b + h // 2, (h % 2) * C:(h % 2 + 1) * C], ALU.mult, ALU.add)
                ins.then_inc(s["sums_read"], 1)
                eng.wait_ge(s["sums_read"], j + 3)
                then(v.scalar_tensor_tensor(mix[b], mix[b], 0.0, x_in[b], ALU.max, ALU.add))
                if not first:
                    eng.wait_ge(s[f"x1_stored{b}"], turn_of(j, b) * 16)
                v.tensor_copy(x1_out[b][:, D:D + 1], fsrc[:, bass.ds(j + 0, 1)])
                normalize(0, j, b, x1_out[b][:, 0:D]).then_inc(s["x1_ready"], 1)
                eng.wait_ge(s["x1_ready"], j + 1)
                eng.sem_inc(s["x_free"], 1)

            def tiles_with_first(finish, per):
                finish(0, 0, True)
                finish(1, 1, True)
                with eng.Fori(1, NT // 2) as i:
                    order.enter(i - 1, 2 * per)
                    finish(Tile(i, 0), 0)
                    finish(Tile(i, 1), 1)
                    order.leave(NT // 2 - 1)
                finish(NT - 1, 0)

            for b in range(2):
                v.memset(x1_out[b][:, D:], 0.0)
            tiles_with_first(finish0, 4)
            edge_loop(1)

            def finish1(j, b, first=False):
                eng.wait_ge(s["product_ready"], j + 1)
                if not first:
                    eng.wait_ge(s[f"out_stored{b}"], turn_of(j, b) * 16)
                v.tensor_tensor(mix[b], pair(b).rearrange("p c n -> p (c n)"), bias_at, ALU.add) \
                    .then_inc(s["product_taken"], 1)
                eng.wait_ge(s["product_taken"], j + 3)
                eng.wait_ge(s[f"x1_in{b}"], turn_of(j, b) * 16 + 16)
                then(v.scalar_tensor_tensor(mix[b], mix[b], 0.0, x1_in[b], ALU.max, ALU.add))
                eng.sem_inc(s["x1_free"], 1)
                normalize(1, j, b, mix[b]).then_inc(s["out_ready"], 1)

            eng.wait_ge(s["bias1_in"], 16)
            tiles_with_first(finish1, 4)


def kernel(x, src, dst, edge_weight, L0_gnn_W, L0_gnn_att_src, L0_gnn_att_dst, L0_gnn_bias, L1_gnn_W, L1_gnn_b):
    import numpy as np
    import concourse.bacc as bacc
    from concourse.bass_utils import run_bass_kernel_spmd

    x = np.asarray(x)
    xpad = np.zeros((NP, D), x.dtype)
    xpad[:N] = x

    def blocks(v, fill):
        v = np.asarray(v)
        b = np.full(((NB + 1) * EB,), fill, v.dtype)
        b[:E] = v
        return b.reshape(NB + 1, EB)

    arrays = {
        "xT": np.ascontiguousarray(xpad.reshape(NT, P, KT, P).transpose(0, 3, 2, 1)).reshape(NT * P, D), "x": xpad,
        "src_blocks": blocks(src, NP - 1), "dst_blocks": blocks(dst, NP - 1), "w_blocks": blocks(edge_weight, 1),
        "W0": np.asarray(L0_gnn_W), "att_src": np.asarray(L0_gnn_att_src), "att_dst": np.asarray(L0_gnn_att_dst),
        "bias0": np.asarray(L0_gnn_bias), "W1": np.asarray(L1_gnn_W), "bias1": np.asarray(L1_gnn_b),
    }
    nc = bacc.Bacc("TRN2", target_bir_lowering=False, num_devices=1)
    args = {n: nc.dram_tensor(n, v.shape, mybir.dt.from_np(v.dtype), kind="ExternalInput").ap() for n, v in arrays.items()}
    out = nc.dram_tensor("out", (N, D), F32, kind="ExternalOutput").ap()
    gnn_kernel(nc, **args, out=out)
    r = run_bass_kernel_spmd(nc, [arrays], core_ids=[0])
    return r.results[0]["out"]
```

```python
from contextlib import ExitStack

import concourse.bass as bass
from concourse import mybir

P = 128
N = 3125
NT = -(-N // P)
NP = NT * P
D = 1024
KT = D // P
H = 4
C = D // H
E = 50000
EB = P
NB = -(-E // EB)
RING = 8
ITERS = -(-(NB + NT - 1) // RING)
VISITS = ITERS * RING
G = -(-VISITS // P)
VPAD = G * P
STEP = -(-VISITS // NT)
SPREAD = NT * STEP
AHEAD = 2
ROW1 = D + 4
NV = 10
BIG = float(2.0 ** 100)
SLOPE = 0.2
EPS = 1e-5
WHOLE = KT
XP_BANKS = ((0, 1), (2, 3), (5, 6))
assert ITERS % 2 == 0 and SPREAD <= VPAD and VISITS + RING <= SPREAD and NT % 5 == 0

ALU = mybir.AluOpType
ACT = mybir.ActivationFunctionType
AX = mybir.AxisListType
F32 = mybir.dt.float32
F32R = mybir.dt.float32r
BF16 = mybir.dt.bfloat16
I32 = mybir.dt.int32


class Tally:

    def __init__(self, sem):
        self.sem, self.n, self.off, self.start = sem, 0, 0, 0

    def inc(self, ins):
        ins.then_inc(self.sem, 1)
        self.n += 1

    def value(self):
        return self.off + self.n

    def enter(self, i, per):
        self.off, self.start, self.per = i * per, self.n, per

    def leave(self, count):
        assert self.n - self.start == self.per, (self.n - self.start, self.per)
        self.off, self.n = 0, self.start + count * self.per


class Tile:

    def __init__(self, turn, slot):
        self.turn, self.at = turn, turn * 2 + slot

    def __add__(self, n):
        return self.at + n

    def __sub__(self, n):
        return self.at - n

    def __mul__(self, n):
        return self.at * n


def gnn_kernel(nc, xT, x, src_blocks, dst_blocks, w_blocks, W0, att_src, att_dst, bias0, W1, bias1, out):
    ctx = ExitStack()
    with ctx:
        def sb(name, shape, dt=F32):
            return ctx.enter_context(nc.sbuf_tensor(name, shape, dt))

        xp_dram = nc.dram_tensor("xp_rows", [NP, D], F32, kind="Internal").ap()
        as_dram = nc.dram_tensor("source_scores", [NP, H], F32, kind="Internal").ap()
        rel_dram = nc.dram_tensor("relative_dst", [VPAD, EB], BF16, kind="Internal").ap()
        x1_dram = nc.dram_tensor("x1_rows", [NP, ROW1], F32, kind="Internal").ap()

        psum = ctx.enter_context(nc.psum_tensor("psum", [P, 8, 512], F32))
        bank = [psum[:, i, :] for i in range(8)]
        psum_flat = psum[:, :, :].rearrange("p b n -> p (b n)")

        def pair(b):
            return psum[:, 2 * b:2 * b + 2, :]

        shapes = (("sums", [P, NT * D]), ("Wt", [P, KT * D]), ("rows", [P, RING * ROW1]), ("vals", [P, SPREAD * NV]),
                  ("relT", [P, VPAD]), ("srcT", [P, VPAD]), ("hots", [P, 4 * (1 + H) * P]))
        with ExitStack() as first_names:
            sums, Wt, rows, vals, relT, srcT, hots = (first_names.enter_context(nc.sbuf_tensor(n, shape, F32))
                                                      for n, shape in shapes)
        sums_r, Wt_r, rows_r, vals_r, relT_r, srcT_r, hots_r = (sb(n + "_parts", shape, F32R) for n, shape in shapes)
        Wt = Wt[:, :].rearrange("p (k n) -> p k n", k=KT)
        Wt_r = Wt_r[:, :].rearrange("p (k n) -> p k n", k=KT)
        srcT = srcT[:, :].bitcast(I32)
        hots = hots[:, :].rearrange("p (q n) -> p q n", q=4)
        iota_f = sb("iota_f", [P, EB])
        ident = sb("ident", [P, P])
        visit_no = sb("visit_no", [P, G])
        tab = sb("tab", [P, NT * 2 * H])
        nodesum = sb("nodesum", [P, NT * 3 * NV])
        tile_of = sb("tile_of", [1, VPAD], I32)
        fsrc = sb("fsrc", [P, NT])
        idx = sb("idx", [P, 2 * RING], I32)
        fdst = sb("fdst", [P, NT])
        zero1 = sb("zero1", [P, 1])

        valv = vals[:, :].rearrange("p (u k) -> p u k", k=NV)
        node_parts = nodesum[:, :].rearrange("p (j t k) -> p j t k", t=3, k=NV)
        nodev = node_parts[:, :, 0, :]
        tabv = tab[:, :].rearrange("p (j k) -> p j k", k=2 * H)

        def cut(tensor, at, n):
            return tensor[:, at:at + n]

        xT_flat = [cut(rows, b * D, D) for b in range(5)]
        xT_ring = [f.rearrange("p (k n) -> p k n", k=KT) for f in xT_flat]
        xp_stage = [cut(rows, (5 + b) * D, D) for b in range(2)]

        row_ring = [cut(rows, q * ROW1, ROW1) for q in range(RING)]
        x_in = [cut(rows, b * D, D) for b in range(2)]
        xp_in = [cut(rows, (2 + b) * D, D) for b in range(2)]
        mix = [cut(rows, (4 + b) * D, D) for b in range(2)]
        x1_out = [cut(rows, 6 * D + b * ROW1, ROW1) for b in range(2)]
        agg = [cut(rows, b * D, D) for b in range(2)]
        aggT = [cut(rows, (2 + b) * D, D).rearrange("p (k n) -> p k n", k=KT) for b in range(2)]
        x1_in = [cut(rows, (6 + b) * D, D) for b in range(2)]
        aggT_high = [rows_r[:, (2 + b) * D:(3 + b) * D].rearrange("p (k n) -> p k n", k=KT) for b in range(2)]
        W_high = [cut(sums_r, k * D, D) for k in range(KT)]

        W_flat = Wt[:, :, :].rearrange("p k n -> p (k n)")
        parts_cols = SPREAD * 3 * NV // 2
        val_parts = W_flat[:, 0:parts_cols].bitcast(BF16)
        val_parts4 = val_parts.rearrange("p (u t k) -> p u t k", t=3, k=NV)
        bias_split = W_flat[0:1, 0:3 * D // 2].bitcast(BF16)
        bias_parts = W_flat[0:3, parts_cols:parts_cols + D // 2].bitcast(BF16)
        bias_row = W_flat[0:1, parts_cols + D // 2:parts_cols + D // 2 + D]
        left = W_flat[:, parts_cols + D // 2 + D:]
        val_rest = left[:, 0:RING * NV].rearrange("p (u k) -> p u k", k=NV)
        ones3 = left[0:3, RING * NV:RING * NV + P // 2].bitcast(BF16)

        hot_of = [hots[:, q, 0:P // 2].bitcast(BF16) for q in range(4)]
        hots_flat = hots[:, :, :].rearrange("p q c -> p (q c)")
        bias_at = hots_flat[:, 0:D]
        diag = [hots_flat[:, D + b * H * P:D + (b + 1) * H * P] for b in range(2)]
        spare = hots_flat[:, 2 * D:]
        r_self = spare[:, 0:NT * H]
        c_self = spare[:, 104:104 + NT * H]
        t_self = spare[:, 208:208 + NT * H]
        stats = [spare[:, 312 + b * 20:312 + b * 20 + 12] for b in range(2)]
        moments = [spare[:, 312 + b * 20 + 12:312 + b * 20 + 14] for b in range(2)]
        spread = [spare[:, 312 + b * 20 + 14:312 + b * 20 + 16] for b in range(2)]
        shifted = [spare[:, 480 + b:481 + b] for b in range(2)]

        place = [0]

        def take(n):
            at = place[0]
            place[0] += n
            assert place[0] <= NT * D
            return cut(sums, at, n)

        def take3(a, b):
            return take(a * b).rearrange("p (a b) -> p a b", a=a)

        ad_flat = take(SPREAD * 2 * H)
        adT = ad_flat.rearrange("p (u k) -> p u k", k=2 * H)
        att = ad_flat[:, 0:2 * H * C].rearrange("p (h c) -> p h c", c=C)
        dump = ad_flat[:, 2 * H * C:2 * H * C + 4 * C]
        brk = take(2 * G * EB).rearrange("p (a g e) -> p a g e", a=2, g=G)
        last = take(VPAD)
        asT = take(2 * RING * H + VPAD * H)
        seg = take(2 * H * G * EB).rearrange("p (a h g e) -> p a h g e", a=2, h=H, g=G)
        tip = take(2 * G * H).rearrange("p (a g h) -> p a g h", a=2, g=G)
        rst = take(2 * G * H).rearrange("p (a g h) -> p a g h", a=2, g=G)
        rst_flat, carry_flat = take(2 * VPAD), take(2 * (VPAD + 1))
        rst_h = rst_flat.rearrange("p (a u) -> p a u", a=2)
        carry = carry_flat.rearrange("p (a u) -> p a u", a=2)
        seed = take(2 * G * H).rearrange("p (a g h) -> p a g h", a=2, g=G)
        stage = [take(RING * H) for _ in range(2)]
        hist_f = take(4 * NT)
        late = place[0]
        wa = take3(KT, 2 * H)
        rows_of_nb = take(3 * NB)
        iota_i = rows_of_nb[:, 0:NB].bitcast(I32)
        iota_w, tmp_row = (rows_of_nb[:, n * NB:(n + 1) * NB] for n in (1, 2))
        visit_i = take(G).bitcast(I32)
        iota_b = take(P // 2).bitcast(BF16)
        tcount = take(G)
        mask = take(NB)
        ksel = take(G)
        jv = take(G)
        jv2 = take(G)
        j128 = take(G)
        block_i = take(G).bitcast(I32)
        dst_flat, src_flat, w_flat, rel_flat = (take(G * EB) for _ in range(4))
        dst_i, src_i = (f.rearrange("p (g e) -> p g e", g=G).bitcast(I32) for f in (dst_flat, src_flat))
        w_f = w_flat.rearrange("p (g e) -> p g e", g=G)
        rel_f = rel_flat.rearrange("p (g e) -> p g e", g=G)
        parts_of_dst = take(5 * G * EB // 2)
        dst_f, src_f = (parts_of_dst[:, n * G * EB:(n + 1) * G * EB].rearrange("p (g e) -> p g e", g=G) for n in range(2))
        rel_c = parts_of_dst[:, 2 * G * EB:].bitcast(BF16).rearrange("p (g e) -> p g e", g=G)
        ends2 = take3(G, 2)
        shift = take(VPAD + 2)
        near = take(4 * G).rearrange("p (a g k) -> p a g k", a=2, g=G)
        lo_i = dst_f.rearrange("p g e -> p (g e)").bitcast(I32)
        hi_i = src_f.rearrange("p g e -> p (g e)").bitcast(I32)
        lo_f, hi_f, okT, wok = dst_flat, src_flat, w_flat, rel_flat
        w_part = take(3 * VPAD // 2).bitcast(BF16).rearrange("p (t u) -> p t u", t=3)
        zeros = take(P)
        near_tab = take(SPREAD * 3 * 2 * H // 2).bitcast(BF16)
        near_tab4 = near_tab.rearrange("p (u t k) -> p u t k", t=3, k=2 * H)
        score_rows = near_tab.bitcast(F32)[0:2 * H, 0:NP]
        tabT = carry_flat[0:NT, 0:2 * H * P]
        chosen = rst_flat[0:NT, 0:VPAD]
        tile_row = rst_flat[0:1, VPAD:2 * VPAD]
        asT3 = asT.rearrange("p (u h) -> p u h", h=H)[:, 2 * RING:, :]
        seg_flat = seg.rearrange("p a h g e -> p (a h g e)")
        ends_i, ends_t, ends_f, endk = (seg_flat[:, n * 2 * NB:(n + 1) * 2 * NB] for n in range(4))
        ends_i, ends_t = ends_i.bitcast(I32), ends_t.bitcast(I32)
        span, ones_row = (seg_flat[:, n * NB:(n + 1) * NB] for n in (8, 9))
        ones_tiles = tip.rearrange("p a g h -> p (a g h)")[0:1, 0:NT]
        W2 = STEP * P // 2
        rel_bc = [seg_flat[:, b * W2:(b + 1) * W2].bitcast(BF16) for b in range(2)]
        hi_w = STEP * 4 * NT // 2
        hi_hot = [seg_flat[:, 2 * W2 + b * hi_w:2 * W2 + (b + 1) * hi_w].bitcast(BF16)
                  .rearrange("p (u t n) -> p u t n", u=STEP, t=4) for b in range(2)]
        hotT = [hots_flat[:, b * W2:(b + 1) * W2].bitcast(BF16) for b in range(2)]
        lo_hot = [free[:, 0:W2].bitcast(BF16) for free in (parts_of_dst, rows_of_nb)]
        visit_tab = valv[:, :, 0:2 * H]

        names = """
                vector_order vector_passed pool_order pool_passed consts ends_in W0_in att_in xT_in0 xT_in1 xT_in2
                xT_in3 xT_in4 xT_scored block_ends_ready block_ends_spread blocks_known blocks_in tiles_ready
                tiles_turned rel_clamped rel_stored rel_bc0 rel_bc1 rel_bc2 rel_bc3 rel_bc4 tile_row_ready
                tile_row_spread scores_turned chosen_ready visit_tab_done visit_tab_taken scratch_used score_rows_taken
                scores_in_columns scores_kept normal_ready sums_zero0 last_taken hotT_ready spread_done spread_taken
                block_tips block_tips_turned tips_shifted tips_back wa_ready scores_out scores_stored edge_turned
                edge_taken src_index_ready xp_done xp_taken xp_stored0 xp_stored1 W1_in scores_got0 scores_got1
                source_scores_ready histo_ready histo_used histo_done histo_flags as_turned first_scan carry_turned
                carry_ready seeds_turned seg_ready seg_turned exp_in exp_out factors_in factors_out rows_in0 rows_in1
                rows_in2 rows_in3 rows_in4 rows_in5 rows_in6 rows_in7 rows_used0 rows_used1 hot_ready0 hot_ready1
                scaled_a0 scaled_a1 sums_taken0 sums_taken1 bias0_in bias1_in bias_cut bias_parts_in values_cut
                values_ready x_in0 x_in1 xp_in0 xp_in1 self_in self_out self_ready diag_ready mixed sums_mixed variance0
                variance1 deviation0 deviation1 x_free x1_ready x1_stored0 x1_stored1 W_high_ready W_low_ready
                aggT_low_ready agg_ready agg_turned aggT_ready product_ready product_taken x1_free x1_in0 x1_in1
                out_ready out_stored0 out_stored1 dst_sq_in dst_sq_out sums_zero1
                """.split()
        s = {name: ctx.enter_context(nc.semaphore(name)) for name in names}

        v, a, pe, gp = nc.vector, nc.scalar, nc.tensor, nc.gpsimd

        def low_of_W(k):
            return vals_r[:, k * D:(k + 1) * D] if k < KT // 2 else Wt_r[:, k, :]

        def low_of_sums(b, half):
            to = hots_r[:, D + half * 512:D + (half + 1) * 512] if b == 0 else (relT_r, srcT_r)[half][:, :]
            return to.rearrange("p (k n) -> p k n", n=P)

        def by_tiles(eng, body):
            with eng.Fori(0, NT // 2) as i:
                body(Tile(i, 0), 0)
                body(Tile(i, 1), 1)
            body(NT - 1, 0)

        def turn_of(j, b):
            return (j - b) // 2 if isinstance(j, int) else j.turn

        def by_visits(eng, body):
            with eng.Fori(0, ITERS) as i:
                for k in range(RING):
                    body(i, k)

        def by_steps(eng, body):
            with eng.Fori(0, NT // 5) as i:
                for b in range(5):
                    body(i, b)

        def load_xT(eng, slots):
            with eng.Fori(0, NT // 5) as i:
                for b in slots:
                    eng.wait_ge(s["xT_scored"], i * 5 + b + 1)
                    eng.dma_start(xT_flat[b], xT[bass.ds(i * (5 * P) + b * P, P), :]).then_inc(s[f"xT_in{b}"], 16)

        block = ctx.enter_context(nc.Block())

        @block.sync
        def _(eng):
            with nc.allow_non_contiguous_dma(reason="two words of each block"):
                eng.dma_start(ends_i[0:1, 0:NB], dst_blocks[0:NB, 0:1].rearrange("b e -> e b")).then_inc(s["ends_in"], 16)
                eng.dma_start(ends_i[0:1, NB:2 * NB],
                              dst_blocks[0:NB, EB - 1:EB].rearrange("b e -> e b")).then_inc(s["ends_in"], 16)
            eng.dma_start(Wt[:, :, :], W0.rearrange("(k p) n -> p k n", p=P)).then_inc(s["W0_in"], 16)
            eng.dma_start(att[:, 0:H, :], att_src.unsqueeze(0).broadcast_to([P, H, C])).then_inc(s["att_in"], 16)
            eng.dma_start(att[:, H:2 * H, :], att_dst.unsqueeze(0).broadcast_to([P, H, C])).then_inc(s["att_in"], 16)

            load_xT(eng, (0, 2, 4))
            eng.wait_ge(s["rel_clamped"], 1)
            eng.dma_start(rel_dram.rearrange("(g s) e -> s g e", g=G), rel_c).then_inc(s["rel_stored"], 16)
            eng.wait_ge(s["rel_stored"], 16)
            flat = rel_dram.rearrange("s e -> (s e)").unsqueeze(0)
            for b in range(5):
                eng.wait_ge(s["xT_scored"], NT + b + 1)
                eng.dma_start(xT_flat[b], xT[b * P:(b + 1) * P, :]).then_inc(s[f"xT_in{b}"], 16)

            def load_rel(i, b):
                eng.wait_ge(s["hotT_ready"], i * 5 + b + (2 if b == 0 else 1))
                eng.dma_start(rel_bc[b % 2], flat[:, bass.ds(i * (5 * STEP * P) + b * STEP * P, STEP * P)]
                              .broadcast_to([P, STEP * P])).then_inc(s[f"rel_bc{b}"], 16)

            with eng.Fori(0, NT // 5 - 1) as i:
                for b in range(5):
                    load_rel(i, b)
                    eng.wait_ge(s["xp_done"], i * 10 + 2 * b + 2)
                    eng.dma_start(xT_flat[b], xT[bass.ds(i * (5 * P) + (5 + b) * P, P), :]).then_inc(s[f"xT_in{b}"], 16)
            for b in range(5):
                load_rel(NT // 5 - 1, b)
            eng.wait_ge(s["xp_done"], 2 * NT)
            eng.dma_start(bias_row, bias0.unsqueeze(0)).then_inc(s["bias0_in"], 16)
            eng.wait_ge(s["bias_cut"], 1)
            for part in range(3):
                eng.dma_start(bias_parts[part:part + 1, :], bias_split[:, part * D:(part + 1) * D]) \
                    .then_inc(s["bias_parts_in"], 16)

            eng.wait_ge(s["rows_used0"], RING + VISITS)
            eng.wait_ge(s["hot_ready0"], VISITS + AHEAD)

            def load_xp(j, b):
                eng.wait_ge(s["mixed"], j + 1)
                eng.dma_start(xp_in[b], xp_dram[bass.ds(j * P, P), :]).then_inc(s[f"xp_in{b}"], 16)

            by_tiles(eng, load_xp)
            eng.wait_ge(s["mixed"], NT + 2)
            eng.wait_ge(s["values_cut"], ITERS + 1)
            eng.wait_ge(s["rows_used1"], 5 * RING)
            eng.dma_start(Wt[:, :, :], W1.rearrange("(k p) n -> p k n", p=P)).then_inc(s["W1_in"], 16)

            eng.wait_ge(s["rows_used1"], RING + VISITS)
            eng.wait_ge(s["hot_ready1"], VISITS + AHEAD)
            eng.dma_start(bias_at, bias1.unsqueeze(0).broadcast_to([P, D])).then_inc(s["bias1_in"], 16)

            def load_x1(j, b):
                eng.wait_ge(s["x1_free"], j + 1)
                eng.dma_start(x1_in[b], x1_dram[bass.ds(j * P, P), 0:D]).then_inc(s[f"x1_in{b}"], 16)

            by_tiles(eng, load_x1)

        @block.gpsimd
        def _(eng):
            order = Tally(s["pool_order"])

            def passed(sem, value):
                eng.wait_ge(sem, value)
                eng.sem_inc(s["pool_passed"], 1)

            gp.iota(iota_i, pattern=[[1, NB]], base=0, channel_multiplier=0).then_inc(s["consts"], 1)
            gp.iota(visit_i, pattern=[[P, G]], base=0, channel_multiplier=1).then_inc(s["consts"], 1)
            eng.wait_ge(s["blocks_known"], 1)
            for g in range(G):
                off = bass.IndirectOffsetOnAxis(ap=block_i[:, g:g + 1], axis=0)
                for to, dram in ((dst_i, dst_blocks), (src_i, src_blocks), (w_f, w_blocks)):
                    gp.indirect_dma_start(to[:, g, :], None, dram, off).then_inc(s["blocks_in"], 16)

            eng.wait_ge(s["src_index_ready"], 1)
            eng.wait_ge(s["scores_stored"], 16)
            turns = ITERS // 2

            def gather_scores(half, i, first):
                if not first:
                    passed(s[f"scores_got{half}"], i * (16 * RING))
                    order.inc(gp.tensor_copy(asT[:, bass.ds(i * (2 * RING * H) + half * RING * H, RING * H)], stage[half]))
                order.inc(gp.tensor_copy(idx[:, half * RING:(half + 1) * RING],
                                         srcT[:, bass.ds(i * (2 * RING) + half * RING, RING)]))
                passed(order.sem, order.value())
                if not first:
                    eng.sem_inc(s["scores_kept"], 1)
                for q in range(RING):
                    at = half * RING + q
                    gp.indirect_dma_start(stage[half][:, q * H:(q + 1) * H], None, as_dram,
                                          bass.IndirectOffsetOnAxis(ap=idx[:, at:at + 1], axis=0)) \
                        .then_inc(s[f"scores_got{half}"], 16)

            gather_scores(0, 0, True)
            gather_scores(1, 0, True)
            with eng.Fori(0, turns - 1) as i:
                order.enter(i, 4)
                gather_scores(0, i + 1, False)
                gather_scores(1, i + 1, False)
                order.leave(turns - 1)
            for half in range(2):
                eng.wait_ge(s[f"scores_got{half}"], 16 * RING * turns)
                at = turns * 2 * RING * H + half * RING * H
                gp.tensor_copy(asT[:, at:at + RING * H], stage[half]).then_inc(s["source_scores_ready"], 1)

            def cut_values(i):
                at = valv[:, bass.ds(i * RING, RING), :]
                parts = [val_parts4[:, bass.ds(i * RING, RING), t, :] for t in range(3)]
                for t in range(3):
                    order.inc(gp.tensor_copy(parts[t], at if t == 0 else val_rest))
                    passed(order.sem, order.value())
                    if t < 2:
                        order.inc(gp.tensor_tensor(val_rest, at if t == 0 else val_rest, parts[t], ALU.subtract))
                        passed(order.sem, order.value())
                eng.sem_inc(s["values_cut"], 1)

            def gather_rows(layer, table, width):
                def visits(i, k):
                    passed(s[f"rows_used{layer}"], i * RING + k + 2)
                    order.inc(gp.tensor_copy(idx[:, k:k + 2], srcT[:, bass.ds(i * RING + k, 2)]))
                    passed(order.sem, order.value())
                    for q in (k, k + 1):
                        gp.indirect_dma_start(row_ring[q][:, 0:width], None, table,
                                              bass.IndirectOffsetOnAxis(ap=idx[:, q:q + 1], axis=0)) \
                            .then_inc(s[f"rows_in{q}"], 16)

                def turn(i, cut_here):
                    for k in range(0, RING, 2):
                        visits(i, k)
                        if cut_here and k == 2:
                            cut_values(i + 1)

                if layer == 0:
                    turn(0, False)
                    eng.wait_ge(s["bias_parts_in"], 48)
                    eng.wait_ge(s["values_ready"], 1)
                    cut_values(0)
                    cut_values(1)
                first = 1 - layer
                with eng.Fori(first, ITERS) as i:
                    order.enter(i - first, RING // 2 + (5 if layer == 0 else 0))
                    turn(i, layer == 0)
                    order.leave(ITERS - first)

            eng.wait_ge(s["xp_stored0"], 16 * NT * 3 // 5)
            eng.wait_ge(s["xp_stored1"], 16 * NT * 2 // 5)
            gather_rows(0, xp_dram, D)

            def store_x1(j, b):
                eng.wait_ge(s["x_free"], j + 3)
                gp.tensor_copy(sums[:, bass.ds(j * D, D)], zero1[:, :].broadcast_to([P, D])).then_inc(s["sums_zero1"], 1)
                eng.wait_ge(s["x1_ready"], j + 3)
                gp.dma_start(x1_dram[bass.ds(j * P, P), :], x1_out[b]).then_inc(s[f"x1_stored{b}"], 16)

            by_tiles(eng, store_x1)
            eng.wait_ge(s["x1_stored0"], 16 * (NT - NT // 2))
            eng.wait_ge(s["x1_stored1"], 16 * (NT // 2))
            gather_rows(1, x1_dram, ROW1)

            def store_out(j, b):
                eng.wait_ge(s["out_ready"], j + 1)
                gp.dma_start(out[bass.ds(j * P, P), :], mix[b]).then_inc(s[f"out_stored{b}"], 16)

            with eng.Fori(0, NT // 2) as i:
                store_out(i * 2, 0)
                store_out(i * 2 + 1, 1)
            eng.wait_ge(s["out_ready"], NT)
            gp.dma_start(out[(NT - 1) * P:N, :], mix[0][0:N - (NT - 1) * P, :]).then_inc(s["out_stored0"], 16)
            eng.wait_ge(s["out_stored0"], 16 * (NT - NT // 2))
            eng.wait_ge(s["out_stored1"], 16 * (NT // 2))

        @block.tensor
        def _(eng):
            eng.wait_ge(s["block_ends_ready"], 1)
            for c in range(2):
                ins = pe.matmul(bank[5 + c][:, 0:NB], ones_row[0:1, 0:P], endk[0:1, c * NB:(c + 1) * NB], start=True,
                                stop=True)
            ins.then_inc(s["block_ends_spread"], 1)
            eng.wait_ge(s["tiles_ready"], 1)
            for g in range(G):
                ins = pe.transpose(bank[2][0:1, g * P:(g + 1) * P], jv[:, g:g + 1], ident[:, :])
            ins.then_inc(s["tiles_turned"], 1)
            eng.wait_ge(s["block_tips"], 1)
            for g in range(G):
                ins = pe.transpose(bank[7][0:2, g * P:(g + 1) * P], ends2[:, g, :], ident[:, :])
            ins.then_inc(s["block_tips_turned"], 1)
            eng.wait_ge(s["tips_shifted"], 1)
            for side in range(2):
                for g in range(G):
                    ins = pe.transpose(bank[4][:, (side * G + g) * 2:(side * G + g) * 2 + 2],
                                       shift[0:2, g * P + 2 * side:g * P + 2 * side + P], ident[0:2, 0:2])
            ins.then_inc(s["tips_back"], 1)

            eng.wait_ge(s["edge_turned"], 1)
            for n, item in enumerate((src_f, rel_f, w_f, brk[:, 1])):
                for g in range(G):
                    ins = pe.transpose(bank[(0, 1, 3, 6)[n]][:, g * P:(g + 1) * P], item[:, g, :], ident[:, :])
                ins.then_inc(s["edge_taken"], 1)

            eng.wait_ge(s["wa_ready"], KT * 2 * H)
            eng.wait_ge(s["last_taken"], 1)
            with eng.Fori(0, NT // 5) as i:
                for b in range(5):
                    eng.wait_ge(s[f"xT_in{b}"], i * 16 + 16)
                    for k in range(KT):
                        ins = pe.matmul(psum_flat[0:2 * H, bass.ds(i * (5 * P) + b * P, P)], wa[:, k, :],
                                        xT_ring[b][:, k, :], start=(k == 0), stop=(k == KT - 1))
                    ins.then_inc(s["xT_scored"], 1)

            eng.wait_ge(s["tile_row_ready"], 1)
            pe.matmul(bank[7][0:NT, 0:VPAD], ones_tiles[0:1, 0:NT], tile_row, start=True, stop=True) \
                .then_inc(s["tile_row_spread"], 1)
            eng.wait_ge(s["score_rows_taken"], 2)
            for j in range(NT):
                ins = pe.transpose(bank[5][:, j * 2 * H:(j + 1) * 2 * H], score_rows[:, j * P:(j + 1) * P],
                                   ident[0:2 * H, 0:2 * H])
            ins.then_inc(s["scores_in_columns"], 1)
            eng.wait_ge(s["scores_out"], 1)
            for k in range(2 * H):
                ins = pe.transpose(bank[k // 4][0:NT, (k % 4) * P:(k % 4 + 1) * P], tabv[:, :, k], ident[:, :])
            ins.then_inc(s["scores_turned"], 1)
            eng.wait_ge(s["chosen_ready"], 2)
            for k in range(2 * H):
                pe.matmul(bank[k][:, 0:SPREAD], tabT[:, k * P:(k + 1) * P], chosen[:, 0:SPREAD], start=True, stop=True) \
                    .then_inc(s["visit_tab_done"], 1)
            eng.wait_ge(s["visit_tab_taken"], 2 * H)
            eng.wait_ge(s["histo_flags"], 1)

            pe.matmul(bank[4][:, 0:4 * NT], zeros, zeros[:, 0:4 * NT], start=True, stop=False, skip_group_check=True)

            def project(i, b):
                eng.wait_ge(s[f"xT_in{b}"], i * 16 + 16 * (NT // 5) + 16)
                for c in range(2):
                    eng.wait_ge(s["xp_taken"], i * 10 + b * 2 + c + 1)
                    for k in range(KT):
                        ins = pe.matmul(bank[XP_BANKS[b % 3][c]][:, :], xT_ring[b][:, k, :],
                                        Wt[:, k, c * 512:(c + 1) * 512], start=(k == 0), stop=(k == KT - 1))
                    ins.then_inc(s["xp_done"], 1)
                eng.wait_ge(s["hotT_ready"], i * 5 + b + 3)
                eng.wait_ge(s["spread_taken"], i * 5 + b + 1)
                for u in range(STEP):
                    ins = pe.matmul(bank[7][:, u * 24:(u + 1) * 24], hotT[b % 2][:, u * P:(u + 1) * P],
                                    near_tab[:, bass.ds((i * 5 + b) * (STEP * 24) + u * 24, 24)], start=True, stop=True)
                ins.then_inc(s["spread_done"], 1)
                eng.wait_ge(s["histo_ready"], i * 5 + b + 1)
                for u in range(STEP):
                    ins = pe.matmul(bank[4][:, 0:4 * NT], lo_hot[b % 2][:, u * P:(u + 1) * P],
                                    hi_hot[b % 2][:, u, :, :].rearrange("p t n -> p (t n)"), start=False,
                                    stop=False, skip_group_check=True)
                ins.then_inc(s["histo_used"], 1)

            by_steps(eng, project)
            pe.matmul(bank[4][:, 0:4 * NT], zeros, zeros[:, 0:4 * NT], start=False, stop=True,
                      skip_group_check=True).then_inc(s["histo_done"], 1)

            eng.wait_ge(s["xp_taken"], 4 + 2 * NT)
            for g in range(G):
                if g < G - 1:
                    eng.wait_ge(s["scores_kept"], P * (g + 1) // RING)
                else:
                    eng.wait_ge(s["source_scores_ready"], 2)
                for h in range(H):
                    ins = pe.transpose(bank[g][:, h * P:(h + 1) * P], asT3[:, g * P:(g + 1) * P, h], ident[:, :])
                ins.then_inc(s["as_turned"], 1)
            eng.wait_ge(s["first_scan"], 1)
            for side in range(2):
                for g in range(G):
                    pe.transpose(bank[(5, 7)[side]][0:H, g * P:(g + 1) * P], tip[:, side, g, :], ident[:, :])
                    ins = pe.transpose(bank[(6, 4)[side]][0:H, g * P:(g + 1) * P], rst[:, side, g, :], ident[:, :])
            ins.then_inc(s["carry_turned"], 1)
            eng.wait_ge(s["carry_ready"], 1)
            for side in range(2):
                for g in range(G):
                    ins = pe.transpose(bank[5][:, (side * G + g) * H:(side * G + g + 1) * H],
                                       carry[0:H, side, g * P + side:g * P + side + P], ident[0:H, 0:H])
            ins.then_inc(s["seeds_turned"], 1)
            for h in range(H):
                eng.wait_ge(s["seg_ready"], h + 1)
                for g in range(G):
                    ins = pe.transpose(bank[4 + h][:, g * P:(g + 1) * P], seg[:, 0, h, g, :], ident[:, :])
                ins.then_inc(s["seg_turned"], 1)

            def carry_rows(layer):
                def visit(i, k):
                    b = k % 2
                    eng.wait_ge(s[f"scaled_a{layer}"], i * RING + k + 1)
                    eng.wait_ge(s[f"sums_taken{layer}"], i * RING + k + 1)
                    eng.wait_ge(s[f"rows_in{k}"], i * 16 + 16 * ITERS * layer + 16)
                    if layer == 0:
                        for h in range(H):
                            pe.matmul(psum[:, 2 * b + h // 2, (h % 2) * C:(h % 2 + 1) * C],
                                      hots[:, k % 4, (1 + h) * P:(2 + h) * P], row_ring[k][:, h * C:(h + 1) * C],
                                      start=(h % 2 == 0), stop=True, skip_group_check=True)
                        if k == 0:
                            eng.wait_ge(s["values_cut"], i + 1)
                        ins = pe.matmul(bank[4 + b][:, 0:3 * NV], hot_of[k % 4],
                                        val_parts[:, bass.ds(i * (RING * 3 * NV) + k * 3 * NV, 3 * NV)], start=True,
                                        stop=True)
                    else:
                        for c in range(2):
                            ins = pe.matmul(psum[:, 2 * b + c, :], hots[:, k % 4, P:2 * P],
                                            row_ring[k][:, c * 512:(c + 1) * 512], start=True, stop=True)
                    ins.then_inc(s[f"rows_used{layer}"], 1)

                by_visits(eng, visit)

            carry_rows(0)

            eng.wait_ge(s["bias_parts_in"], 48)
            eng.wait_ge(s["self_ready"], 1)

            def self_loop(j, b):
                eng.wait_ge(s["diag_ready"], j + 1)
                eng.wait_ge(s[f"xp_in{b}"], turn_of(j, b) * 16 + 16)
                eng.wait_ge(s["sums_mixed"], j + 1)
                for c in range(2):
                    pe.matmul(psum[:, 2 * b + c, :], ones3, bias_parts[:, c * 512:(c + 1) * 512], start=True, stop=False,
                              skip_group_check=True)
                    for h in (2 * c, 2 * c + 1):
                        ins = pe.matmul(psum[:, 2 * b + c, (h % 2) * C:(h % 2 + 1) * C], diag[b][:, h * P:(h + 1) * P],
                                        xp_in[b][:, h * C:(h + 1) * C], start=False, stop=True, skip_group_check=True)
                ins.then_inc(s["mixed"], 1)

            by_tiles(eng, self_loop)
            carry_rows(1)

            eng.wait_ge(s["W1_in"], 16)
            eng.wait_ge(s["sums_taken1"], 2 + VISITS)

            def turn_sums(j, b, low=True):
                eng.wait_ge(s["agg_ready"], j + 1)
                if not (isinstance(j, int) and j == 0):
                    eng.wait_ge(s["aggT_ready"], j + 0)
                if low:
                    eng.wait_ge(s["aggT_low_ready"], j - WHOLE)
                for k in range(KT):
                    ins = pe.transpose(psum[:, 4 + k // 4, (k % 4) * P:(k % 4 + 1) * P], agg[b][:, k * P:(k + 1) * P],
                                       ident[:, :])
                ins.then_inc(s["agg_turned"], 1)

            def product(j, b):
                eng.wait_ge(s["aggT_ready"], j + 1)
                eng.wait_ge(s["product_taken"], j + 1)
                for c in range(2):
                    for k in range(KT):
                        ins = pe.matmul(psum[:, 2 * b + c, :], aggT[b][:, k, :], Wt[:, k, c * 512:(c + 1) * 512],
                                        start=(k == 0), stop=(k == KT - 1))
                ins.then_inc(s["product_ready"], 1)

            def product_in_parts(j, b, first=False):
                eng.wait_ge(s["aggT_ready"], j + 1)
                eng.wait_ge(s["aggT_low_ready"], j - (WHOLE - 1))
                eng.wait_ge(s["product_taken"], j + 1)
                for k in range(KT):
                    for c in range(2):
                        pe.matmul(psum[:, 2 * b + c, :], aggT_high[b][:, k, :], W_high[k][:, c * 512:(c + 1) * 512],
                                  start=(k == 0), stop=False, skip_group_check=True)
                for k in range(KT):
                    for c in range(2):
                        pe.matmul(psum[:, 2 * b + c, :], low_of_sums(b, k // 4)[:, k % 4, :],
                                  W_high[k][:, c * 512:(c + 1) * 512], start=False, stop=False, skip_group_check=True)
                for k in range(KT):
                    if first:
                        eng.wait_ge(s["W_low_ready"], k + 1)
                    for c in range(2):
                        ins = pe.matmul(psum[:, 2 * b + c, :], aggT_high[b][:, k, :],
                                        low_of_W(k)[:, c * 512:(c + 1) * 512], start=False, stop=(k == KT - 1),
                                        skip_group_check=True)
                ins.then_inc(s["product_ready"], 1)

            turn_sums(0, 0, low=False)
            turn_sums(1, 1, low=False)
            with eng.Fori(0, WHOLE // 2 - 1) as i:
                product(Tile(i, 0), 0)
                turn_sums(Tile(i + 1, 0), 0, low=False)
                product(Tile(i, 1), 1)
                turn_sums(Tile(i + 1, 1), 1, low=False)
            product(WHOLE - 2, 0)
            turn_sums(WHOLE, 0, low=False)
            product(WHOLE - 1, 1)
            turn_sums(WHOLE + 1, 1)
            eng.wait_ge(s["W_high_ready"], KT)
            product_in_parts(WHOLE, 0, first=True)
            turn_sums(WHOLE + 2, 0)
            with eng.Fori(WHOLE // 2, NT // 2 - 1) as i:
                product_in_parts(Tile(i, 1), 1)
                turn_sums(Tile(i + 1, 1), 1)
                product_in_parts(Tile(i + 1, 0), 0)
                turn_sums(Tile(i + 2, 0), 0)
            product_in_parts(NT - 2, 1)
            product_in_parts(NT - 1, 0)

        @block.scalar
        def _(eng):
            load_xT(eng, (1, 3))
            eng.wait_ge(s["xT_scored"], 5 + NT)
            a.copy(score_rows[:, 3 * 512:], psum_flat[0:2 * H, 3 * 512:NP]).then_inc(s["score_rows_taken"], 1)
            eng.wait_ge(s["scores_out"], 1)
            with nc.allow_non_contiguous_dma(reason="four scores per node"):
                a.dma_start(as_dram.rearrange("(j p) h -> p j h", p=P), tabv[:, :, 0:H]).then_inc(s["scores_stored"], 16)
            eng.wait_ge(s["scores_turned"], 1)
            for c in range(2):
                ins = a.copy(tabT[:, c * 512:(c + 1) * 512], bank[c][0:NT, :])
            ins.then_inc(s["chosen_ready"], 1)
            for k in range(2 * H):
                eng.wait_ge(s["visit_tab_done"], k + 1)
                a.copy(visit_tab[:, :, k], bank[k][:, 0:SPREAD]).then_inc(s["visit_tab_taken"], 1)

            def take_xp(i, b, first):
                slot = b % 2
                if not (first and b < 2):
                    eng.wait_ge(s[f"xp_stored{slot}"], (i * 3 + b // 2) * 16 if slot == 0 else (i * 2 + b // 2) * 16)
                for c in range(2):
                    eng.wait_ge(s["xp_done"], i * 10 + b * 2 + c + 1)
                    a.copy(xp_stage[slot][:, c * 512:(c + 1) * 512], bank[XP_BANKS[b % 3][c]][:, :]) \
                        .then_inc(s["xp_taken"], 1)
                eng.wait_ge(s["xp_taken"], 4 + i * 10 + b * 2 + 2)
                a.dma_start(xp_dram[bass.ds(i * (5 * P) + b * P, P), :], xp_stage[slot]).then_inc(s[f"xp_stored{slot}"], 16)

            for b in range(5):
                take_xp(0, b, True)
            with eng.Fori(0, NT // 5 - 1) as i:
                for b in range(5):
                    take_xp(i + 1, b, False)
            eng.wait_ge(s["spread_taken"], 1 + NT)
            eng.wait_ge(s["histo_done"], 1)
            a.copy(sums[:, late:], zero1[:, :].broadcast_to([P, NT * D - late]))
            eng.wait_ge(s["factors_in"], 1)
            a.activation(hist_f[:, 0:2 * NT], hist_f[:, 0:2 * NT], ACT.Sqrt).then_inc(s["factors_out"], 1)
            eng.wait_ge(s["exp_in"], 1)
            a.activation(valv[:, :, 0:H], adT[:, :, 0:H], ACT.Exp).then_inc(s["exp_out"], 1)
            eng.wait_ge(s["exp_out"], 1)
            eng.wait_ge(s["scratch_used"], 1)
            a.copy(sums[:, late // 2:late], zero1[:, :].broadcast_to([P, late - late // 2])).then_inc(s["sums_zero0"], 1)

            def scale0(i, k):
                eng.wait_ge(s["hot_ready0"], i * RING + k + 1)
                for h in range(H):
                    ins = a.activation(hots[:, k % 4, (1 + h) * P:(2 + h) * P], hot_of[k % 4], ACT.Copy,
                                       scale=vals[:, bass.ds(i * (RING * NV) + k * NV + h, 1)])
                ins.then_inc(s["scaled_a0"], 1)

            by_visits(eng, scale0)

            eng.wait_ge(s["rows_used0"], RING + VISITS)
            for b in range(2):
                a.dma_start(x_in[b], x[b * P:(b + 1) * P, :]).then_inc(s[f"x_in{b}"], 16)
            eng.wait_ge(s["self_in"], 1)
            a.activation(t_self, t_self, ACT.Exp, scale=-1.0).then_inc(s["self_out"], 1)
            eng.wait_ge(s["dst_sq_in"], 1)
            a.activation(mix[1][:, 0:2 * NT], mix[1][:, 0:2 * NT], ACT.Sqrt).then_inc(s["dst_sq_out"], 1)
            eng.wait_ge(s["self_ready"], 1)

            def make_diag(j, b):
                eng.wait_ge(s["mixed"], j + 1)
                for h in range(H):
                    ins = a.activation(diag[b][:, h * P:(h + 1) * P], ident[:, :], ACT.Copy,
                                       scale=c_self[:, bass.ds(j * H + h, 1)])
                ins.then_inc(s["diag_ready"], 1)

            def deviate(layer):
                def one(j, b):
                    eng.wait_ge(s[f"variance{layer}"], j + 1)
                    a.activation(spread[b][:, 1:2], spread[b][:, 0:1], ACT.Sqrt).then_inc(s[f"deviation{layer}"], 1)
                return one

            def apply_norm(j, b):
                eng.wait_ge(s["normal_ready"], j + 1)
                a.activation(x1_out[b][:, 0:D], mix[b], ACT.Identity, bias=shifted[b], scale=spread[b][:, 0:1]) \
                    .then_inc(s["x1_ready"], 1)

            def load_x(j, b):
                eng.wait_ge(s["x_free"], j + 1)
                a.dma_start(x_in[b], x[bass.ds(j * P, P), :]).then_inc(s[f"x_in{b}"], 16)

            make_diag(0, 0)
            make_diag(1, 1)
            make_diag(2, 0)
            deviate(0)(0, 0)
            load_x(2, 0)
            with eng.Fori(0, NT // 2 - 1) as i:
                make_diag(i * 2 + 3, 1)
                deviate(0)(i * 2 + 1, 1)
                load_x(i * 2 + 3, 1)
                apply_norm(i * 2, 0)
                make_diag(i * 2 + 4, 0)
                deviate(0)(i * 2 + 2, 0)
                load_x(i * 2 + 4, 0)
                apply_norm(i * 2 + 1, 1)
            deviate(0)(NT - 2, 1)
            apply_norm(NT - 3, 0)
            deviate(0)(NT - 1, 0)
            apply_norm(NT - 2, 1)
            apply_norm(NT - 1, 0)

            def scale1(i, k):
                eng.wait_ge(s["hot_ready1"], i * RING + k + 1)
                eng.wait_ge(s[f"rows_in{k}"], i * 16 + 16 * ITERS + 16)
                ins = a.activation(hots[:, k % 4, P:2 * P], hots[:, k % 4, 0:P], ACT.Copy, scale=row_ring[k][:, D:D + 1])
                ins.then_inc(s["scaled_a1"], 1)

            by_visits(eng, scale1)

            def scale_sums(j, b):
                if not (isinstance(j, int) and j < 2):
                    eng.wait_ge(s["agg_turned"], j - 1)
                a.activation(agg[b], sums[:, bass.ds(j * D, D)], ACT.Copy, scale=fdst[:, bass.ds(j + 0, 1)]) \
                    .then_inc(s["agg_ready"], 1)

            def take_turned(j, b, part=True):
                eng.wait_ge(s["agg_turned"], j + 1)
                if not (isinstance(j, int) and j < 2):
                    eng.wait_ge(s["product_ready"], j - 1)
                to = aggT_high[b] if part else aggT[b]
                a.copy(to.rearrange("p k n -> p (k n)"), psum[:, 4:6, :].rearrange("p c n -> p (c n)")) \
                    .then_inc(s["aggT_ready"], 1)

            def high_of_W(k):
                eng.wait_ge(s["agg_ready"], k + 1)
                a.copy(sums_r[:, bass.ds(k * D, D)], W_flat[:, bass.ds(k * D, D)]).then_inc(s["W_high_ready"], 1)

            eng.wait_ge(s["sums_taken1"], 2 + VISITS)
            eng.wait_ge(s["W1_in"], 16)
            for j in range(2):
                scale_sums(j, j)
                take_turned(j, j, part=False)

            def whole(j, b):
                scale_sums(j + 2, b)
                take_turned(j + 2, b, part=False)
                high_of_W(j + 0)
                deviate(1)(j + 0, b)

            with eng.Fori(0, WHOLE // 2 - 1) as i:
                whole(Tile(i, 0), 0)
                whole(Tile(i, 1), 1)
            for j in (WHOLE - 2, WHOLE - 1):
                high_of_W(j)
                scale_sums(j + 2, j % 2)
                take_turned(j + 2, j % 2)
                deviate(1)(j, j % 2)

            def in_parts(j, b):
                scale_sums(j + 2, b)
                take_turned(j + 2, b)
                deviate(1)(j + 0, b)

            in_parts(WHOLE, 0)
            with eng.Fori(WHOLE // 2, NT // 2 - 1) as i:
                in_parts(Tile(i, 1), 1)
                in_parts(Tile(i + 1, 0), 0)
            deviate(1)(NT - 2, 1)
            deviate(1)(NT - 1, 0)

        @block.vector
        def _(eng):
            order = Tally(s["vector_order"])

            def then(ins):
                order.inc(ins)
                eng.wait_ge(order.sem, order.value())

            eng.sem_inc(s["xT_scored"], 5)
            eng.sem_inc(s["hotT_ready"], 2)
            eng.sem_inc(s["spread_taken"], 1)
            eng.sem_inc(s["xp_taken"], 4)
            eng.sem_inc(s["histo_used"], 2)
            for layer in range(2):
                eng.sem_inc(s[f"rows_used{layer}"], RING)
                eng.sem_inc(s[f"sums_taken{layer}"], 2)
            for name in ("x_free", "mixed", "sums_mixed", "product_taken", "x1_free", "x1_ready"):
                eng.sem_inc(s[name], 2)
            v.memset(zero1[:, :], 0.0)
            eng.wait_ge(s["consts"], 2)
            v.tensor_copy(iota_f[:, :], iota_i[:, 0:EB])
            v.tensor_copy(iota_w, iota_i)
            v.tensor_copy(iota_b, iota_i[:, 0:P])
            v.memset(ones_row, 1.0)
            v.memset(vals[:, :], 0.0)
            v.memset(nodesum[:, :], 0.0)
            v.memset(asT, 0.0)
            v.memset(shift, -7.0)
            v.memset(zeros, 0.0)
            then(v.tensor_copy(visit_no[:, :], visit_i))
            then(v.tensor_scalar(ident[:, :], iota_f[:, 0:P], visit_no[:, 0:1], None, ALU.is_equal))
            v.memset(valv[:, :, NV - 1], 1.0)

            eng.wait_ge(s["ends_in"], 32)
            then(v.tensor_single_scalar(ends_t[0:1, :], ends_i[0:1, :], 7, ALU.arith_shift_right))
            then(v.tensor_copy(ends_f[0:1, :], ends_t[0:1, :]))
            then(v.scalar_tensor_tensor(span[0:1, :], ends_f[0:1, NB:2 * NB], 1.0, ends_f[0:1, 0:NB], ALU.add, ALU.subtract))
            then(v.tensor_tensor_scan(endk[0:1, 0:NB], ones_row[0:1, 0:NB], span[0:1, :], 0.0, ALU.mult, ALU.add))
            then(v.tensor_tensor(tmp_row[0:1, :], endk[0:1, 0:NB], span[0:1, :], ALU.subtract))
            v.tensor_tensor(endk[0:1, NB:2 * NB], tmp_row[0:1, :], ends_f[0:1, 0:NB], ALU.subtract) \
                .then_inc(s["block_ends_ready"], 1)
            eng.wait_ge(s["block_ends_spread"], 1)
            for g in range(G):
                then(v.tensor_scalar(dump[:, 0:NB], bank[5][:, 0:NB], visit_no[:, g:g + 1], None, ALU.is_le, ALU.add,
                                     accum_out=tcount[:, g:g + 1]))
                then(v.tensor_scalar(mask, iota_w, tcount[:, g:g + 1], None, ALU.is_equal))
                then(v.tensor_tensor_reduce(dump[:, 0:NB], mask, bank[6][:, 0:NB], 1.0, 0.0, ALU.mult, ALU.add,
                                            ksel[:, g:g + 1]))
            v.tensor_copy(block_i, tcount).then_inc(s["blocks_known"], 1)
            then(v.scalar_tensor_tensor(jv2, ksel, -1.0, visit_no[:, :], ALU.mult, ALU.add))
            v.tensor_scalar(jv, jv2, float(NT - 1), None, ALU.min).then_inc(s["tiles_ready"], 1)
            eng.wait_ge(s["tiles_ready"], 1)
            then(v.tensor_scalar(j128, jv, float(P), None, ALU.mult))
            eng.wait_ge(s["tiles_turned"], 1)
            v.memset(ones_tiles, 1.0)
            v.tensor_copy(tile_row, bank[2][0:1, 0:VPAD])
            v.tensor_copy(tile_of[:, :], bank[2][0:1, 0:VPAD]).then_inc(s["tile_row_ready"], 1)

            eng.wait_ge(s["W0_in"], 16)
            eng.wait_ge(s["att_in"], 32)
            for k in range(KT):
                for h in range(2 * H):
                    if k * 2 * H + h >= 4:
                        eng.wait_ge(s["wa_ready"], k * 2 * H + h - 3)
                    head = Wt[:, k, (h % H) * C:(h % H + 1) * C]
                    v.tensor_tensor_reduce(dump[:, (h % 4) * C:(h % 4 + 1) * C], head, att[:, h, :], 1.0, 0.0, ALU.mult,
                                           ALU.add, wa[:, k, h:h + 1]).then_inc(s["wa_ready"], 1)

            eng.wait_ge(s["blocks_in"], 16 * 3 * G)
            v.tensor_copy(src_f, src_i)
            then(v.tensor_copy(dst_f, dst_i))
            v.tensor_copy(ends2, dst_f[:, :, 0:EB:EB - 1]).then_inc(s["block_tips"], 1)
            for g in range(G):
                ins = v.tensor_scalar(rel_f[:, g, :], dst_f[:, g, :], j128[:, g:g + 1], None, ALU.subtract)
            then(ins)
            v.tensor_scalar(rel_c, rel_f, -1.0, float(P), ALU.max, ALU.min).then_inc(s["rel_clamped"], 1)
            v.tensor_tensor(brk[:, 0, :, 1:EB], dst_f[:, :, 1:EB], dst_f[:, :, 0:EB - 1], ALU.not_equal)
            v.tensor_tensor(brk[:, 1, :, 0:EB - 1], dst_f[:, :, 1:EB], dst_f[:, :, 0:EB - 1], ALU.not_equal)
            eng.wait_ge(s["block_tips_turned"], 1)
            v.tensor_copy(shift[0:2, 1:VPAD + 1], bank[7][0:2, 0:VPAD]).then_inc(s["tips_shifted"], 1)
            eng.wait_ge(s["tips_back"], 1)
            then(v.tensor_copy(near, bank[4][:, 0:4 * G].rearrange("p (a g k) -> p a g k", a=2, g=G)))
            v.tensor_tensor(brk[:, 0, :, 0:1], dst_f[:, :, 0:1], near[:, 0, :, 1:2], ALU.not_equal)
            then(v.tensor_tensor(brk[:, 1, :, EB - 1:EB], dst_f[:, :, EB - 1:EB], near[:, 1, :, 0:1], ALU.not_equal))
            eng.sem_inc(s["edge_turned"], 1)
            eng.wait_ge(s["edge_taken"], 4)
            pen = brk

            then(v.tensor_copy(srcT[:, :], bank[0]))
            eng.sem_inc(s["src_index_ready"], 1)
            v.tensor_copy(relT[:, :], bank[1])
            v.tensor_copy(valv[:, :, 2 * H], bank[3][:, 0:SPREAD])
            then(v.tensor_copy(last, bank[6]))
            brk_flat = brk.rearrange("p a g e -> p (a g e)")
            eng.sem_inc(s["last_taken"], 1)

            sent = [v.tensor_single_scalar(w_i, srcT[:, :], n, op) for w_i, n, op in
                    ((lo_i, P - 1, ALU.bitwise_and), (hi_i, 7, ALU.arith_shift_right))]
            then(sent[-1])
            v.tensor_copy(lo_f, lo_i)
            v.tensor_copy(hi_f, hi_i)
            then(v.tensor_scalar(wok, relT[:, :], 0.0, None, ALU.is_ge))
            then(v.scalar_tensor_tensor(okT, relT[:, :], float(P - 1), wok, ALU.is_le, ALU.mult))
            then(v.tensor_tensor(wok[:, 0:SPREAD], okT[:, 0:SPREAD], valv[:, :, 2 * H], ALU.mult))
            then(v.tensor_copy(w_part[:, 0, :], wok))
            then(v.tensor_tensor(wok, wok, w_part[:, 0, :], ALU.subtract))
            then(v.tensor_copy(w_part[:, 1, :], wok))
            then(v.tensor_tensor(wok, wok, w_part[:, 1, :], ALU.subtract))
            v.tensor_copy(w_part[:, 2, :], wok).then_inc(s["histo_flags"], 1)
            eng.wait_ge(s["histo_flags"], 1)

            eng.wait_ge(s["tile_row_spread"], 1)
            v.tensor_scalar(chosen, bank[7][0:NT, 0:VPAD], visit_no[0:NT, 0:1], None, ALU.is_equal) \
                .then_inc(s["chosen_ready"], 1)
            eng.wait_ge(s["xT_scored"], 5 + NT)
            v.tensor_copy(score_rows[:, 0:3 * 512], psum_flat[0:2 * H, 0:3 * 512]).then_inc(s["score_rows_taken"], 1)
            eng.wait_ge(s["scores_in_columns"], 1)
            then(v.tensor_copy(tab[:, :], bank[5][:, 0:NT * 2 * H]))
            eng.sem_inc(s["scores_out"], 1)
            eng.wait_ge(s["visit_tab_taken"], 2 * H)
            for part in range(3):
                then(v.tensor_copy(near_tab4[:, :, part, :], visit_tab))
                if part < 2:
                    then(v.tensor_tensor(visit_tab, visit_tab, near_tab4[:, :, part, :], ALU.subtract))
            v.memset(carry, -BIG)
            v.memset(rst_h[0:H], 0.0)

            def spread_step(i, b):
                u0, slot = i * (5 * STEP) + b * STEP, b % 2
                eng.wait_ge(s[f"rel_bc{b}"], i * 16 + 16)
                eng.wait_ge(s["spread_taken"], i * 5 + b + 1)
                v.tensor_scalar(hotT[slot], rel_bc[slot], visit_no[:, 0:1], None, ALU.is_equal).then_inc(s["hotT_ready"], 1)
                eng.wait_ge(s["histo_used"], i * 5 + b + (2 if b == 0 else 1))
                for u in range(STEP):
                    v.tensor_scalar(lo_hot[slot][:, u * P:(u + 1) * P], iota_b, lo_f[:, bass.ds(u0 + u, 1)], None,
                                    ALU.is_equal)
                hi = hi_f[:, bass.ds(u0, STEP)].unsqueeze(2).broadcast_to([P, STEP, NT])
                then(v.tensor_tensor(hi_hot[slot][:, :, 0, :], iota_f[:, 0:NT].unsqueeze(1).broadcast_to([P, STEP, NT]), hi,
                                     ALU.is_equal))
                for part in range(3):
                    v.tensor_tensor(hi_hot[slot][:, :, 1 + part, :], hi_hot[slot][:, :, 0, :],
                                    w_part[:, part, bass.ds(u0, STEP)].unsqueeze(2).broadcast_to([P, STEP, NT]), ALU.mult)
                then(v.tensor_tensor(hi_hot[slot][:, :, 0, :], hi_hot[slot][:, :, 0, :],
                                     okT[:, bass.ds(u0, STEP)].unsqueeze(2).broadcast_to([P, STEP, NT]), ALU.mult))
                eng.sem_inc(s["histo_ready"], 1)
                eng.wait_ge(s["spread_done"], i * 5 + b + 1)
                v.tensor_reduce(ad_flat[:, bass.ds(u0 * (2 * H), STEP * 2 * H)].rearrange("p (u k) -> p u k", u=STEP),
                                bank[7][:, 0:STEP * 24].rearrange("p (u t k) -> p u k t", u=STEP, t=3), AX.X, ALU.add) \
                    .then_inc(s["spread_taken"], 1)

            with eng.Fori(0, NT // 5) as i:
                order.enter(i, 10)
                for b in range(5):
                    spread_step(i, b)
                order.leave(NT // 5)
            eng.wait_ge(s["spread_taken"], 1 + NT)
            then(v.tensor_scalar(brk_flat, brk_flat, -BIG, None, ALU.mult))
            for side in range(2):
                for h in range(H):
                    v.tensor_reduce(rst[:, side, :, h], pen[:, side], AX.X, ALU.min)
            eng.wait_ge(s["histo_done"], 1)
            then(v.tensor_scalar(hist_f[:, 0:NT], bank[4][:, 0:NT], 1.0, None, ALU.max))
            then(v.tensor_scalar(hist_f[:, 2 * NT:3 * NT], bank[4][:, 0:NT], 0.0, None, ALU.is_equal))
            then(v.tensor_copy(hist_f[:, 3 * NT:4 * NT], bank[4][:, NT:2 * NT]))
            for part in (2, 3):
                weight_sum = hist_f[:, 3 * NT:4 * NT]
                then(v.tensor_tensor(weight_sum, weight_sum, bank[4][:, part * NT:(part + 1) * NT], ALU.add))
            then(v.tensor_tensor(hist_f[:, NT:2 * NT], hist_f[:, 3 * NT:4 * NT], hist_f[:, 2 * NT:3 * NT], ALU.add))
            eng.sem_inc(s["factors_in"], 1)
            eng.wait_ge(s["factors_out"], 1)
            then(v.tensor_tensor(hist_f[:, 2 * NT:3 * NT], hist_f[:, 0:NT], hist_f[:, NT:2 * NT], ALU.mult))
            then(v.reciprocal(fsrc[:, :], hist_f[:, 2 * NT:3 * NT]))

            eng.wait_ge(s["bias0_in"], 16)
            v.memset(ones3, 1.0)
            for part in range(3):
                then(v.tensor_copy(bias_split[:, part * D:(part + 1) * D], bias_row))
                if part < 2:
                    then(v.tensor_tensor(bias_row, bias_row, bias_split[:, part * D:(part + 1) * D], ALU.subtract))
            eng.sem_inc(s["bias_cut"], 1)

            def scan(side, h, g, first):
                o, p_, d_ = seg[:, side, h, g, :], pen[:, side, g, :], bank[g][:, h * EB:(h + 1) * EB]
                if side:
                    o, p_, d_ = o[:, ::-1], p_[:, ::-1], d_[:, ::-1]
                return v.tensor_tensor_scan(o, p_, d_, -BIG if first else seed[:, side, g, h:h + 1], ALU.add, ALU.max)

            for g in range(G):
                eng.wait_ge(s["as_turned"], g + 1)
                for side in range(2):
                    for h in range(H):
                        ins = scan(side, h, g, True)
            then(ins)
            for side in range(2):
                end = EB - 1 if side == 0 else 0
                ins = v.tensor_copy(tip[:, side], seg[:, side, :, :, end].rearrange("p h g -> p g h"))
            ins.then_inc(s["first_scan"], 1)
            e = asT3[:, 0:SPREAD, :]
            then(v.tensor_tensor(e, e, adT[:, :, H:2 * H], ALU.add))
            v.scalar_tensor_tensor(e, e, SLOPE, e, ALU.mult, ALU.max)
            eng.wait_ge(s["carry_turned"], 1)
            for side in range(2):
                ins = v.tensor_copy(rst_h[0:H, side, :], bank[(6, 4)[side]][0:H, :])
            then(ins)
            v.tensor_tensor_scan(carry[0:H, 0, 1:VPAD + 1], rst_h[0:H, 0, :], bank[5][0:H, :], -BIG, ALU.add, ALU.max)
            then(v.tensor_tensor_scan(carry[0:H, 1, 0:VPAD][:, ::-1], rst_h[0:H, 1, ::-1],
                                      bank[7][0:H, ::-1], -BIG, ALU.add, ALU.max))
            eng.sem_inc(s["carry_ready"], 1)
            eng.wait_ge(s["seeds_turned"], 1)
            then(v.tensor_copy(seed, bank[5][:, 0:2 * G * H].rearrange("p (a g h) -> p a g h", a=2, g=G)))
            for h in range(H):
                for side in range(2):
                    for g in range(G):
                        ins = scan(side, h, g, False)
                then(ins)
                v.tensor_tensor(seg[:, 0, h], seg[:, 0, h], seg[:, 1, h], ALU.max).then_inc(s["seg_ready"], 1)
            eng.wait_ge(s["seg_ready"], H)
            mm = seg_flat[:, H * G * EB:H * G * EB + SPREAD * H].rearrange("p (u h) -> p u h", h=H)
            for h in range(H):
                eng.wait_ge(s["seg_turned"], h + 1)
                ins = v.tensor_tensor(mm[:, :, h], bank[4 + h][:, 0:SPREAD], adT[:, :, h], ALU.max)
            then(ins)
            then(v.tensor_tensor(mm, mm, adT[:, :, H:2 * H], ALU.add))
            then(v.scalar_tensor_tensor(mm, mm, SLOPE, mm, ALU.mult, ALU.max))
            v.tensor_tensor(adT[:, :, 0:H], e, mm, ALU.subtract).then_inc(s["exp_in"], 1)
            for h in range(H):
                ins = v.tensor_tensor(valv[:, :, H + h], mm[:, :, h], last[:, 0:SPREAD], ALU.mult)
            then(ins)
            eng.wait_ge(s["exp_out"], 1)
            eng.sem_inc(s["values_ready"], 1)
            eng.sem_inc(s["scratch_used"], 1)
            then(v.memset(sums[:, 0:late // 2], 0.0))
            eng.wait_ge(s["sums_zero0"], 1)

            def build(layer, i, k):
                eng.wait_ge(s[f"rows_used{layer}"], i * RING + k + RING - 3)
                u = i * RING + k
                if layer == 0:
                    ins = v.tensor_scalar(hot_of[k % 4], iota_f[:, :], relT[:, bass.ds(u, 1)], None, ALU.is_equal)
                else:
                    ins = v.tensor_scalar(hots[:, k % 4, 0:P], iota_f[:, :], relT[:, bass.ds(u, 1)],
                                          vals[:, bass.ds(u * NV + 2 * H, 1)], ALU.is_equal, ALU.mult)
                ins.then_inc(s[f"hot_ready{layer}"], 1)

            def take_sums(layer, i, k):
                n = i * RING + k
                j = eng.value_load(tile_of[0:1, bass.ds(n, 1)], min_val=0, max_val=NT - 1)
                eng.wait_ge(s[f"rows_used{layer}"], n + RING + 1)
                eng.wait_ge(s[f"sums_taken{layer}"], n + 2)
                to = sums[:, bass.ds(j * D, D)]
                ins = v.tensor_tensor(to, to, pair(k % 2).rearrange("p c n -> p (c n)"), ALU.add)
                if layer == 0:
                    to = nodesum[:, bass.ds(j * (3 * NV), 3 * NV)]
                    ins = v.tensor_tensor(to, to, bank[4 + k % 2][:, 0:3 * NV], ALU.add)
                ins.then_inc(s[f"sums_taken{layer}"], 1)

            def edge_loop(layer):
                for k in range(AHEAD):
                    build(layer, 0, k)
                with eng.Fori(0, ITERS) as i:
                    for k in range(RING):
                        build(layer, i, k + AHEAD)
                        take_sums(layer, i, k)
                eng.wait_ge(s[f"sums_taken{layer}"], 2 + VISITS)

            edge_loop(0)

            tv = t_self.rearrange("p (j h) -> p j h", h=H)
            cv = c_self[:, 0:NT * H].rearrange("p (j h) -> p j h", h=H)
            rv = r_self.rearrange("p (j h) -> p j h", h=H)
            for part in (1, 2):
                then(v.tensor_tensor(nodev, nodev, node_parts[:, :, part, :], ALU.add))
            then(v.tensor_tensor(tv, tabv[:, :, 0:H], tabv[:, :, H:2 * H], ALU.add))
            then(v.scalar_tensor_tensor(t_self, t_self, SLOPE, t_self, ALU.mult, ALU.max))
            then(v.tensor_tensor(tv, nodev[:, :, H:2 * H], tv, ALU.subtract))
            then(v.tensor_scalar(fdst[:, :], nodev[:, :, NV - 1], 0.0, None, ALU.is_gt))
            for h in range(H):
                ins = v.tensor_tensor(tv[:, :, h], tv[:, :, h], fdst[:, :], ALU.mult)
            ins.then_inc(s["self_in"], 1)
            sq = mix[1][:, 0:2 * NT]
            eng.wait_ge(s["self_in"], 1)
            then(v.tensor_scalar(fdst[:, :], nodev[:, :, NV - 1], 0.0, None, ALU.is_equal))
            v.tensor_scalar(sq[:, 0:NT], nodev[:, :, NV - 1], 1.0, None, ALU.max)
            v.tensor_tensor(sq[:, NT:2 * NT], nodev[:, :, 2 * H], fdst[:, :], ALU.add).then_inc(s["dst_sq_in"], 1)
            eng.wait_ge(s["self_out"], 1)
            then(v.tensor_tensor(rv, nodev[:, :, 0:H], tv, ALU.add))
            then(v.reciprocal(r_self, r_self))
            then(v.tensor_tensor(cv, tv, rv, ALU.mult))
            eng.wait_ge(s["dst_sq_out"], 1)
            then(v.tensor_tensor(sq[:, 0:NT], sq[:, 0:NT], sq[:, NT:2 * NT], ALU.mult))
            then(v.reciprocal(fdst[:, :], sq[:, 0:NT]))
            eng.sem_inc(s["self_ready"], 1)

            def normalize(j, b, to):
                for c in range(2):
                    ins = v.bn_stats(stats[b][:, c * 6:(c + 1) * 6], mix[b][:, c * 512:(c + 1) * 512])
                then(ins)
                eng.sem_inc(s["vector_passed"], 1)
                then(v.bn_aggr(moments[b], stats[b]))
                v.tensor_scalar(spread[b][:, 0:1], moments[b][:, 1:2], EPS, None, ALU.add).then_inc(s["variance1"], 1)
                eng.wait_ge(s["deviation1"], j + 1)
                then(v.reciprocal(spread[b][:, 0:1], spread[b][:, 1:2]))
                return v.tensor_scalar(to, mix[b], moments[b][:, 0:1], spread[b][:, 0:1], ALU.subtract, ALU.mult)

            def mix0(j, b):
                eng.wait_ge(s["mixed"], j + 3)
                for h in range(H):
                    part = sums[:, bass.ds(j * D + h * C, C)]
                    ins = v.scalar_tensor_tensor(part, part, r_self[:, bass.ds(j * H + h, 1)],
                                                 psum[:, 2 * b + h // 2, (h % 2) * C:(h % 2 + 1) * C], ALU.mult, ALU.add)
                ins.then_inc(s["sums_mixed"], 1)
                eng.wait_ge(s["sums_mixed"], j + 3)
                eng.wait_ge(s[f"x_in{b}"], turn_of(j, b) * 16 + 16)
                eng.wait_ge(s["x1_ready"], j + 1)
                v.scalar_tensor_tensor(mix[b], sums[:, bass.ds(j * D, D)], 0.0, x_in[b], ALU.max, ALU.add) \
                    .then_inc(s["x_free"], 1)
                eng.wait_ge(s["x_free"], j + 3)
                for c in range(2):
                    ins = v.bn_stats(stats[b][:, c * 6:(c + 1) * 6], mix[b][:, c * 512:(c + 1) * 512])
                then(ins)
                eng.sem_inc(s["vector_passed"], 1)
                then(v.bn_aggr(moments[b], stats[b]))
                v.tensor_scalar(spread[b][:, 0:1], moments[b][:, 1:2], EPS, None, ALU.add).then_inc(s["variance0"], 1)

            def norm0(j, b, first=False):
                if not first:
                    eng.wait_ge(s[f"x1_stored{b}"], turn_of(j, b) * 16)
                v.tensor_copy(x1_out[b][:, D:D + 1], fsrc[:, bass.ds(j + 0, 1)])
                eng.wait_ge(s["deviation0"], j + 1)
                then(v.reciprocal(spread[b][:, 0:1], spread[b][:, 1:2]))
                v.scalar_tensor_tensor(shifted[b], moments[b][:, 0:1], -1.0, spread[b][:, 0:1], ALU.mult, ALU.mult) \
                    .then_inc(s["normal_ready"], 1)

            def tiles0():
                mix0(0, 0)
                mix0(1, 1)
                norm0(0, 0, True)
                mix0(2, 0)
                norm0(1, 1, True)
                with eng.Fori(1, NT // 2) as i:
                    order.enter(i - 1, 6)
                    mix0(Tile(i, 1), 1)
                    norm0(Tile(i, 0), 0)
                    mix0(Tile(i + 1, 0), 0)
                    norm0(Tile(i, 1), 1)
                    order.leave(NT // 2 - 1)
                norm0(NT - 1, 0)

            for b in range(2):
                v.memset(x1_out[b][:, D:], 0.0)
            tiles0()
            edge_loop(1)

            def finish1(j, b, first=False):
                eng.wait_ge(s["product_ready"], j + 1)
                if not first:
                    eng.wait_ge(s[f"out_stored{b}"], turn_of(j, b) * 16)
                v.tensor_tensor(mix[b], pair(b).rearrange("p c n -> p (c n)"), bias_at, ALU.add) \
                    .then_inc(s["product_taken"], 1)
                eng.wait_ge(s["product_taken"], j + 3)
                eng.wait_ge(s[f"x1_in{b}"], turn_of(j, b) * 16 + 16)
                then(v.scalar_tensor_tensor(mix[b], mix[b], 0.0, x1_in[b], ALU.max, ALU.add))
                eng.sem_inc(s["x1_free"], 1)
                normalize(j, b, mix[b]).then_inc(s["out_ready"], 1)

            eng.wait_ge(s["bias1_in"], 16)

            def cut_W(k):
                eng.wait_ge(s["W_high_ready"], k + 1)
                if isinstance(k, int):
                    to, whole, high = low_of_W(k), Wt[:, k, :], W_high[k].bitcast(F32)
                else:
                    at = bass.ds(k * D, D)
                    to, whole, high = vals_r[:, at], W_flat[:, at], sums_r[:, at].bitcast(F32)
                v.tensor_tensor(to, whole, high, ALU.subtract).then_inc(s["W_low_ready"], 1)

            def cut_sums(j, b):
                eng.wait_ge(s["aggT_ready"], j + 1)
                eng.wait_ge(s["product_ready"], j - 1)
                for half in range(2):
                    ins = v.tensor_tensor(low_of_sums(b, half), bank[4 + half].rearrange("p (k n) -> p k n", n=P),
                                          aggT_high[b][:, half * 4:half * 4 + 4, :].bitcast(F32), ALU.subtract)
                ins.then_inc(s["aggT_low_ready"], 1)

            finish1(0, 0, True)
            finish1(1, 1, True)
            with eng.Fori(1, 1 + KT // 4) as i:
                order.enter(i - 1, 8)
                for b in range(2):
                    finish1(Tile(i, b), b)
                    cut_W((i - 1) * 2 + b)
                order.leave(KT // 4)
            cut_sums(WHOLE, 0)
            finish1(WHOLE - 2, 0)
            eng.wait_ge(s["product_ready"], WHOLE)
            for k in range(KT // 2, KT):
                cut_W(k)
            cut_sums(WHOLE + 1, 1)
            finish1(WHOLE - 1, 1)
            cut_sums(WHOLE + 2, 0)
            finish1(WHOLE, 0)
            with eng.Fori(WHOLE // 2, NT // 2 - 1) as i:
                order.enter(i - WHOLE // 2, 8)
                cut_sums(Tile(i + 1, 1), 1)
                finish1(Tile(i, 1), 1)
                cut_sums(Tile(i + 2, 0), 0)
                finish1(Tile(i + 1, 0), 0)
                order.leave(NT // 2 - 1 - WHOLE // 2)
            finish1(NT - 2, 1)
            finish1(NT - 1, 0)


def kernel(x, src, dst, edge_weight, L0_gnn_W, L0_gnn_att_src, L0_gnn_att_dst, L0_gnn_bias, L1_gnn_W, L1_gnn_b):
    import numpy as np
    import concourse.bacc as bacc
    from concourse.bass_utils import run_bass_kernel_spmd

    x = np.asarray(x)
    xpad = np.zeros((NP, D), x.dtype)
    xpad[:N] = x

    def blocks(v, fill):
        v = np.asarray(v)
        b = np.full(((NB + 1) * EB,), fill, v.dtype)
        b[:E] = v
        return b.reshape(NB + 1, EB)

    arrays = {
        "xT": np.ascontiguousarray(xpad.reshape(NT, P, KT, P).transpose(0, 3, 2, 1)).reshape(NT * P, D), "x": xpad,
        "src_blocks": blocks(src, NP - 1), "dst_blocks": blocks(dst, NP - 1), "w_blocks": blocks(edge_weight, 1),
        "W0": np.asarray(L0_gnn_W), "att_src": np.asarray(L0_gnn_att_src), "att_dst": np.asarray(L0_gnn_att_dst),
        "bias0": np.asarray(L0_gnn_bias), "W1": np.asarray(L1_gnn_W), "bias1": np.asarray(L1_gnn_b),
    }
    nc = bacc.Bacc("TRN2", target_bir_lowering=False, num_devices=1)
    args = {n: nc.dram_tensor(n, v.shape, mybir.dt.from_np(v.dtype), kind="ExternalInput").ap() for n, v in arrays.items()}
    out = nc.dram_tensor("out", (N, D), F32, kind="ExternalOutput").ap()
    gnn_kernel(nc, **args, out=out)
    r = run_bass_kernel_spmd(nc, [arrays], core_ids=[0])
    return r.results[0]["out"]
```
